# Optimizing a Trainium2 kernel written in Bass

```python
import numpy as np
import jax
import jax.numpy as jnp

def _softmax(x, axis=-1):
    return jax.nn.softmax(x, axis=axis)

def _gelu(x):
    return jax.nn.gelu(x, approximate=True)

def _silu(x):
    return jax.nn.silu(x)

def _sigmoid(x):
    return jax.nn.sigmoid(x)

def _layernorm(x, axis=-1, eps=1e-05):
    m = jnp.mean(x, axis=axis, keepdims=True)
    v = jnp.var(x, axis=axis, keepdims=True)
    return (x - m) / jnp.sqrt(v + eps)

def _scatter_add(tgt, idx, src, axis=0):
    return tgt.at[idx].add(src)

def _segment_sum(src, seg, n):
    return jax.ops.segment_sum(src, seg, n)
kernel_name = 'mk_gnn_resnorm_d2_gnn_r8_668768'

def setup_inputs(seed: int=0):
    np.random.seed(seed)
    _w = jnp.asarray

    def _rec_inputs():
        import jax
        import jax.numpy as jnp
        _gk = jax.random.key(seed)
        x = -0.0003713 + 1 * jax.random.normal(jax.random.fold_in(_gk, 1), (6250, 256), jnp.float32)
        src = jax.random.randint(jax.random.fold_in(_gk, 2), (200000,), 0, 6250, jnp.int32)
        dst = jnp.minimum((6250 * jax.random.uniform(jax.random.fold_in(_gk, 3), (200000,)) ** 2.0).astype(jnp.int32), 49999)
        _o = jnp.argsort(dst, stable=True)
        src = src[_o]
        dst = dst[_o]
        edge_type_8 = jax.random.randint(jax.random.fold_in(_gk, 13), (200000,), 0, 8, jnp.int32)
        edge_weight1 = 0.000937891 + 0.999965 * jax.random.normal(jax.random.fold_in(_gk, 14), (200000, 1), jnp.float32)
        return (x, src, dst, edge_type_8, edge_weight1)
    x, src, dst, edge_type_8, edge_weight1 = _rec_inputs()

    def _L0_gnn_setup():
        import jax, jax.numpy as jnp
        import numpy as np
        N_NODES = 6250
        N_EDGES = 100000
        D_IN = 256
        D_OUT = 256
        N_REL = 8
        key = jax.random.key(seed)
        k_x, k_ei, k_et, k_w = jax.random.split(key, 4)
        x = jax.random.normal(k_x, (N_NODES, D_IN), dtype=jnp.float32)
        edge_index = jax.random.randint(k_ei, (2, N_EDGES), 0, N_NODES, dtype=jnp.int32)
        edge_type = jax.random.randint(k_et, (N_EDGES,), 0, N_REL, dtype=jnp.int32)
        limit = float(np.sqrt(6.0 / (D_IN + D_OUT)))
        weight = jax.random.uniform(k_w, (N_REL, D_IN, D_OUT), dtype=jnp.float32, minval=-limit, maxval=limit)
        bias = jnp.zeros((D_OUT,), dtype=jnp.float32)
        return {'x': x, 'edge_index': edge_index, 'edge_type': edge_type, 'weight': weight, 'bias': bias}
    _L0_gnn_all = _L0_gnn_setup()
    _L0_gnn_in = {k: v for k, v in _L0_gnn_all.items() if k in ('weight', 'bias')}
    del _L0_gnn_all

    def _L1_gnn_setup():
        import jax, jax.numpy as jnp
        import numpy as np
        DIM = 256
        H = 8
        HD = DIM // H
        N = 6250
        E = 100000
        FFN = 4 * DIM
        EPS = 1e-05

        def layer_norm(x, g, b):
            mu = jnp.mean(x, axis=-1, keepdims=True)
            var = jnp.mean((x - mu) ** 2, axis=-1, keepdims=True)
            return (x - mu) * jax.lax.rsqrt(var + EPS) * g + b

        def _mhsa(h, edge_bias, src, dst, Wq, Wk, Wv, Wp, bp):
            n = h.shape[0]
            Q = (h @ Wq).reshape(n, H, HD)
            K = (h @ Wk).reshape(n, H, HD)
            V = (h @ Wv).reshape(n, H, HD)
            score = jnp.einsum('ehd,ehd->eh', K[src], Q[dst]) / np.sqrt(HD) + edge_bias
            m = jax.ops.segment_max(score, dst, num_segments=n)
            ex = jnp.exp(score - m[dst])
            denom = jax.ops.segment_sum(ex, dst, num_segments=n)
            attn = ex / denom[dst]
            out = jax.ops.segment_sum(attn[:, :, None] * V[src], dst, num_segments=n)
            return out.reshape(n, DIM) @ Wp + bp
        key = jax.random.key(seed)
        ks = jax.random.split(key, 16)
        s = 1.0 / np.sqrt(DIM)
        inp = {'h': jax.random.normal(ks[0], (N, DIM), jnp.float32), 'edge_bias': jax.random.normal(ks[1], (E, 1), jnp.float32), 'src': jax.random.randint(ks[2], (E,), 0, N, jnp.int32), 'dst': jax.random.randint(ks[3], (E,), 0, N, jnp.int32), 'Wq': jax.random.normal(ks[4], (DIM, DIM), jnp.float32) * s, 'Wk': jax.random.normal(ks[5], (DIM, DIM), jnp.float32) * s, 'Wv': jax.random.normal(ks[6], (DIM, DIM), jnp.float32) * s, 'Wp': jax.random.normal(ks[7], (DIM, DIM), jnp.float32) * s, 'bp': jnp.zeros((DIM,), jnp.float32), 'ln1_g': jnp.ones((DIM,), jnp.float32), 'ln1_b': jnp.zeros((DIM,), jnp.float32), 'ln2_g': jnp.ones((DIM,), jnp.float32), 'ln2_b': jnp.zeros((DIM,), jnp.float32), 'W1': jax.random.normal(ks[8], (DIM, FFN), jnp.float32) * s, 'b1': jnp.zeros((FFN,), jnp.float32), 'W2': jax.random.normal(ks[9], (FFN, DIM), jnp.float32) * (1.0 / np.sqrt(FFN)), 'b2': jnp.zeros((DIM,), jnp.float32)}
        return inp
    _L1_gnn_all = _L1_gnn_setup()
    _L1_gnn_in = {k: v for k, v in _L1_gnn_all.items() if k in ('Wq', 'Wk', 'Wv', 'Wp', 'bp', 'ln1_g', 'ln1_b', 'ln2_g', 'ln2_b', 'W1', 'b1', 'W2', 'b2')}
    del _L1_gnn_all
    return {'x': x, 'src': src, 'dst': dst, 'edge_type_8': edge_type_8, 'edge_weight1': edge_weight1, 'L0_gnn_weight': _L0_gnn_in['weight'], 'L0_gnn_bias': _L0_gnn_in['bias'], 'L1_gnn_Wq': _L1_gnn_in['Wq'], 'L1_gnn_Wk': _L1_gnn_in['Wk'], 'L1_gnn_Wv': _L1_gnn_in['Wv'], 'L1_gnn_Wp': _L1_gnn_in['Wp'], 'L1_gnn_bp': _L1_gnn_in['bp'], 'L1_gnn_ln1_g': _L1_gnn_in['ln1_g'], 'L1_gnn_ln1_b': _L1_gnn_in['ln1_b'], 'L1_gnn_ln2_g': _L1_gnn_in['ln2_g'], 'L1_gnn_ln2_b': _L1_gnn_in['ln2_b'], 'L1_gnn_W1': _L1_gnn_in['W1'], 'L1_gnn_b1': _L1_gnn_in['b1'], 'L1_gnn_W2': _L1_gnn_in['W2'], 'L1_gnn_b2': _L1_gnn_in['b2']}

def reference(x, src, dst, edge_type_8, edge_weight1, L0_gnn_weight, L0_gnn_bias, L1_gnn_Wq, L1_gnn_Wk, L1_gnn_Wv, L1_gnn_Wp, L1_gnn_bp, L1_gnn_ln1_g, L1_gnn_ln1_b, L1_gnn_ln2_g, L1_gnn_ln2_b, L1_gnn_W1, L1_gnn_b1, L1_gnn_W2, L1_gnn_b2):
    import jax
    import jax.numpy as jnp

    def _L0_gnn_ref(x, edge_index, edge_type, weight, bias):
        import jax, jax.numpy as jnp
        import numpy as np
        N_NODES = 6250
        N_EDGES = 100000
        D_IN = 256
        D_OUT = 256
        N_REL = 8
        num_nodes = x.shape[0]
        row, col = (edge_index[0], edge_index[1])
        xt = jnp.einsum('ni,rio->rno', x, weight)
        messages = xt[edge_type, col]
        out = jax.ops.segment_sum(messages, row, num_segments=num_nodes)
        return jax.nn.relu(out + bias)

    def _L1_gnn_ref(h, edge_bias, src, dst, Wq, Wk, Wv, Wp, bp, ln1_g, ln1_b, ln2_g, ln2_b, W1, b1, W2, b2):
        import jax, jax.numpy as jnp
        import numpy as np
        DIM = 256
        H = 8
        HD = DIM // H
        N = 6250
        E = 100000
        FFN = 4 * DIM
        EPS = 1e-05

        def layer_norm(x, g, b):
            mu = jnp.mean(x, axis=-1, keepdims=True)
            var = jnp.mean((x - mu) ** 2, axis=-1, keepdims=True)
            return (x - mu) * jax.lax.rsqrt(var + EPS) * g + b

        def _mhsa(h, edge_bias, src, dst, Wq, Wk, Wv, Wp, bp):
            n = h.shape[0]
            Q = (h @ Wq).reshape(n, H, HD)
            K = (h @ Wk).reshape(n, H, HD)
            V = (h @ Wv).reshape(n, H, HD)
            score = jnp.einsum('ehd,ehd->eh', K[src], Q[dst]) / np.sqrt(HD) + edge_bias
            m = jax.ops.segment_max(score, dst, num_segments=n)
            ex = jnp.exp(score - m[dst])
            denom = jax.ops.segment_sum(ex, dst, num_segments=n)
            attn = ex / denom[dst]
            out = jax.ops.segment_sum(attn[:, :, None] * V[src], dst, num_segments=n)
            return out.reshape(n, DIM) @ Wp + bp
        attn_out = _mhsa(h, edge_bias, src, dst, Wq, Wk, Wv, Wp, bp)
        h1 = layer_norm(h + attn_out, ln1_g, ln1_b)
        ffn_out = jax.nn.gelu(h1 @ W1 + b1, approximate=False) @ W2 + b2
        return layer_norm(h1 + ffn_out, ln2_g, ln2_b)
    edge_index = jnp.stack([src, dst])
    x = _layernorm(x + _L0_gnn_ref(x, edge_index, edge_type_8, L0_gnn_weight, L0_gnn_bias), axis=-1)
    x = _layernorm(x + _L1_gnn_ref(x, edge_weight1, src, dst, L1_gnn_Wq, L1_gnn_Wk, L1_gnn_Wv, L1_gnn_Wp, L1_gnn_bp, L1_gnn_ln1_g, L1_gnn_ln1_b, L1_gnn_ln2_g, L1_gnn_ln2_b, L1_gnn_W1, L1_gnn_b1, L1_gnn_W2, L1_gnn_b2), axis=-1)
    return x

_drawn_inputs = setup_inputs


def setup_inputs(seed=0):
    import zlib

    import numpy as np

    out = dict(_drawn_inputs(seed))
    spreads = {'L0_gnn_bias': (0.0, 0.368),
     'L1_gnn_bp': (0.0, 0.1),
     'L1_gnn_ln1_g': (1.0, 0.2),
     'L1_gnn_ln1_b': (0.0, 0.1),
     'L1_gnn_ln2_g': (1.0, 0.2),
     'L1_gnn_ln2_b': (0.0, 0.1),
     'L1_gnn_b1': (0.0, 0.272),
     'L1_gnn_b2': (0.0, 0.1)}
    factors = {}
    for name, (base, spread) in spreads.items():
        noise = np.random.default_rng([zlib.crc32(name.encode()), seed]).standard_normal(out[name].shape)
        drawn = base * np.exp(spread * noise) if base else spread * noise
        out[name] = jnp.asarray(drawn.astype(out[name].dtype))
    for name, factor in factors.items():
        out[name] = (out[name] * factor).astype(out[name].dtype)
    return out
```

```python
from contextlib import ExitStack

import numpy as np

import concourse.bass as bass
from concourse import mybir

F32 = mybir.dt.float32
BF16 = mybir.dt.bfloat16
I32 = mybir.dt.int32
ALU = mybir.AluOpType
ACT = mybir.ActivationFunctionType
AX = mybir.AxisListType

P = 128
N, D, E = 6250, 256, 200000
REL, HEADS = 8, 8
HD = D // HEADS
FFN = 4 * D
FC = FFN // P
KC = D // P
LOG_P = 7
W = -(-N // P)
NP_ = W * P
JUNK = NP_ - 1
BLOCKS = 4
PERM_U, ITEM_U, ROUNDS = 8, 9, 49
BT = PERM_U * ROUNDS
T = BLOCKS * BT
BI = ITEM_U * ROUNDS
assert T * P >= E and BI * P >= BT * P + W * (P - 1) - P
RAW_G = -(-T // P)
WALK = T + W - 1
WALK_U = 8
assert WALK % WALK_U == 0
AW = D + HEADS
CH = P // HEADS
CJ = T // CH
CL = CJ * P
assert CH * CJ == T
LOW = -1e30
EPS = 1e-5
SCALE = 1.0 / float(np.sqrt(HD))


class Progress:

    def __init__(self, sem, ring):
        self.sem, self.ring = sem, ring

    def start(self, e):
        e.sem_inc(self.sem, self.ring)

    def done(self, e, i):
        e.wait_ge(self.sem, i + (1 + self.ring))

    def free(self, e, i, ring):
        e.wait_ge(self.sem, i + (1 + self.ring - ring))


class Chain:

    def __init__(self, e, sem):
        self.e, self.sem, self.n = e, sem, 0

    def __call__(self, ins):
        ins.then_inc(self.sem, 1)
        self.n += 1
        self.e.wait_ge(self.sem, self.n)


def build(nc, a, out):
    ctx = ExitStack()
    with ctx:
        def sb(name, cols, dt=F32, rows=P):
            return ctx.enter_context(nc.sbuf_tensor(name, [rows, cols], dt))

        def sem(name):
            return ctx.enter_context(nc.semaphore(name))

        def dram(name, shape, dt=F32):
            return nc.dram_tensor(name, shape, dt, kind="Internal").ap()

        xt_table = dram("xt_table", (REL * NP_, D))
        k_table = dram("k_table", (NP_, D))
        v_table = dram("v_table", (NP_, D))
        x1_store = dram("x1_store", (NP_, D))

        node_a = sb("node_a", W * AW)
        node_b = sb("node_b", W * D)
        edge_s = sb("edge_s", T * HEADS)
        src_c, dst_c, wgt_c = sb("src_c", T), sb("dst_c", T), sb("wgt_c", T)
        table = sb("table", 2 * WALK, I32)
        rows_g = sb("rows_g", ITEM_U * D)
        stage_i = sb("stage_i", ITEM_U, I32)
        stage_d = sb("stage_d", WALK_U)
        onehot = sb("onehot", 3 * P)
        msg = sb("msg", 3 * AW)
        prod = sb("prod", 2 * D)
        part = sb("part", 2 * HEADS)
        iota_q = sb("iota_q", 512)
        iota_p = sb("iota_p", 1)
        win_neg = sb("win_neg", W)
        win_pos = sb("win_pos", W)
        ident, tri, ones = sb("ident", P), sb("tri", P), sb("ones", 512)
        tile_u = sb("tile_u", RAW_G)
        stats = sb("stats", 2 * 6)
        mv = sb("mv", W * 2)
        rstd, nmr = sb("rstd", W), sb("nmr", W)
        small = sb("small", 64)
        pb = ctx.enter_context(nc.psum_tensor("pb", [P, 8, 512], F32))

        class Cut:

            def __init__(self, region):
                self.region, self.at = region, 0

            def __call__(self, cols, dt=F32):
                words = cols if dt in (F32, I32) else -(-cols // 2)
                piece = self.region[:, self.at:self.at + words]
                self.at += words
                assert self.at <= self.region.shape[1]
                return piece if dt == F32 else piece.bitcast(dt)[:, 0:cols]

        cut = Cut(node_a)
        raw_i = {n: cut(RAW_G * P, I32) for n in ("src", "dst", "type")}
        raw_w = cut(RAW_G * P)
        raw_f = {n: cut(RAW_G * P) for n in ("src", "dst", "row")}
        acc = node_a
        acc_w = node_a[:].rearrange("p (w d) -> p w d", w=W)
        cut = Cut(edge_s)
        win_c, loc_c, lo_c, hi_c, pos_c, q_c, c_c = (cut(T) for _ in range(7))
        int_c = cut(T, I32)
        cut = Cut(node_b)
        w0 = cut(KC * REL * D).rearrange("p (k r o) -> p k r o", k=KC, r=REL)
        xt_out = cut(2 * 4 * D).rearrange("p (s n) -> p s n", s=2)
        x_in = cut(3 * D).rearrange("p (s n) -> p s n", s=3)
        x_t = cut(2 * D).rearrange("p (s k n) -> p s k n", s=2, k=KC)
        mask, cum, tmp = cut(BT), cut(BT), cut(BT)
        tot, offs, end_t = cut(W), cut(W), cut(P)
        tot_i = cut(W, I32)
        end_c, cmp_i = cut(1), cut(BI)
        idx_s = cut(2 * BI, I32).rearrange("p (s n) -> p s n", s=2)
        loc_s = cut(2 * BI).rearrange("p (s n) -> p s n", s=2)
        lo_s = cut(BI)
        hot_q = cut(2 * 3 * P, BF16).rearrange("p (s v q) -> p s v q", s=2, v=3)
        hot_c = cut(2 * BI + 2, BF16)[:, 0:2 * BI].rearrange("p (s n) -> p s n", s=2)
        zero_b = sb("zero_b", 448, BF16)[:]
        cut = Cut(edge_s)
        wqkv = cut(KC * 3 * D).rearrange("p (k n) -> p k n", k=KC)
        bias0 = cut(D)
        x1t = cut(2 * D).rearrange("p (s k n) -> p s k n", s=2, k=KC)
        kv_out = cut(2 * 2 * D).rearrange("p (s n) -> p s n", s=2)
        iota_w = cut(WALK)
        before = cut(2 * WALK, BF16).rearrange("p (s n) -> p s n", s=2)
        tile_at, chunk_at = cut(WALK), cut(WALK)
        scratch = cut(T)
        cut = Cut(edge_s)
        wp = cut(KC * D).rearrange("p (k n) -> p k n", k=KC)
        w1 = cut(KC * FFN).rearrange("p (k n) -> p k n", k=KC)
        w2 = cut(FC * D).rearrange("p (k n) -> p k n", k=FC)
        vec = {n: cut(D) for n in ("bp", "ln1_g", "ln1_b", "ln2_g", "ln2_b", "b2")}
        b1c = cut(FC)
        att = cut(2 * D).rearrange("p (s n) -> p s n", s=2)
        att_t = cut(2 * D).rearrange("p (s k n) -> p s k n", s=2, k=KC)
        h1_t = cut(KC * 512).rearrange("p (k n) -> p k n", k=KC)
        hid = cut(FC * 512).rearrange("p (k n) -> p k n", k=FC)
        recip = cut(HEADS * 2).rearrange("p (s n) -> p s n", s=2)
        scan_s = node_a[:, 0:CL]
        pen = node_b[:, 0:CL // 2 + 1].bitcast(BF16)[:, 0:CL + 1]
        dst_t = node_b[:, CL // 2 + 1:CL // 2 + 1 + 257]
        same = node_b[:, CL // 2 + 300:CL // 2 + 556]
        row = [node_b[0:1, CL // 2 + 600 + 130 * i:CL // 2 + 600 + 130 * i + P] for i in range(12)]
        carry = node_b[:, CL // 2 + 2400:CL // 2 + 2402]
        score_v = edge_s[:].rearrange("p (j n) -> p j n", j=CJ)
        dst_x = node_b[:, CL // 2 + 2410:CL // 2 + 2410 + 512].rearrange("p (s n) -> p s n", s=2)

        s_meet = sem("s_meet")
        meets = {}

        def meet(e):
            k = meets[e] = meets.get(e, 0) + 1
            e.drain().then_inc(s_meet, 1)
            e.wait_ge(s_meet, 5 * k)

        engines = {n: [] for n in ("sync", "gpsimd", "scalar", "tensor", "vector")}

        def phase(**parts):
            for n, todo in engines.items():
                todo.append(parts.get(n))

        s_padded, s_consts, s_rawload = sem("s_padded"), sem("s_consts"), sem("s_rawload")
        s_float, s_turned, s_cols = sem("s_float"), sem("s_turned"), sem("s_cols")
        s_dv0, s_gp0 = sem("s_dv0"), sem("s_gp0")
        full = (E // P)
        whole = full // P
        rest, tail = full - whole * P, E - full * P
        turned = [("src", raw_f["src"], src_c), ("dst", raw_f["dst"], dst_c),
                  ("row", raw_f["row"], pos_c), ("wgt", raw_w, wgt_c)]
        packs = [(v, g) for v in range(4) for g in range(0, RAW_G, 4)]

        def load_edges(e):
            e.wait_ge(s_padded, 4)
            for name, to in (("src", raw_i["src"]), ("dst", raw_i["dst"]),
                             ("edge_type_8", raw_i["type"]), ("edge_weight1", raw_w)):
                v = to.rearrange("p (g e) -> p g e", e=P)
                d = a[name]
                e.dma_start(v[:, 0:whole, :], d[0:whole * P * P].rearrange("(g p e) -> p g e", p=P, e=P))\
                    .then_inc(s_rawload, 16)
                e.dma_start(v[0:rest, whole, :], d[whole * P * P:full * P].rearrange("(p e) -> p e", e=P))\
                    .then_inc(s_rawload, 16)
                e.dma_start(v[rest:rest + 1, whole, 0:tail], d[full * P:E].rearrange("(a e) -> a e", a=1))\
                    .then_inc(s_rawload, 16)

        def make_consts(e):
            c = Chain(e, s_gp0)
            c(e.memset(ident[:], 0.0))
            c(e.affine_select(out=ident[:], in_=ident[:], compare_op=ALU.not_equal, fill=1.0, base=0,
                              pattern=[[-1, P]], channel_multiplier=1))
            c(e.memset(ones[:], 1.0))
            c(e.affine_select(out=tri[:], in_=ones[:, 0:P], compare_op=ALU.is_gt, fill=0.0, base=0,
                              pattern=[[1, P]], channel_multiplier=-1))
            c(e.iota(iota_q[:], [[1, 512]], base=0, channel_multiplier=0, allow_small_or_imprecise_dtypes=True))
            c(e.iota(iota_p[:], [[1, 1]], base=0, channel_multiplier=1, allow_small_or_imprecise_dtypes=True))
            c(e.iota(win_neg[:], [[-P, W]], base=0, channel_multiplier=0, allow_small_or_imprecise_dtypes=True))
            c(e.iota(win_pos[:], [[P, W]], base=0, channel_multiplier=0, allow_small_or_imprecise_dtypes=True))
            c(e.iota(tile_u[:], [[P, RAW_G]], base=0, channel_multiplier=1, allow_small_or_imprecise_dtypes=True))
            e.sem_inc(s_consts, 1)

        def edges_float(e):
            e.memset(raw_i["src"], JUNK).then_inc(s_padded, 1)
            e.memset(raw_i["dst"], JUNK).then_inc(s_padded, 1)
            e.memset(raw_i["type"], 0).then_inc(s_padded, 1)
            e.memset(raw_w, 0.0).then_inc(s_padded, 1)
            e.wait_ge(s_rawload, 16 * 12)
            e.tensor_copy(raw_f["src"], raw_i["src"]).then_inc(s_float, 1)
            e.tensor_copy(raw_f["dst"], raw_i["dst"]).then_inc(s_float, 1)
            e.scalar_tensor_tensor(raw_f["row"], raw_i["type"], float(NP_), raw_i["dst"], ALU.mult, ALU.add)\
                .then_inc(s_float, 1)
            c = Chain(e, s_dv0)
            last = raw_i["dst"].rearrange("p (g e) -> p g e", e=P)[:, :, P - 1]
            e.wait_ge(s_consts, 1)
            c(e.tensor_scalar(tot_i[:, 0:RAW_G], last, LOG_P, None, ALU.arith_shift_right))
            c(e.tensor_copy(tot[:, 0:RAW_G], tot_i[:, 0:RAW_G]))
            c(e.tensor_tensor(tile_u[:], tile_u[:], tot[:, 0:RAW_G], ALU.add))
            e.wait_ge(s_cols, len(packs))
            for src, sh, ms, to, one in ((src_c[:], LOG_P, None, win_c, 0), (src_c[:], None, P - 1, loc_c, 1),
                                         (pos_c, 8, None, hi_c, 0), (pos_c, None, 255, lo_c, 0)):
                c(e.tensor_copy(int_c, src))
                if sh is not None:
                    c(e.tensor_scalar(int_c, int_c, sh, None, ALU.arith_shift_right))
                else:
                    c(e.tensor_scalar(int_c, int_c, ms, None, ALU.bitwise_and))
                c(e.tensor_scalar(to, int_c, float(one), None, ALU.add))
            c(e.memset(zero_b, 0.0))

        def edges_turn(e):
            e.wait_ge(s_consts, 1)
            e.wait_ge(s_float, 3)
            for n, (v, g0) in enumerate(packs):
                if n >= 4:
                    e.wait_ge(s_cols, n - 3)
                for g in range(g0, min(g0 + 4, RAW_G)):
                    ins = e.transpose(pb[:, n % 4, (g - g0) * P:(g - g0 + 1) * P],
                                      turned[v][1].rearrange("p (g e) -> p g e", e=P)[:, g, :], ident[:])
                ins.then_inc(s_turned, 1)

        def edges_cols(e):
            for n, (v, g0) in enumerate(packs):
                e.wait_ge(s_turned, n + 1)
                cols = min(T - g0 * P, 512)
                to = turned[v][2]
                e.activation(to[:, g0 * P:g0 * P + cols], pb[:, n % 4, 0:cols], ACT.Copy).then_inc(s_cols, 1)

        phase(sync=load_edges, gpsimd=make_consts, vector=edges_float, tensor=edges_turn, scalar=edges_cols)

        s_w0, s_x = sem("s_w0"), [sem("s_x0"), sem("s_x1")]
        s_xz, s_xtr, s_xtc, s_xm, s_xe = sem("s_xz"), sem("s_xtr"), sem("s_xtc"), sem("s_xm"), sem("s_xe")
        s_xst = [sem("s_xst0"), sem("s_xst1")]
        s_rank, s_tot, s_pre, s_end, s_endt, s_cmp, s_win = (sem(n) for n in (
            "s_rank", "s_tot", "s_pre", "s_end", "s_endt", "s_cmp", "s_win"))
        s_accz = sem("s_accz")
        xt_v = xt_table.rearrange("(r n) o -> n r o", r=REL)
        HALF = 4 * D

        def node_rows(w):
            return min(N - w * P, P)

        def x_slot(w):
            return 2 if w == W - 1 else w % 2

        def table_io(e):
            for k in range(KC):
                e.dma_start(w0[:, k, :, :], a["L0_gnn_weight"][:, k * P:(k + 1) * P, :].rearrange("r p o -> p r o"))\
                    .then_inc(s_w0, 16)

            def store(n):
                w, half = divmod(n, 2)
                e.wait_ge(s_xe, 2 * (n + 1))
                e.dma_start(xt_v[w * P:(w + 1) * P, half * 4:half * 4 + 4, :],
                            xt_out[:, n % 2, :].rearrange("p (r o) -> p r o", r=4)).then_inc(s_xst[n % 2], 16)

            for w in range(W + 1):
                if w < W:
                    if w == W - 1:
                        e.wait_ge(s_xz, 1)
                    elif w >= 2:
                        e.wait_ge(s_xtr, w - 1)
                    e.dma_start(x_in[0:node_rows(w), x_slot(w), :], a["x"][w * P:w * P + node_rows(w), :])\
                        .then_inc(s_x[w % 2], 16)
                if w >= 1:
                    store(2 * w - 2)
                    store(2 * w - 1)
            e.wait_ge(s_xst[0], 16 * W)
            e.wait_ge(s_xst[1], 16 * W)

        def table_products(e):
            def turn(w):
                e.wait_ge(s_x[w % 2], 16 * (w // 2 + 1))
                if w >= 1:
                    e.wait_ge(s_xtc, w)
                for k in range(KC):
                    ins = e.transpose(pb[:, 4, k * P:(k + 1) * P], x_in[:, x_slot(w), k * P:(k + 1) * P], ident[:])
                ins.then_inc(s_xtr, 1)

            turn(0)
            e.wait_ge(s_w0, 16 * KC)
            for w in range(W):
                if w + 1 < W:
                    turn(w + 1)
                e.wait_ge(s_xtc, w + 1)
                for half in range(2):
                    for q in range(2):
                        n = 4 * w + 2 * half + q
                        if n >= 4:
                            e.wait_ge(s_xe, n - 3)
                        for k in range(KC):
                            ins = e.matmul(pb[:, n % 4, :], x_t[:, w % 2, k, :],
                                           w0[:, k, half * 4 + q * 2:half * 4 + q * 2 + 2, :],
                                           start=(k == 0), stop=(k == KC - 1))
                        ins.then_inc(s_xm, 1)
                if w % 12 == 11:
                    rank_products(e, w // 12)

        def table_copies(e):
            def turned_x(w):
                e.wait_ge(s_xtr, w + 1)
                if w >= 2:
                    e.wait_ge(s_xm, 4 * (w - 1))
                e.activation(x_t[:, w % 2, :, :], pb[:, 4, 0:D].rearrange("p (k n) -> p k n", k=KC), ACT.Copy)\
                    .then_inc(s_xtc, 1)

            turned_x(0)
            for w in range(W):
                if w + 1 < W:
                    turned_x(w + 1)
                for n in range(4 * w, 4 * w + 4):
                    half = n // 2
                    e.wait_ge(s_xm, n + 1)
                    if n % 2 == 0 and half >= 2:
                        e.wait_ge(s_xst[half % 2], 16 * (half // 2))
                    e.activation(xt_out[:, half % 2, (n % 2) * 512:(n % 2 + 1) * 512], pb[:, n % 4, :], ACT.Copy)\
                        .then_inc(s_xe, 1)

        def rank_products(e, b):
            e.wait_ge(s_tot, b + 1)
            if b:
                e.wait_ge(s_win, b)
            e.matmul(pb[:, 5, 0:W], tri[:], tot, start=True, stop=True).then_inc(s_pre, 1)
            e.matmul(pb[:, 6, 0:W], ones[:, 0:P], tot, start=True, stop=True).then_inc(s_pre, 1)
            e.wait_ge(s_end, b + 1)
            e.transpose(pb[:, 7, 0:P], end_t, ident[:]).then_inc(s_endt, 1)
            e.wait_ge(s_cmp, b + 1)
            e.matmul(pb[0:1, 6, 0:BI], ones[:, 0:1], cmp_i, start=True, stop=True).then_inc(s_endt, 1)

        def ranks(e):
            c = Chain(e, s_rank)
            e.memset(acc[:], 0.0).then_inc(s_accz, 1)
            e.memset(x_in[:, 2, :], 0.0).then_inc(s_xz, 1)
            c(e.memset(end_t, 1e6))
            for b in range(BLOCKS):
                win = win_c[:, b * BT:(b + 1) * BT]
                pos = pos_c[:, b * BT:(b + 1) * BT]
                for w in range(W):
                    c(e.tensor_scalar(mask, win, float(w), None, ALU.is_equal))
                    c(e.tensor_tensor_scan(cum, ones[:, 0:BT], mask, 0.0, ALU.mult, ALU.add))
                    c(e.copy_predicated(pos, mask.bitcast(I32), cum))
                    c(e.tensor_copy(tot[:, w:w + 1], cum[:, BT - 1:BT]))
                e.sem_inc(s_tot, 1)
                e.wait_ge(s_pre, 2 * b + 2)
                c(e.tensor_scalar(tot_i, pb[:, 6, 0:W], float(P - 1), None, ALU.add))
                c(e.tensor_scalar(tot_i, tot_i, LOG_P, None, ALU.arith_shift_right))
                c(e.tensor_copy(offs, tot_i))
                c(e.tensor_tensor_scan(end_t[:, 0:W], ones[:, 0:W], offs, 0.0, ALU.mult, ALU.add))
                e.sem_inc(s_end, 1)
                c(e.tensor_tensor(offs, end_t[:, 0:W], offs, ALU.subtract))
                c(e.tensor_scalar(offs, offs, float(P), -1.0, ALU.mult, ALU.add))
                c(e.tensor_tensor(offs, offs, pb[:, 5, 0:W], ALU.add))
                for w in range(W):
                    c(e.tensor_scalar(tmp, win, float(w), offs[:, w:w + 1], ALU.is_equal, ALU.mult))
                    c(e.tensor_tensor(pos, pos, tmp, ALU.add))
                ints = int_c[:, 0:BT]
                c(e.tensor_copy(ints, pos))
                c(e.tensor_scalar(ints, ints, P - 1, None, ALU.bitwise_and))
                c(e.tensor_copy(q_c[:, b * BT:(b + 1) * BT], ints))
                c(e.tensor_copy(ints, pos))
                c(e.tensor_scalar(ints, ints, LOG_P, None, ALU.arith_shift_right))
                c(e.tensor_copy(c_c[:, b * BT:(b + 1) * BT], ints))
                e.wait_ge(s_endt, 2 * b + 1)
                c(e.tensor_copy(end_c, pb[:, 7, 0:1]))
                c(e.tensor_scalar(cmp_i, iota_q[:, 0:BI], end_c, None, ALU.is_ge))
                e.sem_inc(s_cmp, 1)
                e.wait_ge(s_endt, 2 * b + 2)
                c(e.tensor_scalar(table[0:1, b * BI:(b + 1) * BI], pb[0:1, 6, 0:BI], float(W - 1), float(AW),
                                  ALU.min, ALU.mult))
                e.sem_inc(s_win, 1)

        phase(sync=table_io, tensor=table_products, scalar=table_copies, vector=ranks)

        s_l0g = [sem(f"s_l0g{k}") for k in range(ITEM_U)]
        built, moved = Progress(sem("s_built"), 2), Progress(sem("s_moved"), 2)
        staged = Progress(sem("s_staged"), ITEM_U)
        hot, summed = Progress(sem("s_hot"), 3), Progress(sem("s_summed"), ITEM_U)
        added = Progress(sem("s_added"), 3)
        s_open, s_close, s_sorted, s_go0 = sem("s_open"), sem("s_close"), sem("s_sorted"), sem("s_go0")
        g_rows = rows_g[:].rearrange("p (s n) -> p s n", s=ITEM_U)
        hots = onehot[:].rearrange("p (s n) -> p s n", s=3)

        def l0_start(e, mine):
            for m in mine:
                m.start(e)

        def stage_of(st):
            perm = st if st < BLOCKS else None
            items = st - 1 if st > 0 else None
            return perm, items

        def l0_scalar(st):
            def go(e):
                _, ib = stage_of(st)
                if st == 0:
                    l0_start(e, [staged])
                if ib is None:
                    return
                with e.Fori(0, ROUNDS) as j:
                    for k in range(ITEM_U):
                        i = j * ITEM_U + (ib * BI + k)
                        summed.free(e, i, ITEM_U)
                        e.activation(stage_i[:, k:k + 1], idx_s[:, ib % 2, bass.ds(j * ITEM_U + k, 1)], ACT.Copy)\
                            .then_inc(staged.sem, 1)
            return go

        def l0_gather(st):
            def go(e):
                _, ib = stage_of(st)
                if ib is None:
                    return
                with e.Fori(0, ROUNDS) as j:
                    for k in range(ITEM_U):
                        staged.done(e, j * ITEM_U + (ib * BI + k))
                        e.sem_inc(s_go0, 1)
                        e.indirect_dma_start(g_rows[:, k, :], None, xt_table,
                                             bass.IndirectOffsetOnAxis(ap=stage_i[:, k:k + 1], axis=0))\
                            .then_inc(s_l0g[k], 16)
            return go

        def l0_tensor(st):
            def go(e):
                pb_, ib = stage_of(st)
                if st == 0:
                    l0_start(e, [moved, summed])
                if pb_ is not None:
                    for v in range(3):
                        ins = e.matmul(pb[:, v, 0:BI], zero_b[:, 0:P], zero_b[:, 0:BI], start=True, stop=False,
                                       skip_group_check=True)
                    ins.then_inc(s_open, 1)
                with e.Fori(0, ROUNDS) as j:
                    for k in range(ITEM_U):
                        if ib is not None:
                            i = j * ITEM_U + (ib * BI + k)
                            hot.done(e, i)
                            e.wait_ge(s_l0g[k], j * 16 + (ib * ROUNDS + 1) * 16)
                            added.free(e, i, 3)
                            e.matmul(pb[:, 3 + k % 3, 0:D], hots[:, k % 3, :], g_rows[:, k, :],
                                     start=True, stop=True).then_inc(summed.sem, 1)
                        if pb_ is not None and k < PERM_U:
                            built.done(e, j * PERM_U + (pb_ * BT + k))
                            for v in range(3):
                                ins = e.matmul(pb[:, v, 0:BI], hot_q[:, k % 2, v, :], hot_c[:, k % 2, :],
                                               start=False, stop=False, skip_group_check=True)
                            ins.then_inc(moved.sem, 1)
                if pb_ is not None:
                    for v in range(3):
                        ins = e.matmul(pb[:, v, 0:BI], zero_b[:, 0:P], zero_b[:, 0:BI], start=False, stop=True,
                                       skip_group_check=True)
                    ins.then_inc(s_close, 1)
            return go

        def l0_vector(st):
            def go(e):
                pb_, ib = stage_of(st)
                if st == 0:
                    l0_start(e, [built, hot, added])

                def add(j, k):
                    i = j * ITEM_U + (ib * BI + k)
                    at = e.value_load(table[0:1, bass.ds(j * ITEM_U + (ib * BI + k), 1)], min_val=0,
                                      max_val=(W - 1) * AW)
                    summed.done(e, i)
                    added.free(e, i, 1)
                    to = acc[:, bass.ds(at, D)]
                    e.tensor_tensor(to, to, pb[:, 3 + k % 3, 0:D], ALU.add).then_inc(added.sem, 1)

                with e.Fori(0, ROUNDS) as j:
                    for k in range(ITEM_U):
                        if ib is not None:
                            i = j * ITEM_U + (ib * BI + k)
                            summed.free(e, i, 3)
                            e.tensor_scalar(hots[:, k % 3, :], iota_q[:, 1:P + 1],
                                            loc_s[:, ib % 2, bass.ds(j * ITEM_U + k, 1)], None, ALU.is_equal)\
                                .then_inc(hot.sem, 1)
                        if pb_ is not None and k < PERM_U:
                            col = j * PERM_U + (pb_ * BT + k)
                            moved.free(e, j * PERM_U + (pb_ * BT + k), 2)
                            for v, byte in enumerate((lo_c, hi_c, loc_c)):
                                e.tensor_scalar(hot_q[:, k % 2, v, :], iota_q[:, 0:P], q_c[:, bass.ds(col, 1)],
                                                byte[:, bass.ds(col, 1)], ALU.is_equal, ALU.mult)
                            e.tensor_scalar(hot_c[:, k % 2, :], iota_q[:, 0:BI], c_c[:, bass.ds(col, 1)], None,
                                            ALU.is_equal).then_inc(built.sem, 1)
                        if ib is not None and k >= 2:
                            add(j, k - 2)
                    if ib is not None:
                        add(j, ITEM_U - 2)
                        add(j, ITEM_U - 1)
                if pb_ is not None:
                    e.wait_ge(s_close, pb_ + 1)
                    c = Chain(e, s_sorted)
                    c.n = 3 * pb_
                    c(e.tensor_copy(lo_s, pb[:, 0, 0:BI]))
                    c(e.scalar_tensor_tensor(idx_s[:, pb_ % 2, :], pb[:, 1, 0:BI], 256.0, lo_s, ALU.mult, ALU.add))
                    c(e.tensor_copy(loc_s[:, pb_ % 2, :], pb[:, 2, 0:BI]))
            return go

        for st in range(BLOCKS + 1):
            phase(scalar=l0_scalar(st), gpsimd=l0_gather(st), tensor=l0_tensor(st), vector=l0_vector(st))

        s_xall, s_wq, s_n1, s_stat, s_sq = sem("s_xall"), sem("s_wq"), sem("s_n1"), sem("s_stat"), sem("s_sq")
        s_norm, s_nt, s_ntc, s_qkv, s_qc, s_kvc = (sem(n) for n in (
            "s_norm", "s_nt", "s_ntc", "s_qkv", "s_qc", "s_kvc"))
        s_kvst = [sem("s_kvst0"), sem("s_kvst1")]
        s_x1st, s_iw, s_bef, s_cnt, s_tab, s_xpad = (sem(n) for n in (
            "s_x1st", "s_iw", "s_bef", "s_cnt", "s_tab", "s_xpad"))
        x1 = node_b[:].rearrange("p (w d) -> p w d", w=W)
        WQ = WALK // 4

        def mid_io(e):
            e.wait_ge(s_xpad, 1)
            full_w = N // P
            e.dma_start(x1[:, 0:full_w, :], a["x"][0:full_w * P, :].rearrange("(w p) d -> p w d", p=P))\
                .then_inc(s_xall, 16)
            e.dma_start(x1[0:N - full_w * P, full_w, :], a["x"][full_w * P:N, :]).then_inc(s_xall, 16)
            e.dma_start(bias0, a["L0_gnn_bias"].rearrange("(a d) -> a d", a=1).to_broadcast([P, D]))\
                .then_inc(s_xall, 16)
            for n, name in enumerate(("L1_gnn_Wq", "L1_gnn_Wk", "L1_gnn_Wv")):
                e.dma_start(wqkv[:, :, n * D:(n + 1) * D], a[name].rearrange("(k p) n -> p k n", p=P))\
                    .then_inc(s_wq, 16)
            for w in range(W):
                e.wait_ge(s_norm, w + 1)
                e.dma_start(x1_store[w * P:(w + 1) * P, :], x1[:, w, :]).then_inc(s_x1st, 16)
                e.wait_ge(s_kvc, w + 1)
                e.dma_start(k_table[w * P:(w + 1) * P, :], kv_out[:, w % 2, 0:D]).then_inc(s_kvst[w % 2], 16)
                e.dma_start(v_table[w * P:(w + 1) * P, :], kv_out[:, w % 2, D:2 * D]).then_inc(s_kvst[w % 2], 16)
            e.wait_ge(s_x1st, 16 * W)
            e.wait_ge(s_kvst[0], 32 * (W - W // 2))
            e.wait_ge(s_kvst[1], 32 * (W // 2))

        def mid_iota(e):
            e.iota(iota_w, [[1, WALK]], base=0, channel_multiplier=0, allow_small_or_imprecise_dtypes=True)\
                .then_inc(s_iw, 1)

        def mid_vector(e):
            c = Chain(e, s_n1)
            e.memset(x1[:, W - 1, :], 0.0).then_inc(s_xpad, 1)
            e.wait_ge(s_iw, 1)
            for g in range(RAW_G):
                if g >= 2:
                    e.wait_ge(s_cnt, g - 1)
                e.tensor_scalar(before[:, g % 2, :], iota_w, tile_u[:, g:g + 1], None, ALU.is_gt)\
                    .then_inc(s_bef, 1)
            e.wait_ge(s_xall, 48)
            for w in range(W):
                z = acc_w[:, w, 0:D]
                c(e.tensor_tensor(z, z, bias0, ALU.add))
                c(e.scalar_tensor_tensor(x1[:, w, :], z, 0.0, x1[:, w, :], ALU.max, ALU.add))
                c(e.bn_stats(stats[:, 0:6], x1[:, w, :]))
                c(e.bn_aggr(mv[:, 2 * w:2 * w + 2], stats[:, 0:6]))
            c(e.tensor_scalar(rstd[:], mv[:].rearrange("p (w t) -> p t w", t=2)[:, 1, :], EPS, None, ALU.add))
            e.sem_inc(s_stat, 1)
            e.wait_ge(s_cnt, RAW_G)
            for h in range(4):
                c(e.tensor_copy(table[0:1, h * WQ:(h + 1) * WQ], pb[0:1, h, 0:WQ]))
            at, ch = tile_at[0:1, :], chunk_at[0:1, :]
            c(e.tensor_copy(at, table[0:1, 0:WALK]))
            c(e.tensor_tensor(table[0:1, WALK:2 * WALK], iota_w[0:1, :], at, ALU.subtract))
            c(e.memset(ch, 0.0))
            for m in range(1, CH):
                c(e.scalar_tensor_tensor(ch, at, float(m * CJ), ch, ALU.is_ge, ALU.add))
            c(e.tensor_scalar(ch, ch, -float(CH * CJ - 1), None, ALU.mult))
            c(e.scalar_tensor_tensor(table[0:1, 0:WALK], at, float(CH), ch, ALU.mult, ALU.add))
            for cols in (src_c, dst_c, wgt_c):
                c(e.tensor_copy(scratch, cols[:]))
                c(e.tensor_copy(cols[:].rearrange("p (j c) -> p c j", c=CH),
                                scratch.rearrange("p (c j) -> p c j", c=CH)))
            e.sem_inc(s_tab, 1)
            e.wait_ge(s_sq, 1)
            c(e.reciprocal(rstd[:], rstd[:]))
            c(e.scalar_tensor_tensor(nmr[:], mv[:].rearrange("p (w t) -> p t w", t=2)[:, 0, :], -1.0, rstd[:],
                                     ALU.mult, ALU.mult))
            for w in range(W + 1):
                if w < W:
                    e.tensor_scalar(x1[:, w, :], x1[:, w, :], rstd[:, w:w + 1], nmr[:, w:w + 1], ALU.mult, ALU.add)\
                        .then_inc(s_norm, 1)
                if w >= 1:
                    e.wait_ge(s_qkv, 2 * w)
                    e.tensor_copy(acc_w[:, w - 1, 0:D], pb[:, 4 + (w - 1) % 2, 0:D]).then_inc(s_qc, 1)

        def mid_tensor(e):
            for g in range(RAW_G):
                e.wait_ge(s_bef, g + 1)
                for h in range(4):
                    ins = e.matmul(pb[0:1, h, 0:WQ], one_b, before[:, g % 2, h * WQ:(h + 1) * WQ],
                                   start=(g == 0), stop=(g == RAW_G - 1))
                ins.then_inc(s_cnt, 1)
            e.wait_ge(s_wq, 48)
            e.wait_ge(s_tab, 1)
            for w in range(W):
                e.wait_ge(s_norm, w + 1)
                if w >= 1:
                    e.wait_ge(s_ntc, w)
                for k in range(KC):
                    ins = e.transpose(pb[:, 0, k * P:(k + 1) * P], x1[:, w, k * P:(k + 1) * P], ident[:])
                ins.then_inc(s_nt, 1)
                e.wait_ge(s_ntc, w + 1)
                if w >= 2:
                    e.wait_ge(s_kvc, w - 1)
                    e.wait_ge(s_qc, w - 1)
                for k in range(KC):
                    ins = e.matmul(pb[:, 2 + w % 2, :], x1t[:, w % 2, k, :], wqkv[:, k, D:3 * D],
                                   start=(k == 0), stop=(k == KC - 1))
                ins.then_inc(s_qkv, 1)
                for k in range(KC):
                    ins = e.matmul(pb[:, 4 + w % 2, 0:D], x1t[:, w % 2, k, :], wqkv[:, k, 0:D],
                                   start=(k == 0), stop=(k == KC - 1))
                ins.then_inc(s_qkv, 1)

        def mid_scalar(e):
            e.wait_ge(s_stat, 1)
            e.activation(rstd[:], rstd[:], ACT.Sqrt).then_inc(s_sq, 1)
            for w in range(W):
                e.wait_ge(s_nt, w + 1)
                if w >= 2:
                    e.wait_ge(s_qkv, 2 * (w - 1))
                e.activation(x1t[:, w % 2, :, :], pb[:, 0, 0:D].rearrange("p (k n) -> p k n", k=KC), ACT.Copy)\
                    .then_inc(s_ntc, 1)
                e.wait_ge(s_qkv, 2 * w + 1)
                if w >= 2:
                    e.wait_ge(s_kvst[w % 2], 32 * (w // 2))
                e.activation(kv_out[:, w % 2, :], pb[:, 2 + w % 2, :], ACT.Copy).then_inc(s_kvc, 1)

        one_b = sb("one_b", 2, BF16)[:, 0:1]
        s_oneb = sem("s_oneb")

        def one_first(e):
            e.memset(one_b, 1.0).then_inc(s_oneb, 1)
            e.wait_ge(s_oneb, 1)

        phase(vector=one_first)
        phase(sync=mid_io, gpsimd=mid_iota, vector=mid_vector, tensor=mid_tensor, scalar=mid_scalar)

        s_kg = [sem(f"s_kg{k}") for k in range(WALK_U)]
        a_idx, a_dst = Progress(sem("s_a_idx"), WALK_U), Progress(sem("s_a_dst"), WALK_U)
        a_spread, a_hot = Progress(sem("s_a_spread"), 3), Progress(sem("s_a_hot"), 3)
        a_q, a_mul = Progress(sem("s_a_q"), WALK_U), Progress(sem("s_a_mul"), WALK_U)
        a_red, a_add = Progress(sem("s_a_red"), 2), Progress(sem("s_a_add"), 2)
        s_goa, s_bias = sem("s_goa"), sem("s_bias")
        prods = prod[:].rearrange("p (s n) -> p s n", s=2)
        parts = part[:].rearrange("p (s n) -> p s n", s=2)

        def tile_of(e, j, k):
            return e.value_load(table[0:1, bass.ds(j * WALK_U + k, 1)], min_val=0, max_val=T - 1)

        def window_of(e, j, k):
            return e.value_load(table[0:1, bass.ds(j * WALK_U + (WALK + k), 1)], min_val=0, max_val=W - 1)

        ROUNDS1 = WALK // WALK_U

        def a_scalar(e):
            a_idx.start(e)
            a_dst.start(e)
            with e.Fori(0, ROUNDS1) as j:
                for k in range(WALK_U):
                    i = j * WALK_U + k
                    t = tile_of(e, j, k)
                    a_mul.free(e, i, WALK_U)
                    e.activation(stage_i[:, k:k + 1], src_c[:, bass.ds(t, 1)], ACT.Copy).then_inc(a_idx.sem, 1)
                    e.activation(stage_d[:, k:k + 1], dst_c[:, bass.ds(t, 1)], ACT.Copy).then_inc(a_dst.sem, 1)

        def a_gather(e):
            with e.Fori(0, ROUNDS1) as j:
                for k in range(WALK_U):
                    a_idx.done(e, j * WALK_U + k)
                    e.sem_inc(s_goa, 1)
                    e.indirect_dma_start(g_rows[:, k, :], None, k_table,
                                         bass.IndirectOffsetOnAxis(ap=stage_i[:, k:k + 1], axis=0))\
                        .then_inc(s_kg[k], 16)

        def a_tensor(e):
            a_spread.start(e)
            a_q.start(e)

            def spread(j, k):
                i = j * WALK_U + k
                a_dst.done(e, i)
                a_hot.free(e, i, 2)
                e.matmul(pb[:, k % 2, 0:P], stage_d[:, k:k + 1].to_broadcast([P, P]), ident[:],
                         start=True, stop=True).then_inc(a_spread.sem, 1)

            def take_q(j, k):
                i = j * WALK_U + k
                w = window_of(e, j, k)
                a_hot.done(e, i)
                a_mul.free(e, i, 2)
                e.matmul(pb[:, 2 + k % 2, 0:D], hots[:, k % 2, :], acc[:, bass.ds(w * AW, D)],
                         start=True, stop=True).then_inc(a_q.sem, 1)

            with e.Fori(0, ROUNDS1) as j:
                for k in range(WALK_U):
                    spread(j, k)
                    if k:
                        take_q(j, k - 1)
                take_q(j, WALK_U - 1)

        def a_vector(e):
            for m in (a_hot, a_mul, a_red, a_add):
                m.start(e)
            e.tensor_copy(edge_s[:].rearrange("p (t h) -> p t h", h=HEADS),
                          wgt_c[:].unsqueeze(2).to_broadcast([P, T, HEADS])).then_inc(s_bias, 1)
            e.wait_ge(s_bias, 1)

            def hot_of(j, k):
                i = j * WALK_U + k
                w = window_of(e, j, k)
                a_spread.done(e, i)
                a_q.free(e, i, 2)
                e.tensor_scalar(hots[:, k % 2, :], pb[:, k % 2, 0:P], iota_p[:], win_pos[:, bass.ds(w, 1)],
                                ALU.subtract, ALU.is_equal).then_inc(a_hot.sem, 1)

            def multiply(j, k):
                i = j * WALK_U + k
                a_q.done(e, i)
                e.wait_ge(s_kg[k], j * 16 + 16)
                a_red.free(e, i, 2)
                e.tensor_tensor(prods[:, k % 2, :], g_rows[:, k, :], pb[:, 2 + k % 2, 0:D], ALU.mult)\
                    .then_inc(a_mul.sem, 1)

            def reduce(j, k):
                i = j * WALK_U + k
                a_mul.done(e, i)
                a_add.free(e, i, 2)
                e.tensor_reduce(parts[:, k % 2, :], prods[:, k % 2, :].rearrange("p (h d) -> p h d", h=HEADS),
                                AX.X, ALU.add).then_inc(a_red.sem, 1)

            def add(j, k):
                i = j * WALK_U + k
                t = tile_of(e, j, k)
                a_red.done(e, i)
                a_add.free(e, i, 1)
                to = edge_s[:, bass.ds(t * HEADS, HEADS)]
                e.scalar_tensor_tensor(to, parts[:, k % 2, :], SCALE, to, ALU.mult, ALU.add)\
                    .then_inc(a_add.sem, 1)

            with e.Fori(0, ROUNDS1) as j:
                for k in range(WALK_U + 2):
                    if k < WALK_U:
                        hot_of(j, k)
                    if 1 <= k <= WALK_U:
                        multiply(j, k - 1)
                    if k >= 2:
                        add_k = k - 2
                        reduce(j, add_k)
                        add(j, add_k)

        phase(scalar=a_scalar, gpsimd=a_gather, tensor=a_tensor, vector=a_vector)

        s_mt, s_mc, s_mp, s_ms = sem("s_mt"), sem("s_mc"), sem("s_mp"), sem("s_ms")
        s_ends, s_edge, s_car = sem("s_ends"), sem("s_edge"), sem("s_car")
        s_mb, s_sub, s_exp, s_dx = sem("s_mb"), sem("s_sub"), sem("s_exp"), sem("s_dx")
        PJ = 2
        PIECES = CJ // PJ

        def max_tensor(e):
            for n in range(PIECES):
                if n >= 2:
                    e.wait_ge(s_mc, n - 1)
                    e.wait_ge(s_mp, n - 1)
                e.wait_ge(s_dx, n + 1)
                for q in range(PJ):
                    j = n * PJ + q
                    e.transpose(pb[:, n % 2, q * P:(q + 1) * P], score_v[:, j, :], ident[:])
                    ins = e.transpose(pb[:, 2 + n % 2, q * P:(q + 1) * P], dst_x[:, n % 2, q * P:(q + 1) * P],
                                      ident[:])
                ins.then_inc(s_mt, 1)
            for r in range(3):
                e.wait_ge(s_ends, r + 1)
                e.transpose(pb[0:1, 4, r * P:(r + 1) * P], small[:, r:r + 1], ident[:]).then_inc(s_edge, 1)
            e.wait_ge(s_ends, 4)
            e.matmul(pb[:, 5, 0:1], row[8], ones[0:1, 0:1], start=True, stop=True).then_inc(s_edge, 1)
            e.wait_ge(s_ends, 5)
            e.transpose(pb[0:1, 6, 0:P], small[:, 3:4], ident[:]).then_inc(s_edge, 1)
            e.wait_ge(s_ends, 6)
            e.matmul(pb[:, 7, 0:1], row[8], ones[0:1, 0:1], start=True, stop=True).then_inc(s_edge, 1)
            e.wait_ge(s_car, 1)
            for n in range(PIECES):
                if n >= 2:
                    e.wait_ge(s_sub, n - 1)
                for q in range(PJ):
                    j = n * PJ + q
                    ins = e.transpose(pb[:, n % 2, q * P:(q + 1) * P], scan_s[:, j * P:(j + 1) * P], ident[:])
                ins.then_inc(s_mb, 1)

        def max_scalar(e):
            for n in range(PIECES):
                e.wait_ge(s_mt, n + 1)
                e.activation(scan_s[:, n * PJ * P:(n + 1) * PJ * P], pb[:, n % 2, 0:PJ * P], ACT.Copy)\
                    .then_inc(s_mc, 1)
            for c in range(CH):
                e.wait_ge(s_sub, PIECES)
                part_ = edge_s[:, c * CJ * HEADS:(c + 1) * CJ * HEADS]
                e.activation(part_, part_, ACT.Exp).then_inc(s_exp, 1)

        def max_vector(e):
            c = Chain(e, s_ms)
            PL = PJ * P

            def expand(n):
                if n >= 2:
                    e.wait_ge(s_mt, n - 1)
                e.tensor_copy(dst_x[:, n % 2, :].rearrange("p (n h) -> p n h", h=HEADS),
                              dst_c[:, n * PJ * CH:(n + 1) * PJ * CH].unsqueeze(2).to_broadcast([P, PJ * CH, HEADS]))\
                    .then_inc(s_dx, 1)

            expand(0)
            for n in range(PIECES):
                if n + 1 < PIECES:
                    expand(n + 1)
                e.wait_ge(s_mt, n + 1)
                if n:
                    c(e.tensor_copy(dst_t[:, 0:1], dst_t[:, PL:PL + 1]))
                ins = e.tensor_copy(dst_t[:, 1:PL + 1], pb[:, 2 + n % 2, 0:PL])
                ins.then_inc(s_mp, 1)
                e.wait_ge(s_mp, n + 1)
                if n == 0:
                    c(e.tensor_copy(dst_t[:, 0:1], dst_t[:, 1:2]))
                    c(e.tensor_copy(small[:, 0:1], dst_t[:, 1:2]))
                    e.sem_inc(s_ends, 1)
                c(e.tensor_tensor(same, dst_t[:, 1:PL + 1], dst_t[:, 0:PL], ALU.is_equal))
                c(e.tensor_scalar(pen[:, n * PL:(n + 1) * PL], same, 1.0, -LOW, ALU.subtract, ALU.mult))
            c(e.memset(pen[:, CL:CL + 1], 0.0))
            c(e.tensor_copy(small[:, 1:2], dst_t[:, PL:PL + 1]))
            e.sem_inc(s_ends, 1)
            e.wait_ge(s_mc, PIECES)
            c(e.tensor_tensor_scan(scan_s, pen[:, 0:CL], scan_s, LOW, ALU.add, ALU.max))
            c(e.tensor_copy(small[:, 2:3], scan_s[:, CL - 1:CL]))
            e.sem_inc(s_ends, 1)
            e.wait_ge(s_edge, 3)
            first, last, value, cont, whole, step, base, t0 = row[0:8]
            hc = "a (c h) -> a h c"

            def by_head(to, ps):
                c(e.tensor_copy(to.rearrange("a (h c) -> a h c", h=HEADS), ps.rearrange(hc, h=HEADS)))

            by_head(first, pb[0:1, 4, 0:P])
            by_head(last, pb[0:1, 4, P:2 * P])
            by_head(value, pb[0:1, 4, 2 * P:3 * P])
            c(e.memset(cont, 0.0))
            c(e.tensor_tensor(cont[:, 1:P], first[:, 1:P], last[:, 0:P - 1], ALU.is_equal))
            c(e.memset(cont.rearrange("a (h c) -> a h c", h=HEADS)[:, :, 0:1], 0.0))
            c(e.tensor_tensor(whole, first, last, ALU.is_equal))

            def carry_in(shift):
                c(e.memset(step, LOW))
                c(e.memset(base, LOW))
                if shift == 1:
                    here, there, flag = slice(1, P), slice(0, P - 1), cont[:, 1:P]
                else:
                    here, there, flag = slice(0, P - 1), slice(1, P), cont[:, 1:P]
                c(e.tensor_tensor(t0[:, 0:P - 1], flag, whole[:, there], ALU.mult))
                c(e.tensor_scalar(step[:, here], t0[:, 0:P - 1], 1.0, -LOW, ALU.subtract, ALU.mult))
                c(e.tensor_scalar(t0[:, 0:P - 1], flag, 1.0, -LOW, ALU.subtract, ALU.mult))
                c(e.tensor_tensor(base[:, here], value[:, there], t0[:, 0:P - 1], ALU.add))
                if shift == 1:
                    c(e.tensor_tensor_scan(row[9], step, base, LOW, ALU.add, ALU.max))
                else:
                    c(e.tensor_tensor_scan(row[9][:, ::-1], step[:, ::-1], base[:, ::-1], LOW, ALU.add, ALU.max))
                c(e.tensor_copy(row[8].rearrange("a (c h) -> a c h", h=HEADS),
                                row[9].rearrange("a (h c) -> a c h", h=HEADS)))
                e.sem_inc(s_ends, 1)

            carry_in(1)
            e.wait_ge(s_edge, 4)
            c(e.tensor_copy(carry[:, 0:1], pb[:, 5, 0:1]))
            c(e.tensor_tensor_scan(scan_s, pen[:, 0:CL], scan_s, carry[:, 0:1], ALU.add, ALU.max))
            back_s, back_p = scan_s[:, ::-1], pen[:, 1:CL + 1][:, ::-1]
            c(e.tensor_tensor_scan(back_s, back_p, back_s, LOW, ALU.add, ALU.max))
            c(e.tensor_copy(small[:, 3:4], scan_s[:, 0:1]))
            e.sem_inc(s_ends, 1)
            e.wait_ge(s_edge, 5)
            by_head(value, pb[0:1, 6, 0:P])
            carry_in(-1)
            e.wait_ge(s_edge, 6)
            c(e.tensor_copy(carry[:, 1:2], pb[:, 7, 0:1]))
            c(e.tensor_tensor_scan(back_s, back_p, back_s, carry[:, 1:2], ALU.add, ALU.max))
            e.sem_inc(s_car, 1)
            for n in range(PIECES):
                e.wait_ge(s_mb, n + 1)
                to = edge_s[:, n * PL:(n + 1) * PL]
                e.tensor_tensor(to, to, pb[:, n % 2, 0:PL], ALU.subtract).then_inc(s_sub, 1)

        phase(scalar=max_scalar, tensor=max_tensor, vector=max_vector)

        s_vg = [sem(f"s_vg{k}") for k in range(WALK_U)]
        b_idx, b_exp = Progress(sem("s_b_idx"), WALK_U), Progress(sem("s_b_exp"), WALK_U)
        b_hot, b_msg = Progress(sem("s_b_hot"), 3), Progress(sem("s_b_msg"), WALK_U)
        b_sum, b_add = Progress(sem("s_b_sum"), WALK_U), Progress(sem("s_b_add"), 2)
        s_gob, s_bz = sem("s_gob"), sem("s_bz")
        msgs = msg[:].rearrange("p (s n) -> p s n", s=3)

        def b_scalar(e):
            b_idx.start(e)
            b_exp.start(e)
            with e.Fori(0, ROUNDS1) as j:
                for k in range(WALK_U):
                    i = j * WALK_U + k
                    t = tile_of(e, j, k)
                    b_msg.free(e, i, WALK_U)
                    e.activation(stage_i[:, k:k + 1], src_c[:, bass.ds(t, 1)], ACT.Copy).then_inc(b_idx.sem, 1)
                    b_sum.free(e, i, 2)
                    e.activation(msgs[:, k % 2, D:AW], edge_s[:, bass.ds(t * HEADS, HEADS)], ACT.Copy)\
                        .then_inc(b_exp.sem, 1)

        def b_gather(e):
            with e.Fori(0, ROUNDS1) as j:
                for k in range(WALK_U):
                    b_idx.done(e, j * WALK_U + k)
                    e.sem_inc(s_gob, 1)
                    e.indirect_dma_start(g_rows[:, k, :], None, v_table,
                                         bass.IndirectOffsetOnAxis(ap=stage_i[:, k:k + 1], axis=0))\
                        .then_inc(s_vg[k], 16)

        def b_tensor(e):
            b_sum.start(e)
            with e.Fori(0, ROUNDS1) as j:
                for k in range(WALK_U):
                    i = j * WALK_U + k
                    b_hot.done(e, i)
                    b_msg.done(e, i)
                    b_add.free(e, i, 2)
                    e.matmul(pb[:, k % 2, 0:AW], hots[:, k % 2, :], msgs[:, k % 2, :], start=True, stop=True)\
                        .then_inc(b_sum.sem, 1)

        def b_vector(e):
            for m in (b_hot, b_msg, b_add):
                m.start(e)
            e.memset(acc[:], 0.0).then_inc(s_bz, 1)
            e.wait_ge(s_bz, 1)

            def add(j, k):
                i = j * WALK_U + k
                w = window_of(e, j, k)
                b_sum.done(e, i)
                b_add.free(e, i, 1)
                to = acc[:, bass.ds(w * AW, AW)]
                e.tensor_tensor(to, to, pb[:, k % 2, 0:AW], ALU.add).then_inc(b_add.sem, 1)

            with e.Fori(0, ROUNDS1) as j:
                for k in range(WALK_U):
                    i = j * WALK_U + k
                    t, w = tile_of(e, j, k), window_of(e, j, k)
                    b_sum.free(e, i, 2)
                    e.tensor_scalar(hots[:, k % 2, :], iota_q[:, 0:P], dst_c[:, bass.ds(t, 1)],
                                    win_neg[:, bass.ds(w, 1)], ALU.subtract, ALU.is_equal).then_inc(b_hot.sem, 1)
                    e.wait_ge(s_vg[k], j * 16 + 16)
                    b_exp.done(e, i)
                    e.tensor_tensor(msgs[:, k % 2, 0:D].rearrange("p (h d) -> p h d", h=HEADS),
                                    g_rows[:, k, :].rearrange("p (h d) -> p h d", h=HEADS),
                                    msgs[:, k % 2, D:AW].unsqueeze(2).to_broadcast([P, HEADS, HD]), ALU.mult)\
                        .then_inc(b_msg.sem, 1)
                    if k:
                        add(j, k - 1)
                add(j, WALK_U - 1)

        phase(scalar=b_scalar, gpsimd=b_gather, tensor=b_tensor, vector=b_vector)

        s_fw, s_x1l = sem("s_fw"), sem("s_x1l")
        s_fc, s_att, s_ft, s_ftc, s_fp, s_fz = (sem(n) for n in ("s_fc", "s_att", "s_ft", "s_ftc", "s_fp", "s_fz"))
        s_fsq, s_fst = sem("s_fsq"), sem("s_fst")
        s_h1, s_h1t, s_h1c, s_hm, s_hg, s_ym, s_yz = (sem(n) for n in (
            "s_h1", "s_h1t", "s_h1c", "s_hm", "s_hg", "s_ym", "s_yz"))
        s_res, s_store = sem("s_res"), sem("s_store")
        groups = [list(range(g, min(g + 4, W))) for g in range(0, W, 4)]

        def f_io(e):
            e.dma_start(x1, x1_store.rearrange("(w p) d -> p w d", p=P)).then_inc(s_x1l, 16)
            e.dma_start(wp, a["L1_gnn_Wp"].rearrange("(k p) n -> p k n", p=P)).then_inc(s_fw, 16)
            e.dma_start(w1, a["L1_gnn_W1"].rearrange("(k p) n -> p k n", p=P)).then_inc(s_fw, 16)
            e.dma_start(w2, a["L1_gnn_W2"].rearrange("(k p) n -> p k n", p=P)).then_inc(s_fw, 16)
            e.dma_start(b1c, a["L1_gnn_b1"].rearrange("(k p) -> p k", p=P), allow_slow_non_contiguous=True)\
                .then_inc(s_fw, 16)
            for n in vec:
                e.dma_start(vec[n], a["L1_gnn_" + n].rearrange("(a d) -> a d", a=1).to_broadcast([P, D]))\
                    .then_inc(s_fw, 16)
            for w in range(W):
                e.wait_ge(s_res, w + 1)
                e.dma_start(out[w * P:w * P + node_rows(w), :], x1[0:node_rows(w), w, :]).then_inc(s_store, 16)
            e.wait_ge(s_store, 16 * W)

        def f_vector(e):
            c = Chain(e, s_fc)
            e.wait_ge(s_fw, 16 * (4 + len(vec)))
            e.wait_ge(s_x1l, 16)

            def stat(w, z):
                c(e.bn_stats(stats[:, 0:6], z))
                c(e.bn_aggr(mv[:, 2 * w:2 * w + 2], stats[:, 0:6]))

            def roots(n):
                c(e.tensor_scalar(rstd[:], mv[:].rearrange("p (w t) -> p t w", t=2)[:, 1, :], EPS, None, ALU.add))
                e.sem_inc(s_fst, 1)
                e.wait_ge(s_fsq, n)
                c(e.reciprocal(rstd[:], rstd[:]))
                c(e.scalar_tensor_tensor(nmr[:], mv[:].rearrange("p (w t) -> p t w", t=2)[:, 0, :], -1.0, rstd[:],
                                         ALU.mult, ALU.mult))

            def norm(z, w, g, b):
                c(e.tensor_scalar(z, z, rstd[:, w:w + 1], nmr[:, w:w + 1], ALU.mult, ALU.add))
                c(e.tensor_tensor(z, z, vec[g], ALU.mult))
                c(e.tensor_tensor(z, z, vec[b], ALU.add))

            for w in range(W + 1):
                if w < W:
                    if w >= 2:
                        e.wait_ge(s_ft, w - 1)
                    c(e.tensor_scalar(recip[:, w % 2, :], acc_w[:, w, D:AW], 1e-30, None, ALU.max))
                    c(e.reciprocal(recip[:, w % 2, :], recip[:, w % 2, :]))
                    e.tensor_tensor(att[:, w % 2, :].rearrange("p (h d) -> p h d", h=HEADS),
                                    acc_w[:, w, 0:D].rearrange("p (h d) -> p h d", h=HEADS),
                                    recip[:, w % 2, :].unsqueeze(2).to_broadcast([P, HEADS, HD]), ALU.mult)\
                        .then_inc(s_att, 1)
                if w >= 1:
                    v = w - 1
                    z = acc_w[:, v, 0:D]
                    e.wait_ge(s_fp, v + 1)
                    e.wait_ge(s_att, v + 1)
                    e.tensor_tensor(z, pb[:, 2 + v % 2, 0:D], x1[:, v, :], ALU.add).then_inc(s_fz, 1)
                    e.wait_ge(s_fz, v + 1)
                    c(e.tensor_tensor(z, z, vec["bp"], ALU.add))
                    stat(v, z)
            roots(1)
            n = 0
            for g, ws in enumerate(groups + [None]):
                if ws:
                    for w in ws:
                        norm(acc_w[:, w, 0:D], w, "ln1_g", "ln1_b")
                    e.sem_inc(s_h1, 1)
                if g:
                    for v in groups[g - 1]:
                        z = acc_w[:, v, 0:D]
                        e.wait_ge(s_ym, n + 1)
                        e.tensor_tensor(z, z, pb[:, 6 + n % 2, 0:D], ALU.add).then_inc(s_yz, 1)
                        n += 1
                        e.wait_ge(s_yz, n)
                        c(e.tensor_tensor(z, z, vec["b2"], ALU.add))
            for w in range(W):
                stat(w, acc_w[:, w, 0:D])
            roots(2)
            for w in range(W):
                z = acc_w[:, w, 0:D]
                norm(z, w, "ln2_g", "ln2_b")
                c(e.tensor_tensor(z, z, x1[:, w, :], ALU.add))
                stat(w, z)
            roots(3)
            for w in range(W):
                e.tensor_scalar(x1[:, w, :], acc_w[:, w, 0:D], rstd[:, w:w + 1], nmr[:, w:w + 1], ALU.mult, ALU.add)\
                    .then_inc(s_res, 1)

        def f_tensor(e):
            e.wait_ge(s_fw, 16 * (4 + len(vec)))
            for w in range(W):
                e.wait_ge(s_att, w + 1)
                if w >= 1:
                    e.wait_ge(s_ftc, w)
                for k in range(KC):
                    ins = e.transpose(pb[:, 0, k * P:(k + 1) * P], att[:, w % 2, k * P:(k + 1) * P], ident[:])
                ins.then_inc(s_ft, 1)
                e.wait_ge(s_ftc, w + 1)
                if w >= 2:
                    e.wait_ge(s_fz, w - 1)
                for k in range(KC):
                    ins = e.matmul(pb[:, 2 + w % 2, 0:D], att_t[:, w % 2, k, :], wp[:, k, :],
                                   start=(k == 0), stop=(k == KC - 1))
                ins.then_inc(s_fp, 1)
            n = m = t = 0
            for g, ws in enumerate(groups):
                cols = len(ws) * P
                e.wait_ge(s_h1, g + 1)
                for i, w in enumerate(ws):
                    if t >= 2:
                        e.wait_ge(s_h1c, t - 1)
                    for k in range(KC):
                        ins = e.transpose(pb[:, t % 2, k * P:(k + 1) * P], acc_w[:, w, k * P:(k + 1) * P], ident[:])
                    ins.then_inc(s_h1t, 1)
                    t += 1
                e.wait_ge(s_h1c, t)
                for f in range(FC):
                    if m >= 2:
                        e.wait_ge(s_hg, m - 1)
                    for k in range(KC):
                        ins = e.matmul(pb[:, 4 + m % 2, 0:cols], w1[:, k, f * P:(f + 1) * P], h1_t[:, k, 0:cols],
                                       start=(k == 0), stop=(k == KC - 1))
                    ins.then_inc(s_hm, 1)
                    m += 1
                e.wait_ge(s_hg, m)
                for i, w in enumerate(ws):
                    if n >= 2:
                        e.wait_ge(s_yz, n - 1)
                    for f in range(FC):
                        ins = e.matmul(pb[:, 6 + n % 2, 0:D], hid[:, f, i * P:(i + 1) * P], w2[:, f, :],
                                       start=(f == 0), stop=(f == FC - 1))
                    ins.then_inc(s_ym, 1)
                    n += 1

        def f_scalar(e):
            e.wait_ge(s_fw, 16 * (4 + len(vec)))
            for w in range(W):
                e.wait_ge(s_ft, w + 1)
                if w >= 2:
                    e.wait_ge(s_fp, w - 1)
                e.activation(att_t[:, w % 2, :, :], pb[:, 0, 0:D].rearrange("p (k n) -> p k n", k=KC), ACT.Copy)\
                    .then_inc(s_ftc, 1)
            e.wait_ge(s_fst, 1)
            e.activation(rstd[:], rstd[:], ACT.Sqrt).then_inc(s_fsq, 1)
            m = t = n = 0
            for g, ws in enumerate(groups):
                cols = len(ws) * P
                for i, w in enumerate(ws):
                    e.wait_ge(s_h1t, t + 1)
                    e.wait_ge(s_hm, g * FC) if g else None
                    e.activation(h1_t[:, :, i * P:(i + 1) * P],
                                 pb[:, t % 2, 0:D].rearrange("p (k n) -> p k n", k=KC), ACT.Copy).then_inc(s_h1c, 1)
                    t += 1
                for f in range(FC):
                    e.wait_ge(s_hm, m + 1)
                    if g:
                        e.wait_ge(s_ym, n)
                    e.activation(hid[:, f, 0:cols], pb[:, 4 + m % 2, 0:cols], ACT.Gelu, bias=b1c[:, f:f + 1])\
                        .then_inc(s_hg, 1)
                    m += 1
                n += len(ws)
            e.wait_ge(s_fst, 2)
            e.activation(rstd[:], rstd[:], ACT.Sqrt).then_inc(s_fsq, 1)
            e.wait_ge(s_fst, 3)
            e.activation(rstd[:], rstd[:], ACT.Sqrt).then_inc(s_fsq, 1)

        phase(sync=f_io, vector=f_vector, tensor=f_tensor, scalar=f_scalar)

        block = ctx.enter_context(nc.Block())

        def run(e, name):
            for todo in engines[name]:
                if todo is not None:
                    todo(e)
                meet(e)

        @block.sync
        def _(e):
            run(e, "sync")

        @block.gpsimd
        def _(e):
            run(e, "gpsimd")

        @block.scalar
        def _(e):
            run(e, "scalar")

        @block.tensor
        def _(e):
            run(e, "tensor")

        @block.vector
        def _(e):
            run(e, "vector")


INPUTS = ["x", "src", "dst", "edge_type_8", "edge_weight1", "L0_gnn_weight", "L0_gnn_bias", "L1_gnn_Wq",
          "L1_gnn_Wk", "L1_gnn_Wv", "L1_gnn_Wp", "L1_gnn_bp", "L1_gnn_ln1_g", "L1_gnn_ln1_b", "L1_gnn_ln2_g",
          "L1_gnn_ln2_b", "L1_gnn_W1", "L1_gnn_b1", "L1_gnn_W2", "L1_gnn_b2"]


def kernel(**inputs):
    import concourse.bacc as bacc
    from concourse.bass_utils import run_bass_kernel_spmd

    nc = bacc.Bacc("TRN2", target_bir_lowering=False, num_devices=1)
    arrays, args = {}, {}
    for name in INPUTS:
        v = np.ascontiguousarray(inputs[name])
        if name == "edge_weight1":
            v = v.reshape(-1)
        arrays["in_" + name] = v
        args[name] = nc.dram_tensor("in_" + name, v.shape, mybir.dt.from_np(v.dtype), kind="ExternalInput").ap()
    out = nc.dram_tensor("out", (N, D), F32, kind="ExternalOutput").ap()
    build(nc, args, out)
    return run_bass_kernel_spmd(nc, [arrays], core_ids=[0]).results[0]["out"]
```

```python
from contextlib import ExitStack

import numpy as np

import concourse.bass as bass
from concourse import mybir

F32 = mybir.dt.float32
BF16 = mybir.dt.bfloat16
I32 = mybir.dt.int32
ALU = mybir.AluOpType
ACT = mybir.ActivationFunctionType
AX = mybir.AxisListType

P = 128
N, D, E = 6250, 256, 200000
REL, HEADS = 8, 8
HD = D // HEADS
FFN = 4 * D
FC = FFN // P
KC = D // P
LOG_P = 7
W = -(-N // P)
NP_ = W * P
JUNK = NP_ - 1
BLOCKS = 4
PERM_U, ITEM_U, ROUNDS = 8, 9, 49
BT = PERM_U * ROUNDS
T = BLOCKS * BT
BI = ITEM_U * ROUNDS
assert T * P >= E and BI * P >= BT * P + W * (P - 1) - P
RAW_G = -(-T // P)
WALK = T + W - 1
QUAD = 4
QUADS = WALK // QUAD
assert WALK % QUAD == 0
ROW_RING = 4
AW = D + HEADS
CH = P // HEADS
CJ = WALK // CH
CL = CJ * P
assert CH * CJ == WALK
DST, SRC, WGT, REC = 0, 1, 2, 4
LOW = -1e30
EPS = 1e-5
SCALE = 1.0 / float(np.sqrt(HD))


class Progress:

    def __init__(self, sem, ring):
        self.sem, self.ring = sem, ring

    def start(self, e):
        e.sem_inc(self.sem, self.ring)

    def done(self, e, i):
        e.wait_ge(self.sem, i + (1 + self.ring))

    def free(self, e, i, ring):
        e.wait_ge(self.sem, i + (1 + self.ring - ring))


class Count:

    def __init__(self, sem):
        self.sem = sem

    def done(self, e, i):
        e.wait_ge(self.sem, i + 1)

    def free(self, e, i, ring):
        if i >= ring:
            e.wait_ge(self.sem, i - ring + 1)


class Chain:

    def __init__(self, e, sem):
        self.e, self.sem, self.n = e, sem, 0

    def __call__(self, ins):
        ins.then_inc(self.sem, 1)
        self.n += 1
        self.e.wait_ge(self.sem, self.n)


def build(nc, a, out):
    ctx = ExitStack()
    with ctx:
        def sb(name, cols, dt=F32, rows=P):
            return ctx.enter_context(nc.sbuf_tensor(name, [rows, cols], dt))

        def sem(name):
            return ctx.enter_context(nc.semaphore(name))

        def dram(name, shape, dt=F32):
            return nc.dram_tensor(name, shape, dt, kind="Internal").ap()

        xt_table = dram("xt_table", (REL * NP_, D))
        k_table = dram("k_table", (NP_, D))
        v_table = dram("v_table", (NP_, D))
        x1_store = dram("x1_store", (NP_, D))
        edge_table = dram("edge_table", (T, P * REC))

        node_a = sb("node_a", W * AW)
        node_b = sb("node_b", W * D)
        edge_s = sb("edge_s", WALK * HEADS)
        src_i, dst_i = sb("src_i", WALK, I32), sb("dst_i", WALK)
        dl_i, dl_b = sb("dl_i", WALK), sb("dl_b", WALK, BF16)
        table = sb("table", max(BLOCKS * BI, WALK), I32)
        stage_i = sb("stage_i", ITEM_U, I32)
        iota_q = sb("iota_q", 512)
        iota_p = sb("iota_p", 1)
        ident, tri, ones = sb("ident", P), sb("tri", P), sb("ones", 512)
        ident_b = sb("ident_b", P, BF16)
        stats = sb("stats", 2 * 6)
        mv = sb("mv", W * 2)
        rstd, nmr = sb("rstd", W), sb("nmr", W)
        small = sb("small", 64)
        pb = ctx.enter_context(nc.psum_tensor("pb", [P, 8, 512], F32))

        class Cut:

            def __init__(self, region):
                self.region, self.at = region, 0

            def __call__(self, cols, dt=F32):
                words = cols if dt in (F32, I32) else -(-cols // 2)
                piece = self.region[:, self.at:self.at + words]
                self.at += words
                assert self.at <= self.region.shape[1]
                return piece if dt == F32 else piece.bitcast(dt)[:, 0:cols]

        cut = Cut(node_a)
        raw_i = {n: cut(RAW_G * P, I32) for n in ("src", "dst", "type")}
        raw_w = cut(RAW_G * P)
        rec = node_b[:, 0:RAW_G * P * REC].rearrange("p (g e f) -> p g e f", g=RAW_G, e=P)
        raw_f = {n: cut(RAW_G * P) for n in ("src", "dst", "row")}
        acc = node_a
        acc_w = node_a[:].rearrange("p (w d) -> p w d", w=W)
        cut = Cut(edge_s)
        win_c, loc_c, lo_c, hi_c, pos_c, q_c, c_c = (cut(T) for _ in range(7))
        int_c = cut(T, I32)
        cut = Cut(node_b)
        w0 = cut(KC * REL * D).rearrange("p (k r o) -> p k r o", k=KC, r=REL)
        xt_out = cut(2 * 4 * D).rearrange("p (s n) -> p s n", s=2)
        x_in = cut(3 * D).rearrange("p (s n) -> p s n", s=3)
        x_t = cut(2 * D).rearrange("p (s k n) -> p s k n", s=2, k=KC)
        mask, cum, tmp = cut(BT), cut(BT), cut(BT)
        tot, offs, end_t = cut(W), cut(W), cut(P)
        tot_i = cut(W, I32)
        end_c, cmp_i = cut(1), cut(BI)
        idx_s = cut(2 * BI, I32).rearrange("p (s n) -> p s n", s=2)
        loc_s = cut(2 * BI).rearrange("p (s n) -> p s n", s=2)
        lo_s = cut(BI)
        hot_q = cut(2 * 3 * P, BF16).rearrange("p (s v q) -> p s v q", s=2, v=3)
        hot_c = cut(2 * BI + 2, BF16)[:, 0:2 * BI].rearrange("p (s n) -> p s n", s=2)
        g_rows = w0.rearrange("p k r o -> p (k r o)")[:, 0:ITEM_U * D].rearrange("p (s n) -> p s n", s=ITEM_U)
        hots = sb("hots", 3 * P)[:].rearrange("p (s n) -> p s n", s=3)
        zero_b = sb("zero_b", 448, BF16)[:]
        cut = Cut(edge_s)
        wqkv = cut(KC * 3 * D).rearrange("p (k n) -> p k n", k=KC)
        bias0 = cut(D)
        x1t = cut(2 * D).rearrange("p (s k n) -> p s k n", s=2, k=KC)
        kv_out = cut(2 * 2 * D).rearrange("p (s n) -> p s n", s=2)
        cut = Cut(node_b)
        recs = cut(RAW_G * P * REC).rearrange("p (g e f) -> p g e f", g=RAW_G, e=P)
        u_row, w_row, wgt_i = cut(RAW_G * P), cut(RAW_G * P), cut(WALK)
        item_col, u_col, t_col = cut(RAW_G), cut(RAW_G), cut(RAW_G)
        u_int, t_int = cut(RAW_G, I32), cut(RAW_G, I32)
        item_row = edge_s[:, 0:WALK]
        cut = Cut(node_b)
        rows = cut(ROW_RING * QUAD * D).rearrange("p (s k n) -> p s k n", s=ROW_RING, k=QUAD)
        w_hot = cut(2 * QUAD * P).rearrange("p (s n) -> p s n", s=2)
        prods = cut(2 * QUAD * D).rearrange("p (s n) -> p s n", s=2)
        parts = cut(2 * QUAD * HEADS).rearrange("p (s n) -> p s n", s=2)
        msgs = cut(2 * QUAD * AW).rearrange("p (s k n) -> p s k n", s=2, k=QUAD)
        cut = Cut(edge_s)
        wp = cut(KC * D).rearrange("p (k n) -> p k n", k=KC)
        w1 = cut(KC * FFN).rearrange("p (k n) -> p k n", k=KC)
        w2 = cut(FC * D).rearrange("p (k n) -> p k n", k=FC)
        vec = {n: cut(D) for n in ("bp", "ln1_g", "ln1_b", "ln2_g", "ln2_b", "b2")}
        b1c = cut(FC)
        att = cut(2 * D).rearrange("p (s n) -> p s n", s=2)
        att_t = cut(2 * D).rearrange("p (s k n) -> p s k n", s=2, k=KC)
        h1_t = cut(KC * 512).rearrange("p (k n) -> p k n", k=KC)
        hid = cut(FC * 512).rearrange("p (k n) -> p k n", k=FC)
        recip = cut(HEADS * 2).rearrange("p (s n) -> p s n", s=2)
        scan_s = node_a[:, 0:CL]
        pen = node_b[:, 0:CL // 2 + 1].bitcast(BF16)[:, 0:CL + 1]
        dst_t = node_b[:, CL // 2 + 1:CL // 2 + 1 + 257]
        same = node_b[:, CL // 2 + 300:CL // 2 + 556]
        row = [node_b[0:1, CL // 2 + 600 + 130 * i:CL // 2 + 600 + 130 * i + P] for i in range(12)]
        carry = node_b[:, CL // 2 + 2400:CL // 2 + 2402]
        score_v = edge_s[:].rearrange("p (j n) -> p j n", j=CJ)
        dst_x = node_b[:, CL // 2 + 2410:CL // 2 + 2410 + 512].rearrange("p (s n) -> p s n", s=2)

        s_meet = sem("s_meet")
        meets = {}

        def meet(e):
            k = meets[e] = meets.get(e, 0) + 1
            e.drain().then_inc(s_meet, 1)
            e.wait_ge(s_meet, 5 * k)

        engines = {n: [] for n in ("sync", "gpsimd", "scalar", "tensor", "vector")}

        def phase(**parts):
            for n, todo in engines.items():
                todo.append(parts.get(n))

        s_padded, s_consts, s_rawload = sem("s_padded"), sem("s_consts"), sem("s_rawload")
        s_float, s_turned, s_cols = sem("s_float"), sem("s_turned"), sem("s_cols")
        s_dv0, s_gp0 = sem("s_dv0"), sem("s_gp0")
        full = (E // P)
        whole = full // P
        rest, tail = full - whole * P, E - full * P
        turned = [("src", raw_f["src"], c_c), ("row", raw_f["row"], pos_c)]
        packs = [(v, g) for v in range(len(turned)) for g in range(0, RAW_G, 4)]
        s_recz, s_rec, s_recout = sem("s_recz"), sem("s_rec"), sem("s_recout")

        def load_edges(e):
            e.wait_ge(s_padded, 4)
            for name, to in (("src", raw_i["src"]), ("dst", raw_i["dst"]),
                             ("edge_type_8", raw_i["type"]), ("edge_weight1", raw_w)):
                v = to.rearrange("p (g e) -> p g e", e=P)
                d = a[name]
                e.dma_start(v[:, 0:whole, :], d[0:whole * P * P].rearrange("(g p e) -> p g e", p=P, e=P))\
                    .then_inc(s_rawload, 16)
                e.dma_start(v[0:rest, whole, :], d[whole * P * P:full * P].rearrange("(p e) -> p e", e=P))\
                    .then_inc(s_rawload, 16)
                e.dma_start(v[rest:rest + 1, whole, 0:tail], d[full * P:E].rearrange("(a e) -> a e", a=1))\
                    .then_inc(s_rawload, 16)
            e.wait_ge(s_rec, 3)
            g = T // P
            for lo, hi, rows_ in ((0, g, P), (g, RAW_G, T - g * P)):
                e.dma_start(edge_table[lo * P:lo * P + (hi - lo) * rows_, :].rearrange("(g p) n -> p g n", p=rows_),
                            rec[0:rows_, lo:hi, :, :].rearrange("p g e f -> p g (e f)")).then_inc(s_recout, 16)
            e.wait_ge(s_recout, 32)

        def make_consts(e):
            c = Chain(e, s_gp0)
            e.memset(rec, 0.0).then_inc(s_recz, 1)
            c(e.memset(ident[:], 0.0))
            c(e.affine_select(out=ident[:], in_=ident[:], compare_op=ALU.not_equal, fill=1.0, base=0,
                              pattern=[[-1, P]], channel_multiplier=1))
            c(e.memset(ones[:], 1.0))
            c(e.affine_select(out=tri[:], in_=ones[:, 0:P], compare_op=ALU.is_gt, fill=0.0, base=0,
                              pattern=[[1, P]], channel_multiplier=-1))
            c(e.iota(iota_q[:], [[1, 512]], base=0, channel_multiplier=0, allow_small_or_imprecise_dtypes=True))
            c(e.iota(iota_p[:], [[1, 1]], base=0, channel_multiplier=1, allow_small_or_imprecise_dtypes=True))
            c(e.tensor_copy(ident_b[:], ident[:]))
            e.sem_inc(s_consts, 1)

        def edges_float(e):
            e.memset(raw_i["src"], JUNK).then_inc(s_padded, 1)
            e.memset(raw_i["dst"], JUNK).then_inc(s_padded, 1)
            e.memset(raw_i["type"], 0).then_inc(s_padded, 1)
            e.memset(raw_w, 0.0).then_inc(s_padded, 1)
            e.wait_ge(s_rawload, 16 * 12)
            e.tensor_copy(raw_f["src"], raw_i["src"]).then_inc(s_float, 1)
            e.tensor_copy(raw_f["dst"], raw_i["dst"]).then_inc(s_float, 1)
            e.scalar_tensor_tensor(raw_f["row"], raw_i["type"], float(NP_), raw_i["dst"], ALU.mult, ALU.add)\
                .then_inc(s_float, 1)
            c = Chain(e, s_dv0)
            e.wait_ge(s_cols, len(packs))
            for src, sh, ms, to, one in ((c_c, LOG_P, None, win_c, 0), (c_c, None, P - 1, loc_c, 1),
                                         (pos_c, 8, None, hi_c, 0), (pos_c, None, 255, lo_c, 0)):
                c(e.tensor_copy(int_c, src))
                if sh is not None:
                    c(e.tensor_scalar(int_c, int_c, sh, None, ALU.arith_shift_right))
                else:
                    c(e.tensor_scalar(int_c, int_c, ms, None, ALU.bitwise_and))
                c(e.tensor_scalar(to, int_c, float(one), None, ALU.add))
            c(e.memset(zero_b, 0.0))

        def edges_turn(e):
            e.wait_ge(s_consts, 1)
            e.wait_ge(s_float, 3)
            for n, (v, g0) in enumerate(packs):
                if n >= 4:
                    e.wait_ge(s_cols, n - 3)
                for g in range(g0, min(g0 + 4, RAW_G)):
                    ins = e.transpose(pb[:, n % 4, (g - g0) * P:(g - g0 + 1) * P],
                                      turned[v][1].rearrange("p (g e) -> p g e", e=P)[:, g, :], ident[:])
                ins.then_inc(s_turned, 1)

        def edges_cols(e):
            e.wait_ge(s_recz, 1)
            e.wait_ge(s_float, 3)
            for f, v in ((DST, raw_f["dst"]), (SRC, raw_f["src"]), (WGT, raw_w)):
                e.activation(rec[:, :, :, f], v.rearrange("p (g e) -> p g e", e=P), ACT.Copy).then_inc(s_rec, 1)
            for n, (v, g0) in enumerate(packs):
                e.wait_ge(s_turned, n + 1)
                cols = min(T - g0 * P, 512)
                to = turned[v][2]
                e.activation(to[:, g0 * P:g0 * P + cols], pb[:, n % 4, 0:cols], ACT.Copy).then_inc(s_cols, 1)

        phase(sync=load_edges, gpsimd=make_consts, vector=edges_float, tensor=edges_turn, scalar=edges_cols)

        s_w0, s_x = sem("s_w0"), [sem("s_x0"), sem("s_x1")]
        s_xz, s_xtr, s_xtc, s_xm, s_xe = sem("s_xz"), sem("s_xtr"), sem("s_xtc"), sem("s_xm"), sem("s_xe")
        s_xst = [sem("s_xst0"), sem("s_xst1")]
        s_rank, s_tot, s_pre, s_end, s_endt, s_cmp, s_win = (sem(n) for n in (
            "s_rank", "s_tot", "s_pre", "s_end", "s_endt", "s_cmp", "s_win"))
        s_accz = sem("s_accz")
        xt_v = xt_table.rearrange("(r n) o -> n r o", r=REL)
        HALF = 4 * D

        def node_rows(w):
            return min(N - w * P, P)

        def x_slot(w):
            return 2 if w == W - 1 else w % 2

        def table_io(e):
            for k in range(KC):
                e.dma_start(w0[:, k, :, :], a["L0_gnn_weight"][:, k * P:(k + 1) * P, :].rearrange("r p o -> p r o"))\
                    .then_inc(s_w0, 16)

            def store(n):
                w, half = divmod(n, 2)
                e.wait_ge(s_xe, 2 * (n + 1))
                e.dma_start(xt_v[w * P:(w + 1) * P, half * 4:half * 4 + 4, :],
                            xt_out[:, n % 2, :].rearrange("p (r o) -> p r o", r=4)).then_inc(s_xst[n % 2], 16)

            for w in range(W + 1):
                if w < W:
                    if w == W - 1:
                        e.wait_ge(s_xz, 1)
                    elif w >= 2:
                        e.wait_ge(s_xtr, w - 1)
                    e.dma_start(x_in[0:node_rows(w), x_slot(w), :], a["x"][w * P:w * P + node_rows(w), :])\
                        .then_inc(s_x[w % 2], 16)
                if w >= 1:
                    store(2 * w - 2)
                    store(2 * w - 1)
            e.wait_ge(s_xst[0], 16 * W)
            e.wait_ge(s_xst[1], 16 * W)

        def table_products(e):
            def turn(w):
                e.wait_ge(s_x[w % 2], 16 * (w // 2 + 1))
                if w >= 1:
                    e.wait_ge(s_xtc, w)
                for k in range(KC):
                    ins = e.transpose(pb[:, 4, k * P:(k + 1) * P], x_in[:, x_slot(w), k * P:(k + 1) * P], ident[:])
                ins.then_inc(s_xtr, 1)

            turn(0)
            e.wait_ge(s_w0, 16 * KC)
            for w in range(W):
                if w + 1 < W:
                    turn(w + 1)
                e.wait_ge(s_xtc, w + 1)
                for half in range(2):
                    for q in range(2):
                        n = 4 * w + 2 * half + q
                        if n >= 4:
                            e.wait_ge(s_xe, n - 3)
                        for k in range(KC):
                            ins = e.matmul(pb[:, n % 4, :], x_t[:, w % 2, k, :],
                                           w0[:, k, half * 4 + q * 2:half * 4 + q * 2 + 2, :],
                                           start=(k == 0), stop=(k == KC - 1))
                        ins.then_inc(s_xm, 1)
                if w % 12 == 11:
                    rank_products(e, w // 12)

        def table_copies(e):
            def turned_x(w):
                e.wait_ge(s_xtr, w + 1)
                if w >= 2:
                    e.wait_ge(s_xm, 4 * (w - 1))
                e.activation(x_t[:, w % 2, :, :], pb[:, 4, 0:D].rearrange("p (k n) -> p k n", k=KC), ACT.Copy)\
                    .then_inc(s_xtc, 1)

            turned_x(0)
            for w in range(W):
                if w + 1 < W:
                    turned_x(w + 1)
                for n in range(4 * w, 4 * w + 4):
                    half = n // 2
                    e.wait_ge(s_xm, n + 1)
                    if n % 2 == 0 and half >= 2:
                        e.wait_ge(s_xst[half % 2], 16 * (half // 2))
                    e.activation(xt_out[:, half % 2, (n % 2) * 512:(n % 2 + 1) * 512], pb[:, n % 4, :], ACT.Copy)\
                        .then_inc(s_xe, 1)

        def rank_products(e, b):
            e.wait_ge(s_tot, b + 1)
            if b:
                e.wait_ge(s_win, b)
            e.matmul(pb[:, 5, 0:W], tri[:], tot, start=True, stop=True).then_inc(s_pre, 1)
            e.matmul(pb[:, 6, 0:W], ones[:, 0:P], tot, start=True, stop=True).then_inc(s_pre, 1)
            e.wait_ge(s_end, b + 1)
            e.transpose(pb[:, 7, 0:P], end_t, ident[:]).then_inc(s_endt, 1)
            e.wait_ge(s_cmp, b + 1)
            e.matmul(pb[0:1, 6, 0:BI], ones[:, 0:1], cmp_i, start=True, stop=True).then_inc(s_endt, 1)

        def ranks(e):
            c = Chain(e, s_rank)
            e.memset(acc[:], 0.0).then_inc(s_accz, 1)
            e.memset(x_in[:, 2, :], 0.0).then_inc(s_xz, 1)
            c(e.memset(end_t, 1e6))
            for b in range(BLOCKS):
                win = win_c[:, b * BT:(b + 1) * BT]
                pos = pos_c[:, b * BT:(b + 1) * BT]
                for w in range(W):
                    c(e.tensor_scalar(mask, win, float(w), None, ALU.is_equal))
                    c(e.tensor_tensor_scan(cum, ones[:, 0:BT], mask, 0.0, ALU.mult, ALU.add))
                    c(e.copy_predicated(pos, mask.bitcast(I32), cum))
                    c(e.tensor_copy(tot[:, w:w + 1], cum[:, BT - 1:BT]))
                e.sem_inc(s_tot, 1)
                e.wait_ge(s_pre, 2 * b + 2)
                c(e.tensor_scalar(tot_i, pb[:, 6, 0:W], float(P - 1), None, ALU.add))
                c(e.tensor_scalar(tot_i, tot_i, LOG_P, None, ALU.arith_shift_right))
                c(e.tensor_copy(offs, tot_i))
                c(e.tensor_tensor_scan(end_t[:, 0:W], ones[:, 0:W], offs, 0.0, ALU.mult, ALU.add))
                e.sem_inc(s_end, 1)
                c(e.tensor_tensor(offs, end_t[:, 0:W], offs, ALU.subtract))
                c(e.tensor_scalar(offs, offs, float(P), -1.0, ALU.mult, ALU.add))
                c(e.tensor_tensor(offs, offs, pb[:, 5, 0:W], ALU.add))
                for w in range(W):
                    c(e.tensor_scalar(tmp, win, float(w), offs[:, w:w + 1], ALU.is_equal, ALU.mult))
                    c(e.tensor_tensor(pos, pos, tmp, ALU.add))
                ints = int_c[:, 0:BT]
                c(e.tensor_copy(ints, pos))
                c(e.tensor_scalar(ints, ints, P - 1, None, ALU.bitwise_and))
                c(e.tensor_copy(q_c[:, b * BT:(b + 1) * BT], ints))
                c(e.tensor_copy(ints, pos))
                c(e.tensor_scalar(ints, ints, LOG_P, None, ALU.arith_shift_right))
                c(e.tensor_copy(c_c[:, b * BT:(b + 1) * BT], ints))
                e.wait_ge(s_endt, 2 * b + 1)
                c(e.tensor_copy(end_c, pb[:, 7, 0:1]))
                c(e.tensor_scalar(cmp_i, iota_q[:, 0:BI], end_c, None, ALU.is_ge))
                e.sem_inc(s_cmp, 1)
                e.wait_ge(s_endt, 2 * b + 2)
                c(e.tensor_scalar(table[0:1, b * BI:(b + 1) * BI], pb[0:1, 6, 0:BI], float(W - 1), float(AW),
                                  ALU.min, ALU.mult))
                e.sem_inc(s_win, 1)

        phase(sync=table_io, tensor=table_products, scalar=table_copies, vector=ranks)

        s_l0g = [sem(f"s_l0g{k}") for k in range(ITEM_U)]
        built, moved = Progress(sem("s_built"), 2), Progress(sem("s_moved"), 2)
        staged = Progress(sem("s_staged"), ITEM_U)
        hot, summed = Progress(sem("s_hot"), 3), Progress(sem("s_summed"), ITEM_U)
        added = Progress(sem("s_added"), 3)
        s_open, s_close, s_sorted, s_go0 = sem("s_open"), sem("s_close"), sem("s_sorted"), sem("s_go0")

        def l0_start(e, mine):
            for m in mine:
                m.start(e)

        def stage_of(st):
            perm = st if st < BLOCKS else None
            items = st - 1 if st > 0 else None
            return perm, items

        def l0_scalar(st):
            def go(e):
                _, ib = stage_of(st)
                if st == 0:
                    l0_start(e, [staged])
                if ib is None:
                    return
                with e.Fori(0, ROUNDS) as j:
                    for k in range(ITEM_U):
                        i = j * ITEM_U + (ib * BI + k)
                        summed.free(e, i, ITEM_U)
                        e.activation(stage_i[:, k:k + 1], idx_s[:, ib % 2, bass.ds(j * ITEM_U + k, 1)], ACT.Copy)\
                            .then_inc(staged.sem, 1)
            return go

        def l0_gather(st):
            def go(e):
                _, ib = stage_of(st)
                if ib is None:
                    return
                with e.Fori(0, ROUNDS) as j:
                    for k in range(ITEM_U):
                        staged.done(e, j * ITEM_U + (ib * BI + k))
                        e.sem_inc(s_go0, 1)
                        e.indirect_dma_start(g_rows[:, k, :], None, xt_table,
                                             bass.IndirectOffsetOnAxis(ap=stage_i[:, k:k + 1], axis=0))\
                            .then_inc(s_l0g[k], 16)
            return go

        def l0_tensor(st):
            def go(e):
                pb_, ib = stage_of(st)
                if st == 0:
                    l0_start(e, [moved, summed])
                if pb_ is not None:
                    for v in range(3):
                        ins = e.matmul(pb[:, v, 0:BI], zero_b[:, 0:P], zero_b[:, 0:BI], start=True, stop=False,
                                       skip_group_check=True)
                    ins.then_inc(s_open, 1)
                with e.Fori(0, ROUNDS) as j:
                    for k in range(ITEM_U):
                        if ib is not None:
                            i = j * ITEM_U + (ib * BI + k)
                            hot.done(e, i)
                            e.wait_ge(s_l0g[k], j * 16 + (ib * ROUNDS + 1) * 16)
                            added.free(e, i, 3)
                            e.matmul(pb[:, 3 + k % 3, 0:D], hots[:, k % 3, :], g_rows[:, k, :],
                                     start=True, stop=True).then_inc(summed.sem, 1)
                        if pb_ is not None and k < PERM_U:
                            built.done(e, j * PERM_U + (pb_ * BT + k))
                            for v in range(3):
                                ins = e.matmul(pb[:, v, 0:BI], hot_q[:, k % 2, v, :], hot_c[:, k % 2, :],
                                               start=False, stop=False, skip_group_check=True)
                            ins.then_inc(moved.sem, 1)
                if pb_ is not None:
                    for v in range(3):
                        ins = e.matmul(pb[:, v, 0:BI], zero_b[:, 0:P], zero_b[:, 0:BI], start=False, stop=True,
                                       skip_group_check=True)
                    ins.then_inc(s_close, 1)
            return go

        def l0_vector(st):
            def go(e):
                pb_, ib = stage_of(st)
                if st == 0:
                    l0_start(e, [built, hot, added])

                def add(j, k):
                    i = j * ITEM_U + (ib * BI + k)
                    at = e.value_load(table[0:1, bass.ds(j * ITEM_U + (ib * BI + k), 1)], min_val=0,
                                      max_val=(W - 1) * AW)
                    summed.done(e, i)
                    added.free(e, i, 1)
                    to = acc[:, bass.ds(at, D)]
                    e.tensor_tensor(to, to, pb[:, 3 + k % 3, 0:D], ALU.add).then_inc(added.sem, 1)

                with e.Fori(0, ROUNDS) as j:
                    for k in range(ITEM_U):
                        if ib is not None:
                            i = j * ITEM_U + (ib * BI + k)
                            summed.free(e, i, 3)
                            e.tensor_scalar(hots[:, k % 3, :], iota_q[:, 1:P + 1],
                                            loc_s[:, ib % 2, bass.ds(j * ITEM_U + k, 1)], None, ALU.is_equal)\
                                .then_inc(hot.sem, 1)
                        if pb_ is not None and k < PERM_U:
                            col = j * PERM_U + (pb_ * BT + k)
                            moved.free(e, j * PERM_U + (pb_ * BT + k), 2)
                            for v, byte in enumerate((lo_c, hi_c, loc_c)):
                                e.tensor_scalar(hot_q[:, k % 2, v, :], iota_q[:, 0:P], q_c[:, bass.ds(col, 1)],
                                                byte[:, bass.ds(col, 1)], ALU.is_equal, ALU.mult)
                            e.tensor_scalar(hot_c[:, k % 2, :], iota_q[:, 0:BI], c_c[:, bass.ds(col, 1)], None,
                                            ALU.is_equal).then_inc(built.sem, 1)
                        if ib is not None and k >= 2:
                            add(j, k - 2)
                    if ib is not None:
                        add(j, ITEM_U - 2)
                        add(j, ITEM_U - 1)
                if pb_ is not None:
                    e.wait_ge(s_close, pb_ + 1)
                    c = Chain(e, s_sorted)
                    c.n = 3 * pb_
                    c(e.tensor_copy(lo_s, pb[:, 0, 0:BI]))
                    c(e.scalar_tensor_tensor(idx_s[:, pb_ % 2, :], pb[:, 1, 0:BI], 256.0, lo_s, ALU.mult, ALU.add))
                    c(e.tensor_copy(loc_s[:, pb_ % 2, :], pb[:, 2, 0:BI]))
            return go

        for st in range(BLOCKS + 1):
            phase(scalar=l0_scalar(st), gpsimd=l0_gather(st), tensor=l0_tensor(st), vector=l0_vector(st))

        s_xall, s_wq, s_n1, s_stat, s_sq = sem("s_xall"), sem("s_wq"), sem("s_n1"), sem("s_stat"), sem("s_sq")
        s_norm, s_nt, s_ntc, s_qkv, s_qc, s_kvc = (sem(n) for n in (
            "s_norm", "s_nt", "s_ntc", "s_qkv", "s_qc", "s_kvc"))
        s_kvst = [sem("s_kvst0"), sem("s_kvst1")]
        s_x1st, s_xpad = sem("s_x1st"), sem("s_xpad")
        x1 = node_b[:].rearrange("p (w d) -> p w d", w=W)

        def mid_io(e):
            e.wait_ge(s_xpad, 1)
            full_w = N // P
            e.dma_start(x1[:, 0:full_w, :], a["x"][0:full_w * P, :].rearrange("(w p) d -> p w d", p=P))\
                .then_inc(s_xall, 16)
            e.dma_start(x1[0:N - full_w * P, full_w, :], a["x"][full_w * P:N, :]).then_inc(s_xall, 16)
            e.dma_start(bias0, a["L0_gnn_bias"].rearrange("(a d) -> a d", a=1).to_broadcast([P, D]))\
                .then_inc(s_xall, 16)
            for n, name in enumerate(("L1_gnn_Wq", "L1_gnn_Wk", "L1_gnn_Wv")):
                e.dma_start(wqkv[:, :, n * D:(n + 1) * D], a[name].rearrange("(k p) n -> p k n", p=P))\
                    .then_inc(s_wq, 16)
            for w in range(W):
                e.wait_ge(s_norm, w + 1)
                e.dma_start(x1_store[w * P:(w + 1) * P, :], x1[:, w, :]).then_inc(s_x1st, 16)
                e.wait_ge(s_kvc, w + 1)
                e.dma_start(k_table[w * P:(w + 1) * P, :], kv_out[:, w % 2, 0:D]).then_inc(s_kvst[w % 2], 16)
                e.dma_start(v_table[w * P:(w + 1) * P, :], kv_out[:, w % 2, D:2 * D]).then_inc(s_kvst[w % 2], 16)
            e.wait_ge(s_x1st, 16 * W)
            e.wait_ge(s_kvst[0], 32 * (W - W // 2))
            e.wait_ge(s_kvst[1], 32 * (W // 2))

        def mid_vector(e):
            c = Chain(e, s_n1)
            e.memset(x1[:, W - 1, :], 0.0).then_inc(s_xpad, 1)
            e.wait_ge(s_xall, 48)
            for w in range(W):
                z = acc_w[:, w, 0:D]
                c(e.tensor_tensor(z, z, bias0, ALU.add))
                c(e.scalar_tensor_tensor(x1[:, w, :], z, 0.0, x1[:, w, :], ALU.max, ALU.add))
                c(e.bn_stats(stats[:, 0:6], x1[:, w, :]))
                c(e.bn_aggr(mv[:, 2 * w:2 * w + 2], stats[:, 0:6]))
            c(e.tensor_scalar(rstd[:], mv[:].rearrange("p (w t) -> p t w", t=2)[:, 1, :], EPS, None, ALU.add))
            e.sem_inc(s_stat, 1)
            e.wait_ge(s_sq, 1)
            c(e.reciprocal(rstd[:], rstd[:]))
            c(e.scalar_tensor_tensor(nmr[:], mv[:].rearrange("p (w t) -> p t w", t=2)[:, 0, :], -1.0, rstd[:],
                                     ALU.mult, ALU.mult))
            for w in range(W + 1):
                if w < W:
                    e.tensor_scalar(x1[:, w, :], x1[:, w, :], rstd[:, w:w + 1], nmr[:, w:w + 1], ALU.mult, ALU.add)\
                        .then_inc(s_norm, 1)
                if w >= 1:
                    e.wait_ge(s_qkv, 2 * w)
                    e.tensor_copy(acc_w[:, w - 1, 0:D], pb[:, 4 + (w - 1) % 2, 0:D]).then_inc(s_qc, 1)

        def mid_tensor(e):
            e.wait_ge(s_wq, 48)
            for w in range(W):
                e.wait_ge(s_norm, w + 1)
                if w >= 1:
                    e.wait_ge(s_ntc, w)
                for k in range(KC):
                    ins = e.transpose(pb[:, 0, k * P:(k + 1) * P], x1[:, w, k * P:(k + 1) * P], ident[:])
                ins.then_inc(s_nt, 1)
                e.wait_ge(s_ntc, w + 1)
                if w >= 2:
                    e.wait_ge(s_kvc, w - 1)
                    e.wait_ge(s_qc, w - 1)
                for k in range(KC):
                    ins = e.matmul(pb[:, 2 + w % 2, :], x1t[:, w % 2, k, :], wqkv[:, k, D:3 * D],
                                   start=(k == 0), stop=(k == KC - 1))
                ins.then_inc(s_qkv, 1)
                for k in range(KC):
                    ins = e.matmul(pb[:, 4 + w % 2, 0:D], x1t[:, w % 2, k, :], wqkv[:, k, 0:D],
                                   start=(k == 0), stop=(k == KC - 1))
                ins.then_inc(s_qkv, 1)

        def mid_scalar(e):
            e.wait_ge(s_stat, 1)
            e.activation(rstd[:], rstd[:], ACT.Sqrt).then_inc(s_sq, 1)
            for w in range(W):
                e.wait_ge(s_nt, w + 1)
                if w >= 2:
                    e.wait_ge(s_qkv, 2 * (w - 1))
                e.activation(x1t[:, w % 2, :, :], pb[:, 0, 0:D].rearrange("p (k n) -> p k n", k=KC), ACT.Copy)\
                    .then_inc(s_ntc, 1)
                e.wait_ge(s_qkv, 2 * w + 1)
                if w >= 2:
                    e.wait_ge(s_kvst[w % 2], 32 * (w // 2))
                e.activation(kv_out[:, w % 2, :], pb[:, 2 + w % 2, :], ACT.Copy).then_inc(s_kvc, 1)

        phase(sync=mid_io, vector=mid_vector, tensor=mid_tensor, scalar=mid_scalar)

        s_upad, s_uin, s_ucol, s_urow, s_tcol, s_trow = (sem(n) for n in (
            "s_upad", "s_uin", "s_ucol", "s_urow", "s_tcol", "s_trow"))
        s_items, s_recin, s_rect, s_recc, s_st, s_wgt, s_pre1, s_gp1 = (sem(n) for n in (
            "s_items", "s_recin", "s_rect", "s_recc", "s_st", "s_wgt", "s_pre1", "s_gp1"))

        def walk_io(e):
            e.wait_ge(s_upad, 1)
            last = edge_table[:, (P - 1) * REC + DST:(P - 1) * REC + DST + 1]
            g = T // P
            e.dma_start(u_col[:, 0:g].unsqueeze(2), last[0:g * P, :].rearrange("(g p) n -> p g n", p=P),
                        allow_slow_non_contiguous=True).then_inc(s_uin, 16)
            e.dma_start(u_col[0:T - g * P, g:g + 1], last[g * P:T, :], allow_slow_non_contiguous=True)\
                .then_inc(s_uin, 16)

        def walk_gather(e):
            c = Chain(e, s_gp1)
            c(e.iota(item_row, [[1, WALK]], base=0, channel_multiplier=0, allow_small_or_imprecise_dtypes=True))
            c(e.iota(item_col, [[P, RAW_G]], base=0, channel_multiplier=1, allow_small_or_imprecise_dtypes=True))
            e.sem_inc(s_items, 1)
            e.wait_ge(s_tcol, 1)
            for g in range(RAW_G):
                e.indirect_dma_start(recs[:, g, :, :].rearrange("p e f -> p (e f)"), None, edge_table,
                                     bass.IndirectOffsetOnAxis(ap=t_int[:, g:g + 1], axis=0))\
                    .then_inc(s_recin, 16)

        def walk_vector(e):
            c = Chain(e, s_st)
            e.memset(u_col, 1e6).then_inc(s_upad, 1)
            e.wait_ge(s_items, 1)
            e.wait_ge(s_uin, 32)
            c(e.tensor_copy(u_int, u_col))
            c(e.tensor_scalar(u_int, u_int, LOG_P, None, ALU.arith_shift_right))
            c(e.tensor_copy(u_col, u_int))
            c(e.tensor_tensor(u_col, u_col, item_col, ALU.add))
            e.sem_inc(s_ucol, 1)
            e.wait_ge(s_urow, 1)
            for b in range(0, RAW_G, 4):
                n = min(RAW_G - b, 4) * P
                c(e.tensor_copy(u_row[:, b * P:b * P + n], pb[:, b // 4, 0:n]))
            for g in range(RAW_G):
                c(e.tensor_scalar(w_row, u_row, item_col[:, g:g + 1], None, ALU.is_lt, ALU.add,
                                  accum_out=t_col[:, g:g + 1]))
            c(e.tensor_scalar(t_col, t_col, float(T - 1), None, ALU.min))
            c(e.tensor_copy(t_int, t_col))
            e.sem_inc(s_tcol, 1)
            e.wait_ge(s_trow, 1)
            for b in range(0, WALK, 512):
                n = min(WALK - b, 512)
                c(e.tensor_tensor(w_row[:, b:b + n], item_row[:, b:b + n], pb[:, b // 512, 0:n], ALU.subtract))
            c(e.tensor_scalar(table[0:1, 0:WALK], w_row[0:1, 0:WALK], float(AW), None, ALU.mult))
            e.wait_ge(s_recc, 3 * RAW_G)
            c(e.scalar_tensor_tensor(dl_i[:], w_row[:, 0:WALK], -float(P), dst_i[:], ALU.mult, ALU.add))
            c(e.tensor_copy(dl_b[:], dl_i[:]))
            for bound, op in ((0.0, ALU.is_lt), (float(P), ALU.is_ge)):
                c(e.tensor_scalar(u_row[:, 0:WALK], dl_i[:], bound, LOW, op, ALU.mult))
                c(e.tensor_tensor(wgt_i, wgt_i, u_row[:, 0:WALK], ALU.add))
            e.sem_inc(s_wgt, 1)

        def walk_tensor(e):
            def spread(col):
                for g in range(RAW_G):
                    ins = e.matmul(pb[:, g // 4, (g % 4) * P:(g % 4 + 1) * P], col[:, g:g + 1].to_broadcast([P, P]),
                                   ident[:], start=True, stop=True)
                return ins

            e.wait_ge(s_ucol, 1)
            spread(u_col).then_inc(s_urow, 1)
            e.wait_ge(s_tcol, 1)
            spread(t_col).then_inc(s_trow, 1)
            e.wait_ge(s_recin, 16 * RAW_G)
            for g in range(RAW_G):
                if g >= 4:
                    e.wait_ge(s_recc, 3 * (g - 3))
                for f in (DST, SRC, WGT):
                    ins = e.transpose(pb[:, 4 + g % 4, f * P:(f + 1) * P], recs[:, g, :, f], ident[:])
                ins.then_inc(s_rect, 1)

        def walk_scalar(e):
            for g in range(RAW_G):
                e.wait_ge(s_rect, g + 1)
                n = min(WALK - g * P, P)
                for f, to in ((DST, dst_i[:]), (SRC, src_i[:]), (WGT, wgt_i)):
                    e.activation(to[:, g * P:g * P + n], pb[:, 4 + g % 4, f * P:f * P + n], ACT.Copy)\
                        .then_inc(s_recc, 1)
            e.wait_ge(s_wgt, 1)
            for ch in range(CH):
                e.activation(edge_s[:].rearrange("p (j c h) -> p c j h", c=CH, h=HEADS)[:, ch, :, :],
                             wgt_i[:, ch * CJ:(ch + 1) * CJ].unsqueeze(2).to_broadcast([P, CJ, HEADS]), ACT.Copy)\
                    .then_inc(s_pre1, 1)

        phase(sync=walk_io, gpsimd=walk_gather, vector=walk_vector, tensor=walk_tensor, scalar=walk_scalar)

        score_c = edge_s[:].rearrange("p (j c h) -> p c j h", c=CH, h=HEADS)

        def score_parts(q):
            got, i = [], q * QUAD
            while i < (q + 1) * QUAD:
                ch, j = divmod(i, CJ)
                n = min((q + 1) * QUAD - i, CJ - j)
                got.append((i - q * QUAD, n, score_c[:, ch, j:j + n, :]))
                i += n
            return got

        class Windows:

            def __init__(self, e, name):
                self.e, self.regs = e, [e.alloc_register(f"{name}{k}") for k in range(2 * QUAD)]

            def load(self, q):
                r = self.regs[q % 2 * QUAD:(q % 2 + 1) * QUAD]
                self.e.reg_load(r, table[0:1, q * QUAD:(q + 1) * QUAD])
                return [self.e.snap(x, min_val=0, max_val=(W - 1) * AW) for x in r]

        s_kg = [sem(f"s_kg{k}") for k in range(ROW_RING)]
        a_spread, a_hot, a_q, a_mul, a_red, a_add = (Count(sem(n)) for n in (
            "s_a_spread", "s_a_hot", "s_a_q", "s_a_mul", "s_a_red", "s_a_add"))

        def gather_rows(e, from_table, landed, used):
            for q in range(QUADS):
                used.free(e, q, ROW_RING)
                for k in range(QUAD):
                    i = q * QUAD + k
                    e.indirect_dma_start(rows[:, q % ROW_RING, k, :], None, from_table,
                                         bass.IndirectOffsetOnAxis(ap=src_i[:, i:i + 1], axis=0))\
                        .then_inc(landed[q % ROW_RING], 16)

        def rows_in(e, q, landed):
            e.wait_ge(landed[q % ROW_RING], 16 * QUAD * (q // ROW_RING + 1))

        def a_gather(e):
            gather_rows(e, k_table, s_kg, a_mul)

        def a_tensor(e):
            win = Windows(e, "a_win")

            def spread(q):
                a_hot.free(e, q, 2)
                for k in range(QUAD):
                    i = q * QUAD + k
                    ins = e.matmul(pb[:, q % 2, k * P:(k + 1) * P], dl_b[:, i:i + 1].to_broadcast([P, P]),
                                   ident_b[:], start=True, stop=True)
                ins.then_inc(a_spread.sem, 1)

            def take_q(q):
                at = win.load(q)
                a_hot.done(e, q)
                a_mul.free(e, q, 2)
                for k in range(QUAD):
                    ins = e.matmul(pb[:, 2 + q % 2 * 2 + k // 2, k % 2 * D:(k % 2 + 1) * D],
                                   w_hot[:, q % 2, k * P:(k + 1) * P], acc[:, bass.ds(at[k], D)],
                                   start=True, stop=True)
                ins.then_inc(a_q.sem, 1)

            for q in range(QUADS + 1):
                if q < QUADS:
                    spread(q)
                if q:
                    take_q(q - 1)

        def a_vector(e):
            def hot_of(q):
                a_spread.done(e, q)
                a_q.free(e, q, 2)
                e.tensor_scalar(w_hot[:, q % 2, :], pb[:, q % 2, :], iota_p[:], None, ALU.is_equal)\
                    .then_inc(a_hot.sem, 1)

            def multiply(q):
                a_q.done(e, q)
                rows_in(e, q, s_kg)
                a_red.free(e, q, 2)
                e.tensor_tensor(prods[:, q % 2, :].rearrange("p (b n) -> p b n", b=2),
                                rows[:, q % ROW_RING, :, :].rearrange("p (b k) n -> p b (k n)", b=2),
                                pb[:, 2 + q % 2 * 2:4 + q % 2 * 2, :], ALU.mult).then_inc(a_mul.sem, 1)

            def reduce(q):
                a_mul.done(e, q)
                a_add.free(e, q, 2)
                e.tensor_reduce(parts[:, q % 2, :], prods[:, q % 2, :].rearrange("p (h d) -> p h d", d=HD),
                                AX.X, ALU.add).then_inc(a_red.sem, 1)

            def add(q):
                a_red.done(e, q)
                part = parts[:, q % 2, :].rearrange("p (k h) -> p k h", h=HEADS)
                for first, n, to in score_parts(q):
                    ins = e.scalar_tensor_tensor(to, part[:, first:first + n, :], SCALE, to, ALU.mult, ALU.add)
                ins.then_inc(a_add.sem, 1)

            for q in range(QUADS + 2):
                if q < QUADS:
                    hot_of(q)
                if q >= 2:
                    reduce(q - 2)
                if 1 <= q <= QUADS:
                    multiply(q - 1)
                if q >= 2:
                    add(q - 2)

        phase(gpsimd=a_gather, tensor=a_tensor, vector=a_vector)

        s_mt, s_mc, s_mp, s_ms = sem("s_mt"), sem("s_mc"), sem("s_mp"), sem("s_ms")
        s_ends, s_edge, s_car = sem("s_ends"), sem("s_edge"), sem("s_car")
        s_mb, s_sub, s_exp, s_dx = sem("s_mb"), sem("s_sub"), sem("s_exp"), sem("s_dx")
        PJ = 2
        pieces = [(j, min(PJ, CJ - j)) for j in range(0, CJ, PJ)]
        PIECES = len(pieces)

        def max_tensor(e):
            for n in range(PIECES):
                if n >= 2:
                    e.wait_ge(s_mc, n - 1)
                    e.wait_ge(s_mp, n - 1)
                e.wait_ge(s_dx, n + 1)
                j0, nj = pieces[n]
                for q in range(nj):
                    e.transpose(pb[:, n % 2, q * P:(q + 1) * P], score_v[:, j0 + q, :], ident[:])
                    ins = e.transpose(pb[:, 2 + n % 2, q * P:(q + 1) * P], dst_x[:, n % 2, q * P:(q + 1) * P],
                                      ident[:])
                ins.then_inc(s_mt, 1)
            for r in range(3):
                e.wait_ge(s_ends, r + 1)
                e.transpose(pb[0:1, 4, r * P:(r + 1) * P], small[:, r:r + 1], ident[:]).then_inc(s_edge, 1)
            e.wait_ge(s_ends, 4)
            e.matmul(pb[:, 5, 0:1], row[8], ones[0:1, 0:1], start=True, stop=True).then_inc(s_edge, 1)
            e.wait_ge(s_ends, 5)
            e.transpose(pb[0:1, 6, 0:P], small[:, 3:4], ident[:]).then_inc(s_edge, 1)
            e.wait_ge(s_ends, 6)
            e.matmul(pb[:, 7, 0:1], row[8], ones[0:1, 0:1], start=True, stop=True).then_inc(s_edge, 1)
            e.wait_ge(s_car, 1)
            for n in range(PIECES):
                if n >= 2:
                    e.wait_ge(s_sub, n - 1)
                j0, nj = pieces[n]
                for q in range(nj):
                    ins = e.transpose(pb[:, n % 2, q * P:(q + 1) * P], scan_s[:, (j0 + q) * P:(j0 + q + 1) * P],
                                      ident[:])
                ins.then_inc(s_mb, 1)

        def max_scalar(e):
            def expand(n):
                if n >= 2:
                    e.wait_ge(s_mt, n - 1)
                j0, nj = pieces[n]
                for q in range(nj):
                    ins = e.activation(dst_x[:, n % 2, q * P:(q + 1) * P].rearrange("p (c h) -> p c h", h=HEADS),
                                       dst_i[:].rearrange("p (c j) -> p j c", c=CH)[:, j0 + q, :]
                                       .unsqueeze(2).to_broadcast([P, CH, HEADS]), ACT.Copy)
                ins.then_inc(s_dx, 1)

            expand(0)
            for n, (j0, nj) in enumerate(pieces):
                if n + 1 < PIECES:
                    expand(n + 1)
                e.wait_ge(s_mt, n + 1)
                e.activation(scan_s[:, j0 * P:(j0 + nj) * P], pb[:, n % 2, 0:nj * P], ACT.Copy).then_inc(s_mc, 1)
            for c in range(CH):
                e.wait_ge(s_sub, PIECES)
                part_ = edge_s[:, c * CJ * HEADS:(c + 1) * CJ * HEADS]
                e.activation(part_, part_, ACT.Exp).then_inc(s_exp, 1)

        def max_vector(e):
            c = Chain(e, s_ms)
            PL = PJ * P
            for n, (j0, nj) in enumerate(pieces):
                L = nj * P
                e.wait_ge(s_mt, n + 1)
                if n:
                    c(e.tensor_copy(dst_t[:, 0:1], dst_t[:, PL:PL + 1]))
                e.tensor_copy(dst_t[:, 1:L + 1], pb[:, 2 + n % 2, 0:L]).then_inc(s_mp, 1)
                e.wait_ge(s_mp, n + 1)
                if n == 0:
                    c(e.tensor_copy(dst_t[:, 0:1], dst_t[:, 1:2]))
                    c(e.tensor_copy(small[:, 0:1], dst_t[:, 1:2]))
                    e.sem_inc(s_ends, 1)
                c(e.tensor_tensor(same[:, 0:L], dst_t[:, 1:L + 1], dst_t[:, 0:L], ALU.is_equal))
                c(e.tensor_scalar(pen[:, j0 * P:j0 * P + L], same[:, 0:L], 1.0, -LOW, ALU.subtract, ALU.mult))
            c(e.memset(pen[:, CL:CL + 1], 0.0))
            c(e.tensor_copy(small[:, 1:2], dst_t[:, L:L + 1]))
            e.sem_inc(s_ends, 1)
            e.wait_ge(s_mc, PIECES)
            c(e.tensor_tensor_scan(scan_s, pen[:, 0:CL], scan_s, LOW, ALU.add, ALU.max))
            c(e.tensor_copy(small[:, 2:3], scan_s[:, CL - 1:CL]))
            e.sem_inc(s_ends, 1)
            e.wait_ge(s_edge, 3)
            first, last, value, cont, whole, step, base, t0 = row[0:8]
            hc = "a (c h) -> a h c"

            def by_head(to, ps):
                c(e.tensor_copy(to.rearrange("a (h c) -> a h c", h=HEADS), ps.rearrange(hc, h=HEADS)))

            by_head(first, pb[0:1, 4, 0:P])
            by_head(last, pb[0:1, 4, P:2 * P])
            by_head(value, pb[0:1, 4, 2 * P:3 * P])
            c(e.memset(cont, 0.0))
            c(e.tensor_tensor(cont[:, 1:P], first[:, 1:P], last[:, 0:P - 1], ALU.is_equal))
            c(e.memset(cont.rearrange("a (h c) -> a h c", h=HEADS)[:, :, 0:1], 0.0))
            c(e.tensor_tensor(whole, first, last, ALU.is_equal))

            def carry_in(shift):
                c(e.memset(step, LOW))
                c(e.memset(base, LOW))
                if shift == 1:
                    here, there, flag = slice(1, P), slice(0, P - 1), cont[:, 1:P]
                else:
                    here, there, flag = slice(0, P - 1), slice(1, P), cont[:, 1:P]
                c(e.tensor_tensor(t0[:, 0:P - 1], flag, whole[:, there], ALU.mult))
                c(e.tensor_scalar(step[:, here], t0[:, 0:P - 1], 1.0, -LOW, ALU.subtract, ALU.mult))
                c(e.tensor_scalar(t0[:, 0:P - 1], flag, 1.0, -LOW, ALU.subtract, ALU.mult))
                c(e.tensor_tensor(base[:, here], value[:, there], t0[:, 0:P - 1], ALU.add))
                if shift == 1:
                    c(e.tensor_tensor_scan(row[9], step, base, LOW, ALU.add, ALU.max))
                else:
                    c(e.tensor_tensor_scan(row[9][:, ::-1], step[:, ::-1], base[:, ::-1], LOW, ALU.add, ALU.max))
                c(e.tensor_copy(row[8].rearrange("a (c h) -> a c h", h=HEADS),
                                row[9].rearrange("a (h c) -> a c h", h=HEADS)))
                e.sem_inc(s_ends, 1)

            carry_in(1)
            e.wait_ge(s_edge, 4)
            c(e.tensor_copy(carry[:, 0:1], pb[:, 5, 0:1]))
            c(e.tensor_tensor_scan(scan_s, pen[:, 0:CL], scan_s, carry[:, 0:1], ALU.add, ALU.max))
            back_s, back_p = scan_s[:, ::-1], pen[:, 1:CL + 1][:, ::-1]
            c(e.tensor_tensor_scan(back_s, back_p, back_s, LOW, ALU.add, ALU.max))
            c(e.tensor_copy(small[:, 3:4], scan_s[:, 0:1]))
            e.sem_inc(s_ends, 1)
            e.wait_ge(s_edge, 5)
            by_head(value, pb[0:1, 6, 0:P])
            carry_in(-1)
            e.wait_ge(s_edge, 6)
            c(e.tensor_copy(carry[:, 1:2], pb[:, 7, 0:1]))
            c(e.tensor_tensor_scan(back_s, back_p, back_s, carry[:, 1:2], ALU.add, ALU.max))
            e.sem_inc(s_car, 1)
            for n, (j0, nj) in enumerate(pieces):
                e.wait_ge(s_mb, n + 1)
                to = edge_s[:, j0 * P:(j0 + nj) * P]
                e.tensor_tensor(to, to, pb[:, n % 2, 0:nj * P], ALU.subtract).then_inc(s_sub, 1)

        phase(scalar=max_scalar, tensor=max_tensor, vector=max_vector)

        s_vg = [sem(f"s_vg{k}") for k in range(ROW_RING)]
        b_exp, b_hot, b_msg, b_sum, b_add = (Count(sem(n)) for n in (
            "s_b_exp", "s_b_hot", "s_b_msg", "s_b_sum", "s_b_add"))
        s_bz = sem("s_bz")

        def b_gather(e):
            gather_rows(e, v_table, s_vg, b_msg)

        def b_scalar(e):
            for q in range(QUADS):
                b_sum.free(e, (q + 1) * QUAD - 1, 2 * QUAD)
                for first, n, ex in score_parts(q):
                    ins = e.activation(msgs[:, q % 2, first:first + n, D:AW], ex, ACT.Copy)
                ins.then_inc(b_exp.sem, 1)

        def b_tensor(e):
            for q in range(QUADS):
                b_hot.done(e, q)
                b_msg.done(e, q)
                for k in range(QUAD):
                    i = q * QUAD + k
                    b_add.free(e, i, 8)
                    e.matmul(pb[:, i % 8, 0:AW], w_hot[:, q % 2, k * P:(k + 1) * P], msgs[:, q % 2, k, :],
                             start=True, stop=True).then_inc(b_sum.sem, 1)

        def b_vector(e):
            win = Windows(e, "b_win")
            e.memset(acc[:], 0.0).then_inc(s_bz, 1)
            e.wait_ge(s_bz, 1)

            def hot_of(q, k):
                i = q * QUAD + k
                return e.tensor_scalar(w_hot[:, q % 2, k * P:(k + 1) * P], iota_q[:, 0:P], dl_i[:, i:i + 1], None,
                                       ALU.is_equal)

            def add(q, k, at):
                i = q * QUAD + k
                b_sum.done(e, i)
                b_add.free(e, i, 1)
                to = acc[:, bass.ds(at[k], AW)]
                e.tensor_tensor(to, to, pb[:, i % 8, 0:AW], ALU.add).then_inc(b_add.sem, 1)

            for q in range(QUADS + 1):
                if q:
                    at = win.load(q - 1)
                if q < QUADS:
                    b_sum.free(e, (q + 1) * QUAD - 1, 2 * QUAD)
                for k in range(QUAD):
                    if q < QUADS:
                        ins = hot_of(q, k)
                    if q < QUADS and k == QUAD - 1:
                        ins.then_inc(b_hot.sem, 1)
                        rows_in(e, q, s_vg)
                        b_exp.done(e, q)
                        e.tensor_tensor(msgs[:, q % 2, :, 0:D].rearrange("p k (h d) -> p k h d", h=HEADS),
                                        rows[:, q % ROW_RING, :, :].rearrange("p k (h d) -> p k h d", h=HEADS),
                                        msgs[:, q % 2, :, D:AW].unsqueeze(3).to_broadcast([P, QUAD, HEADS, HD]),
                                        ALU.mult).then_inc(b_msg.sem, 1)
                    if q:
                        add(q - 1, k, at)

        phase(scalar=b_scalar, gpsimd=b_gather, tensor=b_tensor, vector=b_vector)

        s_fw, s_x1l = sem("s_fw"), sem("s_x1l")
        s_fc, s_att, s_ft, s_ftc, s_fp, s_fz = (sem(n) for n in ("s_fc", "s_att", "s_ft", "s_ftc", "s_fp", "s_fz"))
        s_fsq, s_fst = sem("s_fsq"), sem("s_fst")
        s_h1, s_h1t, s_h1c, s_hm, s_hg, s_ym, s_yz = (sem(n) for n in (
            "s_h1", "s_h1t", "s_h1c", "s_hm", "s_hg", "s_ym", "s_yz"))
        s_res, s_store = sem("s_res"), sem("s_store")
        groups = [list(range(g, min(g + 4, W))) for g in range(0, W, 4)]

        def f_io(e):
            e.dma_start(x1, x1_store.rearrange("(w p) d -> p w d", p=P)).then_inc(s_x1l, 16)
            e.dma_start(wp, a["L1_gnn_Wp"].rearrange("(k p) n -> p k n", p=P)).then_inc(s_fw, 16)
            e.dma_start(w1, a["L1_gnn_W1"].rearrange("(k p) n -> p k n", p=P)).then_inc(s_fw, 16)
            e.dma_start(w2, a["L1_gnn_W2"].rearrange("(k p) n -> p k n", p=P)).then_inc(s_fw, 16)
            e.dma_start(b1c, a["L1_gnn_b1"].rearrange("(k p) -> p k", p=P), allow_slow_non_contiguous=True)\
                .then_inc(s_fw, 16)
            for n in vec:
                e.dma_start(vec[n], a["L1_gnn_" + n].rearrange("(a d) -> a d", a=1).to_broadcast([P, D]))\
                    .then_inc(s_fw, 16)
            for w in range(W):
                e.wait_ge(s_res, w + 1)
                e.dma_start(out[w * P:w * P + node_rows(w), :], x1[0:node_rows(w), w, :]).then_inc(s_store, 16)
            e.wait_ge(s_store, 16 * W)

        def f_vector(e):
            c = Chain(e, s_fc)
            e.wait_ge(s_fw, 16 * (4 + len(vec)))
            e.wait_ge(s_x1l, 16)

            def stat(w, z):
                c(e.bn_stats(stats[:, 0:6], z))
                c(e.bn_aggr(mv[:, 2 * w:2 * w + 2], stats[:, 0:6]))

            def roots(n):
                c(e.tensor_scalar(rstd[:], mv[:].rearrange("p (w t) -> p t w", t=2)[:, 1, :], EPS, None, ALU.add))
                e.sem_inc(s_fst, 1)
                e.wait_ge(s_fsq, n)
                c(e.reciprocal(rstd[:], rstd[:]))
                c(e.scalar_tensor_tensor(nmr[:], mv[:].rearrange("p (w t) -> p t w", t=2)[:, 0, :], -1.0, rstd[:],
                                         ALU.mult, ALU.mult))

            def norm(z, w, g, b):
                c(e.tensor_scalar(z, z, rstd[:, w:w + 1], nmr[:, w:w + 1], ALU.mult, ALU.add))
                c(e.tensor_tensor(z, z, vec[g], ALU.mult))
                c(e.tensor_tensor(z, z, vec[b], ALU.add))

            for w in range(W + 1):
                if w < W:
                    if w >= 2:
                        e.wait_ge(s_ft, w - 1)
                    c(e.tensor_scalar(recip[:, w % 2, :], acc_w[:, w, D:AW], 1e-30, None, ALU.max))
                    c(e.reciprocal(recip[:, w % 2, :], recip[:, w % 2, :]))
                    e.tensor_tensor(att[:, w % 2, :].rearrange("p (h d) -> p h d", h=HEADS),
                                    acc_w[:, w, 0:D].rearrange("p (h d) -> p h d", h=HEADS),
                                    recip[:, w % 2, :].unsqueeze(2).to_broadcast([P, HEADS, HD]), ALU.mult)\
                        .then_inc(s_att, 1)
                if w >= 1:
                    v = w - 1
                    z = acc_w[:, v, 0:D]
                    e.wait_ge(s_fp, v + 1)
                    e.wait_ge(s_att, v + 1)
                    e.tensor_tensor(z, pb[:, 2 + v % 2, 0:D], x1[:, v, :], ALU.add).then_inc(s_fz, 1)
                    e.wait_ge(s_fz, v + 1)
                    c(e.tensor_tensor(z, z, vec["bp"], ALU.add))
                    stat(v, z)
            roots(1)
            n = 0
            for g, ws in enumerate(groups + [None]):
                if ws:
                    for w in ws:
                        norm(acc_w[:, w, 0:D], w, "ln1_g", "ln1_b")
                    e.sem_inc(s_h1, 1)
                if g:
                    for v in groups[g - 1]:
                        z = acc_w[:, v, 0:D]
                        e.wait_ge(s_ym, n + 1)
                        e.tensor_tensor(z, z, pb[:, 6 + n % 2, 0:D], ALU.add).then_inc(s_yz, 1)
                        n += 1
                        e.wait_ge(s_yz, n)
                        c(e.tensor_tensor(z, z, vec["b2"], ALU.add))
            for w in range(W):
                stat(w, acc_w[:, w, 0:D])
            roots(2)
            for w in range(W):
                z = acc_w[:, w, 0:D]
                norm(z, w, "ln2_g", "ln2_b")
                c(e.tensor_tensor(z, z, x1[:, w, :], ALU.add))
                stat(w, z)
            roots(3)
            for w in range(W):
                e.tensor_scalar(x1[:, w, :], acc_w[:, w, 0:D], rstd[:, w:w + 1], nmr[:, w:w + 1], ALU.mult, ALU.add)\
                    .then_inc(s_res, 1)

        def f_tensor(e):
            e.wait_ge(s_fw, 16 * (4 + len(vec)))
            for w in range(W):
                e.wait_ge(s_att, w + 1)
                if w >= 1:
                    e.wait_ge(s_ftc, w)
                for k in range(KC):
                    ins = e.transpose(pb[:, 0, k * P:(k + 1) * P], att[:, w % 2, k * P:(k + 1) * P], ident[:])
                ins.then_inc(s_ft, 1)
                e.wait_ge(s_ftc, w + 1)
                if w >= 2:
                    e.wait_ge(s_fz, w - 1)
                for k in range(KC):
                    ins = e.matmul(pb[:, 2 + w % 2, 0:D], att_t[:, w % 2, k, :], wp[:, k, :],
                                   start=(k == 0), stop=(k == KC - 1))
                ins.then_inc(s_fp, 1)
            n = m = t = 0
            for g, ws in enumerate(groups):
                cols = len(ws) * P
                e.wait_ge(s_h1, g + 1)
                for i, w in enumerate(ws):
                    if t >= 2:
                        e.wait_ge(s_h1c, t - 1)
                    for k in range(KC):
                        ins = e.transpose(pb[:, t % 2, k * P:(k + 1) * P], acc_w[:, w, k * P:(k + 1) * P], ident[:])
                    ins.then_inc(s_h1t, 1)
                    t += 1
                e.wait_ge(s_h1c, t)
                for f in range(FC):
                    if m >= 2:
                        e.wait_ge(s_hg, m - 1)
                    for k in range(KC):
                        ins = e.matmul(pb[:, 4 + m % 2, 0:cols], w1[:, k, f * P:(f + 1) * P], h1_t[:, k, 0:cols],
                                       start=(k == 0), stop=(k == KC - 1))
                    ins.then_inc(s_hm, 1)
                    m += 1
                e.wait_ge(s_hg, m)
                for i, w in enumerate(ws):
                    if n >= 2:
                        e.wait_ge(s_yz, n - 1)
                    for f in range(FC):
                        ins = e.matmul(pb[:, 6 + n % 2, 0:D], hid[:, f, i * P:(i + 1) * P], w2[:, f, :],
                                       start=(f == 0), stop=(f == FC - 1))
                    ins.then_inc(s_ym, 1)
                    n += 1

        def f_scalar(e):
            e.wait_ge(s_fw, 16 * (4 + len(vec)))
            for w in range(W):
                e.wait_ge(s_ft, w + 1)
                if w >= 2:
                    e.wait_ge(s_fp, w - 1)
                e.activation(att_t[:, w % 2, :, :], pb[:, 0, 0:D].rearrange("p (k n) -> p k n", k=KC), ACT.Copy)\
                    .then_inc(s_ftc, 1)
            e.wait_ge(s_fst, 1)
            e.activation(rstd[:], rstd[:], ACT.Sqrt).then_inc(s_fsq, 1)
            m = t = n = 0
            for g, ws in enumerate(groups):
                cols = len(ws) * P
                for i, w in enumerate(ws):
                    e.wait_ge(s_h1t, t + 1)
                    e.wait_ge(s_hm, g * FC) if g else None
                    e.activation(h1_t[:, :, i * P:(i + 1) * P],
                                 pb[:, t % 2, 0:D].rearrange("p (k n) -> p k n", k=KC), ACT.Copy).then_inc(s_h1c, 1)
                    t += 1
                for f in range(FC):
                    e.wait_ge(s_hm, m + 1)
                    if g:
                        e.wait_ge(s_ym, n)
                    e.activation(hid[:, f, 0:cols], pb[:, 4 + m % 2, 0:cols], ACT.Gelu, bias=b1c[:, f:f + 1])\
                        .then_inc(s_hg, 1)
                    m += 1
                n += len(ws)
            e.wait_ge(s_fst, 2)
            e.activation(rstd[:], rstd[:], ACT.Sqrt).then_inc(s_fsq, 1)
            e.wait_ge(s_fst, 3)
            e.activation(rstd[:], rstd[:], ACT.Sqrt).then_inc(s_fsq, 1)

        phase(sync=f_io, vector=f_vector, tensor=f_tensor, scalar=f_scalar)

        block = ctx.enter_context(nc.Block())

        def run(e, name):
            for todo in engines[name]:
                if todo is not None:
                    todo(e)
                meet(e)

        @block.sync
        def _(e):
            run(e, "sync")

        @block.gpsimd
        def _(e):
            run(e, "gpsimd")

        @block.scalar
        def _(e):
            run(e, "scalar")

        @block.tensor
        def _(e):
            run(e, "tensor")

        @block.vector
        def _(e):
            run(e, "vector")


INPUTS = ["x", "src", "dst", "edge_type_8", "edge_weight1", "L0_gnn_weight", "L0_gnn_bias", "L1_gnn_Wq",
          "L1_gnn_Wk", "L1_gnn_Wv", "L1_gnn_Wp", "L1_gnn_bp", "L1_gnn_ln1_g", "L1_gnn_ln1_b", "L1_gnn_ln2_g",
          "L1_gnn_ln2_b", "L1_gnn_W1", "L1_gnn_b1", "L1_gnn_W2", "L1_gnn_b2"]


def kernel(**inputs):
    import concourse.bacc as bacc
    from concourse.bass_utils import run_bass_kernel_spmd

    nc = bacc.Bacc("TRN2", target_bir_lowering=False, num_devices=1)
    arrays, args = {}, {}
    for name in INPUTS:
        v = np.ascontiguousarray(inputs[name])
        if name == "edge_weight1":
            v = v.reshape(-1)
        arrays["in_" + name] = v
        args[name] = nc.dram_tensor("in_" + name, v.shape, mybir.dt.from_np(v.dtype), kind="ExternalInput").ap()
    out = nc.dram_tensor("out", (N, D), F32, kind="ExternalOutput").ap()
    build(nc, args, out)
    return run_bass_kernel_spmd(nc, [arrays], core_ids=[0]).results[0]["out"]
```

```python
from contextlib import ExitStack

import numpy as np

import concourse.bass as bass
from concourse import mybir

F32 = mybir.dt.float32
BF16 = mybir.dt.bfloat16
I32 = mybir.dt.int32
I16 = mybir.dt.int16
ALU = mybir.AluOpType
ACT = mybir.ActivationFunctionType
AX = mybir.AxisListType

P = 128
N, D, E = 6250, 256, 200000
REL, HEADS = 8, 8
HD = D // HEADS
FFN = 4 * D
FC = FFN // P
KC = D // P
LOG_P = 7
W = -(-N // P)
NP_ = W * P
JUNK = NP_ - 1
BLOCKS = 4
T = -(-E // (P * 16)) * 16
BT = T // BLOCKS
BI = BT + W
assert T * P >= E and BI * P >= BT * P + W * (P - 1) - P
RAW_G = -(-T // P)
WALK = T + W - 1
QUAD = 4
QUADS = WALK // QUAD
assert WALK % QUAD == 0
ROW_RING = 4
AW = D + HEADS
CH = P // HEADS
CJ = WALK // CH
CL = CJ * P
assert CH * CJ == WALK
DST, SRC, WGT, REC = 0, 1, 2, 4
LOW = -1e30
EPS = 1e-5
SCALE = 1.0 / float(np.sqrt(HD))


class Count:

    def __init__(self, sem):
        self.sem = sem

    def done(self, e, i):
        e.wait_ge(self.sem, i + 1)

    def free(self, e, i, ring):
        if i >= ring:
            e.wait_ge(self.sem, i - ring + 1)


class Chain:

    def __init__(self, e, sem):
        self.e, self.sem, self.n = e, sem, 0

    def __call__(self, ins):
        self.upto(self.add(ins))

    def add(self, ins):
        ins.then_inc(self.sem, 1)
        self.n += 1
        return self.n

    def upto(self, n):
        if n > 0:
            self.e.wait_ge(self.sem, n)


def staggered(chain, items, *steps):
    items = list(items)
    done = [[] for _ in steps]
    for n in range(len(items) + len(steps) - 1):
        for k, step in enumerate(steps):
            if 0 <= n - k < len(items):
                if k:
                    chain.upto(done[k - 1][n - k])
                ins = step(items[n - k])
                done[k].append(chain.add(ins) if ins is not None else 0)
    chain.upto(chain.n)


def build(nc, a, out):
    ctx = ExitStack()
    with ctx:
        def sb(name, cols, dt=F32, rows=P):
            return ctx.enter_context(nc.sbuf_tensor(name, [rows, cols], dt))

        def sem(name):
            return ctx.enter_context(nc.semaphore(name))

        def dram(name, shape, dt=F32):
            return nc.dram_tensor(name, shape, dt, kind="Internal").ap()

        xt_table = dram("xt_table", (REL * NP_, D))
        k_table = dram("k_table", (NP_, D))
        v_table = dram("v_table", (NP_, D))
        x1_store = dram("x1_store", (NP_, D))
        edge_table = dram("edge_table", (T, P * REC))
        half_sorted = dram("half_sorted", (T, P * REC))

        node_a = sb("node_a", W * AW)
        node_b = sb("node_b", W * D)
        edge_s = sb("edge_s", WALK * HEADS)
        walk_s = sb("walk_s", 3 * WALK + WALK // 2)
        src_i, dst_i, dl_i = (walk_s[:, k * WALK:(k + 1) * WALK] for k in range(3))
        src_i = src_i.bitcast(I32)
        dl_b = walk_s[:, 3 * WALK:].bitcast(BF16)
        table = sb("table", max(BLOCKS * BI, WALK), I32)
        iota_q = sb("iota_q", 512)
        iota_s = sb("iota_s", 512, I16)
        iota_p = sb("iota_p", 1)
        ident, tri, ones = sb("ident", P), sb("tri", P), sb("ones", 512)
        ident_b = sb("ident_b", P, BF16)
        STATS = 3
        stats = sb("stats", STATS * 6)
        mv = sb("mv", W * 2)
        mv2 = sb("mv2", 2 * W * 2)
        rstd, nmr = sb("rstd", W), sb("nmr", W)
        small = sb("small", 64)
        pb = ctx.enter_context(nc.psum_tensor("pb", [P, 8, 512], F32))

        class Cut:

            def __init__(self, region):
                self.region, self.at = region, 0

            def __call__(self, cols, dt=F32):
                words = cols if dt in (F32, I32) else -(-cols // 2)
                piece = self.region[:, self.at:self.at + words]
                self.at += words
                assert self.at <= self.region.shape[1]
                return piece if dt == F32 else piece.bitcast(dt)[:, 0:cols]

        cut = Cut(node_a)
        raw_i = {n: cut(RAW_G * P, I32) for n in ("src", "dst", "type")}
        raw_w = cut(RAW_G * P)
        rec = node_b[:, 0:RAW_G * P * REC].rearrange("p (g e f) -> p g e f", g=RAW_G, e=P)
        raw_f = {n: cut(RAW_G * P) for n in ("src", "dst", "row")}
        acc = node_a
        acc_w = node_a[:].rearrange("p (w d) -> p w d", w=W)
        cut = Cut(edge_s)
        win_c, loc_c, lo_c, hi_c, pos_c, q_c, c_c = (cut(T) for _ in range(7))
        int_c = cut(T, I32)
        cut = Cut(node_b)
        w0 = cut(KC * REL * D).rearrange("p (k r o) -> p k r o", k=KC, r=REL)
        xt_out = cut(2 * 4 * D).rearrange("p (s n) -> p s n", s=2)
        x_in = cut(3 * D).rearrange("p (s n) -> p s n", s=3)
        x_t = cut(2 * D).rearrange("p (s k n) -> p s k n", s=2, k=KC)
        RANK_RING = 3
        mask = cut(RANK_RING * BT, BF16).rearrange("p (s n) -> p s n", s=RANK_RING)
        win_b = cut(T, BF16)
        cum = cut(RANK_RING * BT).rearrange("p (s n) -> p s n", s=RANK_RING)
        tot, offs, ends = (cut(BLOCKS * W).rearrange("p (b w) -> p b w", b=BLOCKS) for _ in range(3))
        tot_i = cut(BLOCKS * W, I32)
        end_t = cut(BLOCKS * P).rearrange("p (b w) -> p b w", b=BLOCKS)
        end_c = cut(BLOCKS)
        passed = cut(BLOCKS * BI, BF16)
        cut = Cut(node_b)
        SUM_ROWS, SUM_HOTS, SORT_HOTS = 4, 5, 4
        sum_rows = cut(SUM_ROWS * 4 * D).rearrange("p (s k n) -> p s k n", s=SUM_ROWS, k=4)
        sum_hot = cut(SUM_HOTS * P).rearrange("p (s n) -> p s n", s=SUM_HOTS)
        idx_s = cut(2 * BI, I32).rearrange("p (s n) -> p s n", s=2)
        loc_s = cut(2 * BI).rearrange("p (s n) -> p s n", s=2)
        lo_s = cut(BI)
        hot_q = cut(SORT_HOTS * P, BF16).rearrange("p (s q) -> p s q", s=SORT_HOTS)
        hot_v = cut(SORT_HOTS * 3 * P, BF16).rearrange("p (s v q) -> p s v q", s=SORT_HOTS, v=3)
        BIE = BI + BI % 2
        hot_c = cut(SORT_HOTS * BIE, BF16).rearrange("p (s n) -> p s n", s=SORT_HOTS)
        bias0 = sb("bias0", D)
        one_b = sb("one_b", 2, BF16)[:, 0:1]
        cut = Cut(node_a)
        DIGITS = (P, W)
        sort_rec = cut(T * REC).rearrange("p (j f) -> p j f", f=REC)
        sort_pos, sort_mask, sort_cum, sort_dig = (cut(T) for _ in range(4))
        cut = Cut(node_b)
        sort_idx = cut(T, I32)
        sort_tot, sort_offs, sort_end = cut(P), cut(P), cut(P)
        unsorted = sb("unsorted", 1, I32)
        zero_b = sb("zero_b", 448, BF16)[:]
        cut = Cut(edge_s)
        wqkv = cut(KC * 3 * D).rearrange("p (k n) -> p k n", k=KC)
        x1t = cut(2 * D).rearrange("p (s k n) -> p s k n", s=2, k=KC)
        kv_out = cut(2 * 2 * D).rearrange("p (s n) -> p s n", s=2)
        cut = Cut(node_b)
        recs = cut(RAW_G * P * REC).rearrange("p (g e f) -> p g e f", g=RAW_G, e=P)
        u_row, w_row, wgt_i = cut(RAW_G * P), cut(RAW_G * P), cut(WALK)
        item_col, u_col, t_col = cut(RAW_G), cut(RAW_G), cut(RAW_G)
        u_int, t_int = cut(RAW_G, I32), cut(RAW_G, I32)
        item_row = edge_s[:, 0:WALK]
        cut = Cut(node_b)
        rows = cut(ROW_RING * QUAD * D).rearrange("p (s k n) -> p s k n", s=ROW_RING, k=QUAD)
        w_hot = cut(2 * QUAD * P).rearrange("p (s n) -> p s n", s=2)
        prods = sb("prods", 2 * QUAD * D)[:].rearrange("p (s n) -> p s n", s=2)
        parts = cut(2 * QUAD * HEADS).rearrange("p (s n) -> p s n", s=2)
        PEN0 = cut.at
        msgs = cut(2 * QUAD * AW).rearrange("p (s k n) -> p s k n", s=2, k=QUAD)
        cut = Cut(edge_s)
        wp = cut(KC * D).rearrange("p (k n) -> p k n", k=KC)
        w1 = cut(KC * FFN).rearrange("p (k n) -> p k n", k=KC)
        w2 = cut(FC * D).rearrange("p (k n) -> p k n", k=FC)
        vec = {n: cut(D) for n in ("bp", "ln1_g", "ln1_b", "ln2_g", "ln2_b", "b2")}
        b1c = cut(FC)
        att_t = cut(2 * D).rearrange("p (s k n) -> p s k n", s=2, k=KC)
        h1_t = cut(2 * KC * 512).rearrange("p (s k n) -> p s k n", s=2, k=KC)
        hid = [r.rearrange("p (k n) -> p k n", k=FC) for r in (cut(FC * 512), walk_s[:, 0:FC * 512])]
        CHUNK = 8
        recip = sb("recip", CHUNK * HEADS)
        roots_s = sb("roots_s", 2 * 3 * CHUNK)
        scan_s = node_a[:, 0:CL]
        PENW = CL // 2 + 1
        pen = node_b[:, PEN0:PEN0 + PENW].bitcast(BF16)[:, 0:CL + 1]
        dst_t = node_b[:, PEN0 + PENW:PEN0 + PENW + 257]
        same = node_b[:, PEN0 + PENW + 257:PEN0 + PENW + 513]
        dst_x = sb("dst_x", 512)[:].rearrange("p (s n) -> p s n", s=2)
        row = [node_b[0:1, 130 * k:130 * k + P] for k in range(12)]
        carry = node_b[:, 130 * 12:130 * 12 + 2]
        score_v = edge_s[:].rearrange("p (j n) -> p j n", j=CJ)

        class Windows:

            def __init__(self, e, name):
                self.e, self.regs = e, [e.alloc_register(f"{name}{k}") for k in range(2 * QUAD)]

            def load(self, q):
                r = self.regs[q % 2 * QUAD:(q % 2 + 1) * QUAD]
                self.e.reg_load(r, table[0:1, q * QUAD:(q + 1) * QUAD])
                return [self.e.snap(x, min_val=0, max_val=(W - 1) * AW) for x in r]

        s_meet = sem("s_meet")
        meets = {}

        def meet(e):
            k = meets[e] = meets.get(e, 0) + 1
            e.drain().then_inc(s_meet, 1)
            e.wait_ge(s_meet, 5 * k)

        engines = {n: [] for n in ("sync", "gpsimd", "scalar", "tensor", "vector")}

        def phase(**parts):
            for n, todo in engines.items():
                todo.append(parts.get(n))

        s_padded, s_consts, s_rawload = sem("s_padded"), sem("s_consts"), sem("s_rawload")
        s_float, s_turned, s_cols = sem("s_float"), sem("s_turned"), sem("s_cols")
        s_dv0, s_gp0 = sem("s_dv0"), sem("s_gp0")
        turned = [("src", raw_f["src"], c_c), ("row", raw_f["row"], pos_c)]
        packs = [(v, g) for v in range(len(turned)) for g in range(0, RAW_G, 4)]
        s_recz, s_rec, s_recout = sem("s_recz"), sem("s_rec"), sem("s_recout")

        s_nextload, s_bad, s_badsum = sem("s_nextload"), sem("s_bad"), sem("s_badsum")
        raw_next = node_b[:, RAW_G * P * REC:RAW_G * P * (REC + 1)].bitcast(I32)
        falls = node_b[:, RAW_G * P * (REC + 1):RAW_G * P * (REC + 1) + RAW_G * P]
        fall_sum = node_b[:, RAW_G * P * (REC + 2):RAW_G * P * (REC + 2) + 1]

        def load_row(e, to, d, landed):
            v = to.rearrange("p (g e) -> p g e", e=P)
            n = d.shape[0]
            full = n // P
            whole = full // P
            rest, tail = full - whole * P, n - full * P
            e.dma_start(v[:, 0:whole, :], d[0:whole * P * P].rearrange("(g p e) -> p g e", p=P, e=P))\
                .then_inc(landed, 16)
            e.dma_start(v[0:rest, whole, :], d[whole * P * P:full * P].rearrange("(p e) -> p e", e=P))\
                .then_inc(landed, 16)
            e.dma_start(v[rest:rest + 1, whole, 0:tail], d[full * P:n].rearrange("(a e) -> a e", a=1))\
                .then_inc(landed, 16)

        def load_edges(e):
            e.wait_ge(s_padded, 5)
            for name, to in (("src", raw_i["src"]), ("dst", raw_i["dst"]),
                             ("edge_type_8", raw_i["type"]), ("edge_weight1", raw_w)):
                load_row(e, to, a[name], s_rawload)
            load_row(e, raw_next, a["dst"][1:E], s_nextload)
            e.wait_ge(s_rec, 3)
            g = T // P
            for lo, hi, rows_ in ((0, g, P), (g, RAW_G, T - g * P)):
                e.dma_start(edge_table[lo * P:lo * P + (hi - lo) * rows_, :].rearrange("(g p) n -> p g n", p=rows_),
                            rec[0:rows_, lo:hi, :, :].rearrange("p g e f -> p g (e f)")).then_inc(s_recout, 16)
            e.wait_ge(s_recout, 32)

        def make_consts(e):
            c = Chain(e, s_gp0)
            e.memset(rec, 0.0).then_inc(s_recz, 1)
            c(e.memset(ident[:], 0.0))
            c(e.affine_select(out=ident[:], in_=ident[:], compare_op=ALU.not_equal, fill=1.0, base=0,
                              pattern=[[-1, P]], channel_multiplier=1))
            c(e.memset(ones[:], 1.0))
            c(e.affine_select(out=tri[:], in_=ones[:, 0:P], compare_op=ALU.is_gt, fill=0.0, base=0,
                              pattern=[[1, P]], channel_multiplier=-1))
            c(e.iota(iota_q[:], [[1, 512]], base=0, channel_multiplier=0, allow_small_or_imprecise_dtypes=True))
            c(e.iota(iota_s[:], [[1, 512]], base=0, channel_multiplier=0))
            c(e.iota(iota_p[:], [[1, 1]], base=0, channel_multiplier=1, allow_small_or_imprecise_dtypes=True))
            c(e.tensor_copy(ident_b[:], ident[:]))
            c(e.memset(one_b, 1.0))
            e.sem_inc(s_consts, 1)

        def edges_float(e):
            e.memset(raw_i["src"], JUNK).then_inc(s_padded, 1)
            e.memset(raw_i["dst"], JUNK).then_inc(s_padded, 1)
            e.memset(raw_i["type"], 0).then_inc(s_padded, 1)
            e.memset(raw_w, 0.0).then_inc(s_padded, 1)
            e.memset(raw_next, JUNK).then_inc(s_padded, 1)
            e.wait_ge(s_rawload, 16 * 12)
            e.tensor_copy(raw_f["src"], raw_i["src"]).then_inc(s_float, 1)
            e.tensor_copy(raw_f["dst"], raw_i["dst"]).then_inc(s_float, 1)
            e.scalar_tensor_tensor(raw_f["row"], raw_i["type"], float(NP_), raw_i["dst"], ALU.mult, ALU.add)\
                .then_inc(s_float, 1)
            c = Chain(e, s_dv0)
            e.wait_ge(s_nextload, 48)
            c(e.tensor_tensor(falls, raw_i["dst"], raw_next, ALU.is_gt))
            c(e.tensor_reduce(fall_sum, falls, AX.X, ALU.add))
            e.sem_inc(s_bad, 1)
            e.wait_ge(s_badsum, 1)
            c(e.tensor_scalar(unsorted[0:1, :], pb[0:1, 7, 0:1], 1.0, None, ALU.min))
            e.wait_ge(s_cols, len(packs))
            for src, sh, ms, to, one in ((c_c, LOG_P, None, win_c, 0), (c_c, None, P - 1, loc_c, 1),
                                         (pos_c, 8, None, hi_c, 0), (pos_c, None, 255, lo_c, 0)):
                c(e.tensor_copy(int_c, src))
                if sh is not None:
                    c(e.tensor_scalar(int_c, int_c, sh, None, ALU.arith_shift_right))
                else:
                    c(e.tensor_scalar(int_c, int_c, ms, None, ALU.bitwise_and))
                c(e.tensor_scalar(to, int_c, float(one), None, ALU.add))
            c(e.memset(zero_b, 0.0))

        def edges_turn(e):
            e.wait_ge(s_consts, 1)
            e.wait_ge(s_float, 3)
            for n, (v, g0) in enumerate(packs):
                if n >= 4:
                    e.wait_ge(s_cols, n - 3)
                for g in range(g0, min(g0 + 4, RAW_G)):
                    ins = e.transpose(pb[:, n % 4, (g - g0) * P:(g - g0 + 1) * P],
                                      turned[v][1].rearrange("p (g e) -> p g e", e=P)[:, g, :], ident[:])
                ins.then_inc(s_turned, 1)
            e.wait_ge(s_bad, 1)
            e.matmul(pb[0:1, 7, 0:1], fall_sum, ones[:, 0:1], start=True, stop=True).then_inc(s_badsum, 1)

        def edges_cols(e):
            e.wait_ge(s_recz, 1)
            e.wait_ge(s_float, 3)
            for f, v in ((DST, raw_f["dst"]), (SRC, raw_f["src"]), (WGT, raw_w)):
                e.activation(rec[:, :, :, f], v.rearrange("p (g e) -> p g e", e=P), ACT.Copy).then_inc(s_rec, 1)
            for n, (v, g0) in enumerate(packs):
                e.wait_ge(s_turned, n + 1)
                cols = min(T - g0 * P, 512)
                to = turned[v][2]
                e.activation(to[:, g0 * P:g0 * P + cols], pb[:, n % 4, 0:cols], ACT.Copy).then_inc(s_cols, 1)

        phase(sync=load_edges, gpsimd=make_consts, vector=edges_float, tensor=edges_turn, scalar=edges_cols)

        s_recld, s_digs, s_digp, s_ranked, s_sv = (sem(n) for n in (
            "s_recld", "s_digs", "s_digp", "s_ranked", "s_sv"))
        s_scat = [sem("s_scat0"), sem("s_scat1")]
        passes = [(edge_table, half_sorted), (half_sorted, edge_table)]

        def if_unsorted(body):
            def go(e):
                flag = e.value_load(unsorted[0:1, 0:1], min_val=0, max_val=1)
                with e.If(flag == 1):
                    body(e)
            return go

        def order_io(e):
            for n, (src, _) in enumerate(passes):
                if n:
                    e.wait_ge(s_scat[n - 1], 16 * T)
                e.dma_start(sort_rec.rearrange("p j f -> p (j f)"),
                            src.rearrange("t n -> (t n)").rearrange("(p m) -> p m", p=P)).then_inc(s_recld, 16)

        def order_rank(e):
            c = Chain(e, s_sv)
            for n, digits in enumerate(DIGITS):
                e.wait_ge(s_recld, 16 * (n + 1))
                c(e.tensor_copy(sort_idx, sort_rec[:, :, DST]))
                if n == 0:
                    c(e.tensor_scalar(sort_idx, sort_idx, P - 1, None, ALU.bitwise_and))
                else:
                    c(e.tensor_scalar(sort_idx, sort_idx, LOG_P, None, ALU.arith_shift_right))
                c(e.tensor_copy(sort_dig, sort_idx))
                for d in range(digits):
                    c(e.tensor_scalar(sort_mask, sort_dig, float(d), None, ALU.is_equal, ALU.add,
                                      accum_out=sort_tot[:, d:d + 1]))
                e.sem_inc(s_digs, 1)
                e.wait_ge(s_digp, 2 * (n + 1))
                c(e.tensor_tensor_scan(sort_end[:, 0:digits], ones[:, 0:digits], pb[:, 1, 0:digits], 0.0,
                                       ALU.mult, ALU.add))
                c(e.tensor_tensor(sort_offs[:, 0:digits], sort_end[:, 0:digits], pb[:, 1, 0:digits], ALU.subtract))
                c(e.scalar_tensor_tensor(sort_offs[:, 0:digits], pb[:, 0, 0:digits], -1.0, sort_offs[:, 0:digits],
                                         ALU.add, ALU.add))
                c(e.memset(sort_pos, 0.0))
                for d in range(digits):
                    c(e.tensor_scalar(sort_mask, sort_dig, float(d), None, ALU.is_equal))
                    c(e.tensor_tensor_scan(sort_cum, ones[:, 0:1].to_broadcast([P, T]), sort_mask,
                                           sort_offs[:, d:d + 1], ALU.mult, ALU.add))
                    c(e.copy_predicated(sort_pos, sort_mask.bitcast(I32), sort_cum))
                c(e.tensor_copy(sort_idx, sort_pos))
                e.sem_inc(s_ranked, 1)

        def order_count(e):
            for n, digits in enumerate(DIGITS):
                e.wait_ge(s_digs, n + 1)
                e.matmul(pb[:, 0, 0:digits], tri[:], sort_tot[:, 0:digits], start=True, stop=True).then_inc(s_digp, 1)
                e.matmul(pb[:, 1, 0:digits], ones[:, 0:P], sort_tot[:, 0:digits], start=True, stop=True)\
                    .then_inc(s_digp, 1)

        def order_move(e):
            for n, (_, to) in enumerate(passes):
                e.wait_ge(s_ranked, n + 1)
                for j in range(T):
                    e.indirect_dma_start(to.rearrange("t (e f) -> (t e) f", f=REC),
                                         bass.IndirectOffsetOnAxis(ap=sort_idx[:, j:j + 1], axis=0),
                                         sort_rec[:, j, :], None).then_inc(s_scat[n], 16)
                e.wait_ge(s_scat[n], 16 * T)

        phase(sync=if_unsorted(order_io), vector=if_unsorted(order_rank), tensor=if_unsorted(order_count),
              gpsimd=if_unsorted(order_move))

        s_w0, s_x = sem("s_w0"), [sem("s_x0"), sem("s_x1")]
        s_xz, s_xtr, s_xtc, s_xm, s_xe = sem("s_xz"), sem("s_xtr"), sem("s_xtc"), sem("s_xm"), sem("s_xe")
        s_xst = [sem("s_xst0"), sem("s_xst1")]
        s_rank, s_tot, s_pre, s_end, s_endt, s_cmp, s_win = (sem(n) for n in (
            "s_rank", "s_tot", "s_pre", "s_end", "s_endt", "s_cmp", "s_win"))
        s_bias0, s_acc0 = sem("s_bias0"), sem("s_acc0")
        xt_v = xt_table.rearrange("(r n) o -> n r o", r=REL)

        def node_rows(w):
            return min(N - w * P, P)

        def x_slot(w):
            return 2 if w == W - 1 else w % 2

        def table_io(e):
            e.dma_start(bias0[:], a["L0_gnn_bias"].rearrange("(a d) -> a d", a=1).to_broadcast([P, D]))\
                .then_inc(s_bias0, 16)
            for k in range(KC):
                e.dma_start(w0[:, k, :, :], a["L0_gnn_weight"][:, k * P:(k + 1) * P, :].rearrange("r p o -> p r o"))\
                    .then_inc(s_w0, 16)

            def store(n):
                w, half = divmod(n, 2)
                e.wait_ge(s_xe, 2 * (n + 1))
                e.dma_start(xt_v[w * P:(w + 1) * P, half * 4:half * 4 + 4, :],
                            xt_out[:, n % 2, :].rearrange("p (r o) -> p r o", r=4)).then_inc(s_xst[n % 2], 16)

            for n in range(2 * W):
                store(n)
            e.wait_ge(s_xst[0], 16 * W)
            e.wait_ge(s_xst[1], 16 * W)

        def table_x(e):
            for w in range(W):
                if w == W - 1:
                    e.wait_ge(s_xz, 1)
                if w >= 2:
                    e.wait_ge(s_xtr, w - 1)
                e.dma_start(x_in[0:node_rows(w), x_slot(w), :], a["x"][w * P:w * P + node_rows(w), :])\
                    .then_inc(s_x[w % 2], 16)

        def table_products(e):
            def turn(w):
                e.wait_ge(s_x[w % 2], 16 * (w // 2 + 1))
                if w >= 1:
                    e.wait_ge(s_xtc, w)
                for k in range(KC):
                    ins = e.transpose(pb[:, 4, k * P:(k + 1) * P], x_in[:, x_slot(w), k * P:(k + 1) * P], ident[:])
                ins.then_inc(s_xtr, 1)

            turn(0)
            e.wait_ge(s_w0, 16 * KC)
            for w in range(W):
                if w + 1 < W:
                    turn(w + 1)
                e.wait_ge(s_xtc, w + 1)
                for half in range(2):
                    for q in range(2):
                        n = 4 * w + 2 * half + q
                        if n >= 4:
                            e.wait_ge(s_xe, n - 3)
                        for k in range(KC):
                            ins = e.matmul(pb[:, n % 4, :], x_t[:, w % 2, k, :],
                                           w0[:, k, half * 4 + q * 2:half * 4 + q * 2 + 2, :],
                                           start=(k == 0), stop=(k == KC - 1))
                        ins.then_inc(s_xm, 1)
                if w == W // 4:
                    count_products(e)
            window_products(e)

        def table_copies(e):
            def turned_x(w):
                e.wait_ge(s_xtr, w + 1)
                if w >= 2:
                    e.wait_ge(s_xm, 4 * (w - 1))
                e.activation(x_t[:, w % 2, :, :], pb[:, 4, 0:D].rearrange("p (k n) -> p k n", k=KC), ACT.Copy)\
                    .then_inc(s_xtc, 1)

            turned_x(0)
            e.wait_ge(s_bias0, 16)
            for w in range(W):
                if w + 1 < W:
                    turned_x(w + 1)
                e.activation(acc_w[:, w, 0:D], bias0[:], ACT.Copy).then_inc(s_acc0, 1)
                for n in range(4 * w, 4 * w + 4):
                    half = n // 2
                    e.wait_ge(s_xm, n + 1)
                    if n % 2 == 0 and half >= 2:
                        e.wait_ge(s_xst[half % 2], 16 * (half // 2))
                    e.activation(xt_out[:, half % 2, (n % 2) * 512:(n % 2 + 1) * 512], pb[:, n % 4, :], ACT.Copy)\
                        .then_inc(s_xe, 1)

        def count_products(e):
            e.wait_ge(s_tot, 1)
            flat = tot.rearrange("p b w -> p (b w)")
            e.matmul(pb[:, 5, 0:BLOCKS * W], tri[:], flat, start=True, stop=True).then_inc(s_pre, 1)
            e.matmul(pb[:, 6, 0:BLOCKS * W], ones[:, 0:P], flat, start=True, stop=True).then_inc(s_pre, 1)

        def window_products(e):
            e.wait_ge(s_end, 1)
            for b in range(BLOCKS):
                ins = e.transpose(pb[:, 7, b * P:(b + 1) * P], end_t[:, b, :], ident[:])
            ins.then_inc(s_endt, 1)
            e.wait_ge(s_cmp, 1)
            for b in range(BLOCKS):
                if b >= 3:
                    e.wait_ge(s_win, b - 2)
                e.matmul(pb[0:1, 5 + b % 3, 0:BI], one_b, passed[:, b * BI:(b + 1) * BI], start=True, stop=True)\
                    .then_inc(s_endt, 1)

        def ranks(e):
            c = Chain(e, s_rank)
            e.memset(x_in[:, 2, :], 0.0).then_inc(s_xz, 1)
            c(e.tensor_copy(win_b, win_c))
            wins = [win_b[:, b * BT:(b + 1) * BT] for b in range(BLOCKS)]
            at = []
            for b in range(BLOCKS):
                for w in range(W):
                    n = len(at)
                    c.upto(at[n - RANK_RING]) if n >= RANK_RING else None
                    at.append(c.add(e.tensor_scalar(mask[:, n % RANK_RING, :], wins[b], float(w), None, ALU.is_equal,
                                                    ALU.add, accum_out=tot[:, b, w:w + 1])))
            c(e.memset(end_t, 1e6))
            e.sem_inc(s_tot, 1)
            e.wait_ge(s_pre, 2)
            flat = "p b w -> p (b w)"
            offs_f, ends_f = offs.rearrange(flat), ends.rearrange(flat)
            c(e.tensor_scalar(tot_i, pb[:, 6, 0:BLOCKS * W], float(P - 1), None, ALU.add))
            c(e.tensor_scalar(tot_i, tot_i, LOG_P, None, ALU.arith_shift_right))
            c(e.tensor_copy(offs_f, tot_i))
            for b in range(BLOCKS):
                c(e.tensor_tensor_scan(ends[:, b, :], ones[:, 0:W], offs[:, b, :], 0.0, ALU.mult, ALU.add))
            c(e.tensor_copy(end_t[:, :, 0:W], ends))
            c(e.tensor_tensor(offs_f, ends_f, offs_f, ALU.subtract))
            c(e.tensor_scalar(offs_f, offs_f, float(P), -1.0, ALU.mult, ALU.add))
            c(e.tensor_tensor(offs_f, offs_f, pb[:, 5, 0:BLOCKS * W], ALU.add))
            e.sem_inc(s_end, 1)

            steps = [(b, w) for b in range(BLOCKS) for w in range(W)]
            masked, run, taken = [], [], []
            for n in range(len(steps) + 2):
                if n < len(steps):
                    b, w = steps[n]
                    if n >= RANK_RING:
                        c.upto(taken[n - RANK_RING])
                    masked.append(c.add(e.tensor_scalar(mask[:, n % RANK_RING, :], wins[b], float(w), None,
                                                        ALU.is_equal)))
                if 1 <= n <= len(steps):
                    b, w = steps[n - 1]
                    k = (n - 1) % RANK_RING
                    c.upto(masked[n - 1])
                    run.append(c.add(e.tensor_tensor_scan(cum[:, k, :], ones[:, 0:BT], mask[:, k, :],
                                                          offs[:, b, w:w + 1], ALU.mult, ALU.add)))
                if n >= 2:
                    b, w = steps[n - 2]
                    k = (n - 2) % RANK_RING
                    c.upto(max(run[n - 2], taken[-1] if taken else 0))
                    taken.append(c.add(e.copy_predicated(pos_c[:, b * BT:(b + 1) * BT], mask[:, k, :].bitcast(I16),
                                                         cum[:, k, :])))
            c.upto(taken[-1])
            c(e.tensor_copy(int_c, pos_c))
            c(e.tensor_scalar(int_c, int_c, P - 1, None, ALU.bitwise_and))
            c(e.tensor_copy(q_c, int_c))
            c(e.tensor_copy(int_c, pos_c))
            c(e.tensor_scalar(int_c, int_c, LOG_P, None, ALU.arith_shift_right))
            c(e.tensor_copy(c_c, int_c))
            e.wait_ge(s_endt, 1)
            for b in range(BLOCKS):
                c(e.tensor_copy(end_c[:, b:b + 1], pb[:, 7, b * P:b * P + 1]))
                c(e.tensor_scalar(passed[:, b * BI:(b + 1) * BI], iota_q[:, 0:BI], end_c[:, b:b + 1], None,
                                  ALU.is_ge))
            e.sem_inc(s_cmp, 1)
            for b in range(BLOCKS):
                e.wait_ge(s_endt, 2 + b)
                c(e.tensor_scalar(table[0:1, b * BI:(b + 1) * BI], pb[0:1, 5 + b % 3, 0:BI], float(W - 1), float(AW),
                                  ALU.min, ALU.mult))
                e.sem_inc(s_win, 1)

        phase(sync=table_io, gpsimd=table_x, tensor=table_products, scalar=table_copies, vector=ranks)

        s_rows = [sem(f"s_rows{k}") for k in range(SUM_ROWS)]
        built, weighed, moved, sort_done, s_extract = (Count(sem(n)) for n in (
            "s_built", "s_weighed", "s_moved", "s_sort_done", "s_extract"))
        hot, summed, added, got = (Count(sem(n)) for n in ("s_hot", "s_summed", "s_added", "s_got"))
        ITEMS = BLOCKS * BI
        assert ITEMS % 4 == 0
        SUM_BANKS = 5
        stages = [[(((st - 1) * BI + u) if st else None, (st * BT + u) if st < BLOCKS and u < BT else None)
                   for u in range(BI if st else BT)] for st in range(BLOCKS + 1)]

        def l0_gather(e):
            for i in range(ITEMS):
                b, u = divmod(i, BI)
                q, k = divmod(i, 4)
                if u == 0:
                    got.done(e, b)
                if k == 0 and q >= SUM_ROWS:
                    summed.done(e, (q - SUM_ROWS) * 4 + 3)
                e.indirect_dma_start(sum_rows[:, q % SUM_ROWS, k, :], None, xt_table,
                                     bass.IndirectOffsetOnAxis(ap=idx_s[:, b % 2, u:u + 1], axis=0))\
                    .then_inc(s_rows[q % SUM_ROWS], 16)

        def l0_weigh(e, t):
            built.done(e, t)
            moved.free(e, t, SORT_HOTS)
            for v, byte in enumerate((lo_c, hi_c, loc_c)):
                if v or t >= BT:
                    ins = e.activation(hot_v[:, t % SORT_HOTS, v, :], hot_q[:, t % SORT_HOTS, :], ACT.Copy,
                                       scale=byte[:, t:t + 1])
            ins.then_inc(weighed.sem, 1)

        def l0_scalar(e):
            for t in range(T):
                l0_weigh(e, t)

        def l0_tensor(e):
            for st, steps in enumerate(stages):
                if st < BLOCKS:
                    if st:
                        got.done(e, st - 1)
                    for v in range(3):
                        e.matmul(pb[:, v, 0:BI], zero_b[:, 0:P], zero_b[:, 0:BI], start=True, stop=False,
                                 skip_group_check=True)
                for i, t in steps:
                    if t is not None:
                        weighed.done(e, t)
                        built.done(e, t)
                        for v in range(3):
                            ins = e.matmul(pb[:, v, 0:BI], hot_v[:, t % SORT_HOTS, v, :],
                                           hot_c[:, t % SORT_HOTS, 0:BI], start=False, stop=False,
                                           skip_group_check=True)
                        ins.then_inc(moved.sem, 1)
                        if t % BT == BT - 1:
                            for v in range(3):
                                ins = e.matmul(pb[:, v, 0:BI], zero_b[:, 0:P], zero_b[:, 0:BI], start=False,
                                               stop=True, skip_group_check=True)
                            ins.then_inc(sort_done.sem, 1)
                    if i is not None:
                        q, k = divmod(i, 4)
                        hot.done(e, i)
                        if k == 0:
                            e.wait_ge(s_rows[q % SUM_ROWS], 64 * (q // SUM_ROWS + 1))
                        added.free(e, i, SUM_BANKS)
                        e.matmul(pb[:, 3 + i % SUM_BANKS, 0:D], sum_hot[:, i % SUM_HOTS, :],
                                 sum_rows[:, q % SUM_ROWS, k, :], start=True, stop=True).then_inc(summed.sem, 1)

        def l0_vector(e):
            win = Windows(e, "l0_win")
            at = {}

            def add(i):
                if i % QUAD == 0:
                    for k, w in enumerate(win.load(i // QUAD)):
                        at[i + k] = w
                summed.done(e, i)
                added.free(e, i, 1)
                to = acc[:, bass.ds(at[i], D)]
                e.tensor_tensor(to, to, pb[:, 3 + i % SUM_BANKS, 0:D], ALU.add).then_inc(added.sem, 1)

            def extract(b):
                sort_done.done(e, b)
                e.tensor_copy(lo_s, pb[:, 0, 0:BI])
                e.tensor_copy(loc_s[:, b % 2, :], pb[:, 2, 0:BI]).then_inc(s_extract.sem, 1)
                s_extract.done(e, b)
                e.scalar_tensor_tensor(idx_s[:, b % 2, :], pb[:, 1, 0:BI], 256.0, lo_s, ALU.mult, ALU.add)\
                    .then_inc(got.sem, 1)

            LAG = 3
            for st, steps in enumerate(stages):
                for u, (i, t) in enumerate(steps):
                    if i is not None:
                        if i % BI == 0:
                            got.done(e, i // BI)
                        summed.free(e, i, SUM_HOTS)
                        e.tensor_scalar(sum_hot[:, i % SUM_HOTS, :], iota_s[:, 1:P + 1],
                                        loc_s[:, (st - 1) % 2, i % BI:i % BI + 1], None, ALU.is_equal)\
                            .then_inc(hot.sem, 1)
                    if t is not None:
                        k = t % SORT_HOTS
                        moved.free(e, t, SORT_HOTS)
                        if st == 0:
                            e.tensor_scalar(hot_v[:, k, 0, :], iota_s[:, 0:P], q_c[:, t:t + 1], lo_c[:, t:t + 1],
                                            ALU.is_equal, ALU.mult)
                        e.tensor_scalar(hot_q[:, k, :], iota_s[:, 0:P], q_c[:, t:t + 1], None, ALU.is_equal)
                        e.tensor_scalar(hot_c[:, k, 0:BI], iota_s[:, 0:BI], c_c[:, t:t + 1], None, ALU.is_equal)\
                            .then_inc(built.sem, 1)
                    if i is not None and i >= LAG:
                        add(i - LAG)
                    if (st and st < BLOCKS and u == BT + LAG) or (st == 0 and u == BT - 1):
                        extract(st)
            for i in range(ITEMS - LAG, ITEMS):
                add(i)

        phase(scalar=l0_scalar, gpsimd=l0_gather, tensor=l0_tensor, vector=l0_vector)

        s_xall = [sem(f"s_xall{k}") for k in range(-(-W // CHUNK))]
        s_wq, s_n1, s_stat, s_sq = sem("s_wq"), sem("s_n1"), sem("s_stat"), sem("s_sq")
        s_norm, s_nt, s_ntc, s_qkv, s_qc, s_kvc = (sem(n) for n in (
            "s_norm", "s_nt", "s_ntc", "s_qkv", "s_qc", "s_kvc"))
        s_kvst = [sem("s_kvst0"), sem("s_kvst1")]
        s_x1st, s_xpad = sem("s_x1st"), sem("s_xpad")
        x1 = node_b[:].rearrange("p (w d) -> p w d", w=W)
        chunks = [list(range(w, min(w + CHUNK, W))) for w in range(0, W, CHUNK)]
        assert len(chunks[-1]) == 1 and node_rows(W - 2) == P

        def mid_io(e):
            e.wait_ge(s_xpad, 1)
            for k, ws in enumerate(chunks):
                if len(ws) > 1:
                    e.dma_start(x1[:, ws[0]:ws[-1] + 1, :],
                                a["x"][ws[0] * P:(ws[-1] + 1) * P, :].rearrange("(w p) d -> p w d", p=P))\
                        .then_inc(s_xall[k], 16)
                else:
                    e.dma_start(x1[0:node_rows(ws[0]), ws[0], :], a["x"][ws[0] * P:N, :]).then_inc(s_xall[k], 16)
            for n, name in enumerate(("L1_gnn_Wq", "L1_gnn_Wk", "L1_gnn_Wv")):
                e.dma_start(wqkv[:, :, n * D:(n + 1) * D], a[name].rearrange("(k p) n -> p k n", p=P))\
                    .then_inc(s_wq, 16)
            for w in range(W):
                e.wait_ge(s_norm, w + 1)
                e.dma_start(x1_store[w * P:(w + 1) * P, :], x1[:, w, :]).then_inc(s_x1st, 16)
                e.wait_ge(s_kvc, w + 1)
                e.dma_start(k_table[w * P:(w + 1) * P, :], kv_out[:, w % 2, 0:D]).then_inc(s_kvst[w % 2], 16)
                e.dma_start(v_table[w * P:(w + 1) * P, :], kv_out[:, w % 2, D:2 * D]).then_inc(s_kvst[w % 2], 16)
            e.wait_ge(s_x1st, 16 * W)
            e.wait_ge(s_kvst[0], 32 * (W - W // 2))
            e.wait_ge(s_kvst[1], 32 * (W // 2))

        def mid_vector(e):
            c = Chain(e, s_n1)
            e.memset(x1[:, W - 1, :], 0.0).then_inc(s_xpad, 1)
            def relu_add(w):
                if w % CHUNK == 0:
                    e.wait_ge(s_xall[w // CHUNK], 16)
                return e.scalar_tensor_tensor(x1[:, w, :], acc_w[:, w, 0:D], 0.0, x1[:, w, :], ALU.max, ALU.add)

            staggered(
                c, range(W),
                relu_add,
                lambda w: e.bn_stats(stats[:, w % STATS * 6:(w % STATS + 1) * 6], x1[:, w, :]),
                lambda w: e.bn_aggr(mv[:, 2 * w:2 * w + 2], stats[:, w % STATS * 6:(w % STATS + 1) * 6]))
            c(e.tensor_scalar(rstd[:], mv[:].rearrange("p (w t) -> p t w", t=2)[:, 1, :], EPS, None, ALU.add))
            e.sem_inc(s_stat, 1)
            e.wait_ge(s_sq, 1)
            c(e.reciprocal(rstd[:], rstd[:]))
            c(e.scalar_tensor_tensor(nmr[:], mv[:].rearrange("p (w t) -> p t w", t=2)[:, 0, :], -1.0, rstd[:],
                                     ALU.mult, ALU.mult))
            for w in range(W + 2):
                if w < W:
                    e.tensor_scalar(x1[:, w, :], x1[:, w, :], rstd[:, w:w + 1], nmr[:, w:w + 1], ALU.mult, ALU.add)\
                        .then_inc(s_norm, 1)
                if w >= 2:
                    v = w - 2
                    e.wait_ge(s_qkv, 2 * v + 2)
                    e.tensor_copy(acc_w[:, v, 0:D], pb[:, 4 + v % 4, 0:D]).then_inc(s_qc, 1)

        def mid_tensor(e):
            def turn(w):
                e.wait_ge(s_norm, w + 1)
                if w >= 2:
                    e.wait_ge(s_ntc, w - 1)
                for k in range(KC):
                    ins = e.transpose(pb[:, w % 2, k * P:(k + 1) * P], x1[:, w, k * P:(k + 1) * P], ident[:])
                ins.then_inc(s_nt, 1)

            e.wait_ge(s_wq, 48)
            turn(0)
            for w in range(W):
                if w + 1 < W:
                    turn(w + 1)
                e.wait_ge(s_ntc, w + 1)
                if w >= 2:
                    e.wait_ge(s_kvc, w - 1)
                for k in range(KC):
                    ins = e.matmul(pb[:, 2 + w % 2, :], x1t[:, w % 2, k, :], wqkv[:, k, D:3 * D],
                                   start=(k == 0), stop=(k == KC - 1))
                ins.then_inc(s_qkv, 1)
                if w >= 4:
                    e.wait_ge(s_qc, w - 3)
                for k in range(KC):
                    ins = e.matmul(pb[:, 4 + w % 4, 0:D], x1t[:, w % 2, k, :], wqkv[:, k, 0:D],
                                   start=(k == 0), stop=(k == KC - 1))
                ins.then_inc(s_qkv, 1)

        def mid_scalar(e):
            e.wait_ge(s_stat, 1)
            e.activation(rstd[:], rstd[:], ACT.Sqrt).then_inc(s_sq, 1)

            def turned(w):
                e.wait_ge(s_nt, w + 1)
                if w >= 2:
                    e.wait_ge(s_qkv, 2 * (w - 1))
                e.activation(x1t[:, w % 2, :, :], pb[:, w % 2, 0:D].rearrange("p (k n) -> p k n", k=KC), ACT.Copy)\
                    .then_inc(s_ntc, 1)

            turned(0)
            for w in range(W):
                if w + 1 < W:
                    turned(w + 1)
                e.wait_ge(s_qkv, 2 * w + 1)
                if w >= 2:
                    e.wait_ge(s_kvst[w % 2], 32 * (w // 2))
                e.activation(kv_out[:, w % 2, :], pb[:, 2 + w % 2, :], ACT.Copy).then_inc(s_kvc, 1)

        phase(sync=mid_io, vector=mid_vector, tensor=mid_tensor, scalar=mid_scalar)

        s_upad, s_uin, s_ucol, s_urow, s_tcol, s_trow = (sem(n) for n in (
            "s_upad", "s_uin", "s_ucol", "s_urow", "s_tcol", "s_trow"))
        s_items, s_recin, s_rect, s_recc, s_st, s_wgt, s_pre1, s_gp1 = (sem(n) for n in (
            "s_items", "s_recin", "s_rect", "s_recc", "s_st", "s_wgt", "s_pre1", "s_gp1"))

        def walk_io(e):
            e.wait_ge(s_upad, 1)
            last = edge_table[:, (P - 1) * REC + DST:(P - 1) * REC + DST + 1]
            g = T // P
            e.dma_start(u_col[:, 0:g].unsqueeze(2), last[0:g * P, :].rearrange("(g p) n -> p g n", p=P),
                        allow_slow_non_contiguous=True).then_inc(s_uin, 16)
            e.dma_start(u_col[0:T - g * P, g:g + 1], last[g * P:T, :], allow_slow_non_contiguous=True)\
                .then_inc(s_uin, 16)

        def walk_gather(e):
            c = Chain(e, s_gp1)
            c(e.iota(item_row, [[1, WALK]], base=0, channel_multiplier=0, allow_small_or_imprecise_dtypes=True))
            c(e.iota(item_col, [[P, RAW_G]], base=0, channel_multiplier=1, allow_small_or_imprecise_dtypes=True))
            e.sem_inc(s_items, 1)
            e.wait_ge(s_tcol, 1)
            for g in range(RAW_G):
                e.indirect_dma_start(recs[:, g, :, :].rearrange("p e f -> p (e f)"), None, edge_table,
                                     bass.IndirectOffsetOnAxis(ap=t_int[:, g:g + 1], axis=0))\
                    .then_inc(s_recin, 16)

        def walk_vector(e):
            c = Chain(e, s_st)
            e.memset(u_col, 1e6).then_inc(s_upad, 1)
            e.wait_ge(s_items, 1)
            e.wait_ge(s_uin, 32)
            c(e.tensor_copy(u_int, u_col))
            c(e.tensor_scalar(u_int, u_int, LOG_P, None, ALU.arith_shift_right))
            c(e.tensor_copy(u_col, u_int))
            c(e.tensor_tensor(u_col, u_col, item_col, ALU.add))
            e.sem_inc(s_ucol, 1)
            e.wait_ge(s_urow, 1)
            for b in range(0, RAW_G, 4):
                n = min(RAW_G - b, 4) * P
                c(e.tensor_copy(u_row[:, b * P:b * P + n], pb[:, b // 4, 0:n]))
            for g in range(RAW_G):
                c(e.tensor_scalar(w_row, u_row, item_col[:, g:g + 1], None, ALU.is_lt, ALU.add,
                                  accum_out=t_col[:, g:g + 1]))
            c(e.tensor_scalar(t_col, t_col, float(T - 1), None, ALU.min))
            c(e.tensor_copy(t_int, t_col))
            e.sem_inc(s_tcol, 1)
            e.wait_ge(s_trow, 1)
            for b in range(0, WALK, 512):
                n = min(WALK - b, 512)
                c(e.tensor_tensor(w_row[:, b:b + n], item_row[:, b:b + n], pb[:, b // 512, 0:n], ALU.subtract))
            c(e.tensor_scalar(table[0:1, 0:WALK], w_row[0:1, 0:WALK], float(AW), None, ALU.mult))
            e.wait_ge(s_recc, 3 * RAW_G)
            c(e.scalar_tensor_tensor(dl_i, w_row[:, 0:WALK], -float(P), dst_i, ALU.mult, ALU.add))
            c(e.tensor_copy(dl_b, dl_i))
            for bound, op in ((0.0, ALU.is_lt), (float(P), ALU.is_ge)):
                c(e.tensor_scalar(u_row[:, 0:WALK], dl_i, bound, LOW, op, ALU.mult))
                c(e.tensor_tensor(wgt_i, wgt_i, u_row[:, 0:WALK], ALU.add))
            e.sem_inc(s_wgt, 1)

        def walk_tensor(e):
            def spread(col):
                for g in range(RAW_G):
                    ins = e.matmul(pb[:, g // 4, (g % 4) * P:(g % 4 + 1) * P], col[:, g:g + 1].to_broadcast([P, P]),
                                   ident[:], start=True, stop=True)
                return ins

            e.wait_ge(s_ucol, 1)
            spread(u_col).then_inc(s_urow, 1)
            e.wait_ge(s_tcol, 1)
            spread(t_col).then_inc(s_trow, 1)
            e.wait_ge(s_recin, 16 * RAW_G)
            for g in range(RAW_G):
                if g >= 4:
                    e.wait_ge(s_recc, 3 * (g - 3))
                for f in (DST, SRC, WGT):
                    ins = e.transpose(pb[:, 4 + g % 4, f * P:(f + 1) * P], recs[:, g, :, f], ident[:])
                ins.then_inc(s_rect, 1)

        def walk_scalar(e):
            for g in range(RAW_G):
                e.wait_ge(s_rect, g + 1)
                n = min(WALK - g * P, P)
                for f, to in ((DST, dst_i), (SRC, src_i), (WGT, wgt_i)):
                    e.activation(to[:, g * P:g * P + n], pb[:, 4 + g % 4, f * P:f * P + n], ACT.Copy)\
                        .then_inc(s_recc, 1)
            e.wait_ge(s_wgt, 1)
            for ch in range(CH):
                e.activation(edge_s[:].rearrange("p (j c h) -> p c j h", c=CH, h=HEADS)[:, ch, :, :],
                             wgt_i[:, ch * CJ:(ch + 1) * CJ].unsqueeze(2).to_broadcast([P, CJ, HEADS]), ACT.Copy)\
                    .then_inc(s_pre1, 1)

        phase(sync=walk_io, gpsimd=walk_gather, vector=walk_vector, tensor=walk_tensor, scalar=walk_scalar)

        score_c = edge_s[:].rearrange("p (j c h) -> p c j h", c=CH, h=HEADS)

        def score_parts(q):
            got, i = [], q * QUAD
            while i < (q + 1) * QUAD:
                ch, j = divmod(i, CJ)
                n = min((q + 1) * QUAD - i, CJ - j)
                got.append((i - q * QUAD, n, score_c[:, ch, j:j + n, :]))
                i += n
            return got

        s_kg = [sem(f"s_kg{k}") for k in range(ROW_RING)]
        a_spread, a_hot, a_q, a_mul, a_red, a_add = (Count(sem(n)) for n in (
            "s_a_spread", "s_a_hot", "s_a_q", "s_a_mul", "s_a_red", "s_a_add"))

        def gather_rows(e, from_table, landed, used):
            for q in range(QUADS):
                used.free(e, q, ROW_RING)
                for k in range(QUAD):
                    i = q * QUAD + k
                    e.indirect_dma_start(rows[:, q % ROW_RING, k, :], None, from_table,
                                         bass.IndirectOffsetOnAxis(ap=src_i[:, i:i + 1], axis=0))\
                        .then_inc(landed[q % ROW_RING], 16)

        def rows_in(e, q, landed):
            e.wait_ge(landed[q % ROW_RING], 16 * QUAD * (q // ROW_RING + 1))

        pen_x, pen_turn, pen_read = (Count(sem("s_pen_" + n)) for n in ("x", "turn", "read"))
        s_pen, s_ends = sem("s_pen"), sem("s_ends")
        PJ = 2
        PL = PJ * P
        pieces = [(j, min(PJ, CJ - j)) for j in range(0, CJ, PJ)]
        PIECES = len(pieces)
        EVERY = (QUADS - 4) // PIECES

        def piece_at(q, lag):
            n, r = divmod(q - lag, EVERY)
            return n if r == 0 and 0 <= n < PIECES else None

        def a_scalar(e):
            for n, (j0, nj) in enumerate(pieces):
                pen_turn.free(e, n, 2)
                for q in range(nj):
                    ins = e.activation(dst_x[:, n % 2, q * P:(q + 1) * P].rearrange("p (c h) -> p c h", h=HEADS),
                                       dst_i.rearrange("p (c j) -> p j c", c=CH)[:, j0 + q, :]
                                       .unsqueeze(2).to_broadcast([P, CH, HEADS]), ACT.Copy)
                ins.then_inc(pen_x.sem, 1)

        def turn_dst(e, n):
            j0, nj = pieces[n]
            pen_x.done(e, n)
            pen_read.free(e, n, 2)
            for q in range(nj):
                ins = e.transpose(pb[:, 6 + n % 2, q * P:(q + 1) * P], dst_x[:, n % 2, q * P:(q + 1) * P], ident[:])
            ins.then_inc(pen_turn.sem, 1)

        def penalties(e, c, n):
            j0, nj = pieces[n]
            L = nj * P
            pen_turn.done(e, n)
            if n:
                c(e.tensor_copy(dst_t[:, 0:1], dst_t[:, PL:PL + 1]))
            e.tensor_copy(dst_t[:, 1:L + 1], pb[:, 6 + n % 2, 0:L]).then_inc(pen_read.sem, 1)
            pen_read.done(e, n)
            if n == 0:
                c(e.tensor_copy(dst_t[:, 0:1], dst_t[:, 1:2]))
                c(e.tensor_copy(small[:, 0:1], dst_t[:, 1:2]))
            c(e.tensor_tensor(same[:, 0:L], dst_t[:, 1:L + 1], dst_t[:, 0:L], ALU.is_equal))
            c(e.tensor_scalar(pen[:, j0 * P:j0 * P + L], same[:, 0:L], 1.0, -LOW, ALU.subtract, ALU.mult))
            if n == PIECES - 1:
                c(e.memset(pen[:, CL:CL + 1], 0.0))
                c(e.tensor_copy(small[:, 1:2], dst_t[:, L:L + 1]))
                e.sem_inc(s_ends, 2)

        def a_gather(e):
            gather_rows(e, k_table, s_kg, a_mul)

        def a_tensor(e):
            win = Windows(e, "a_win")

            def spread(q):
                a_hot.free(e, q, 2)
                for k in range(QUAD):
                    i = q * QUAD + k
                    ins = e.matmul(pb[:, q % 2, k * P:(k + 1) * P], dl_b[:, i:i + 1].to_broadcast([P, P]),
                                   ident_b[:], start=True, stop=True)
                ins.then_inc(a_spread.sem, 1)

            def take_q(q):
                at = win.load(q)
                a_hot.done(e, q)
                a_mul.free(e, q, 2)
                for k in range(QUAD):
                    ins = e.matmul(pb[:, 2 + q % 2 * 2 + k // 2, k % 2 * D:(k % 2 + 1) * D],
                                   w_hot[:, q % 2, k * P:(k + 1) * P], acc[:, bass.ds(at[k], D)],
                                   start=True, stop=True)
                ins.then_inc(a_q.sem, 1)

            for q in range(QUADS + 1):
                if q < QUADS:
                    spread(q)
                if q:
                    take_q(q - 1)
                if piece_at(q, 0) is not None:
                    turn_dst(e, piece_at(q, 0))

        def a_vector(e):
            c = Chain(e, s_pen)

            def hot_of(q):
                a_spread.done(e, q)
                a_q.free(e, q, 2)
                e.tensor_scalar(w_hot[:, q % 2, :], pb[:, q % 2, :], iota_p[:], None, ALU.is_equal)\
                    .then_inc(a_hot.sem, 1)

            def multiply(q):
                a_q.done(e, q)
                rows_in(e, q, s_kg)
                a_red.free(e, q, 2)
                e.tensor_tensor(prods[:, q % 2, :].rearrange("p (b n) -> p b n", b=2),
                                rows[:, q % ROW_RING, :, :].rearrange("p (b k) n -> p b (k n)", b=2),
                                pb[:, 2 + q % 2 * 2:4 + q % 2 * 2, :], ALU.mult).then_inc(a_mul.sem, 1)

            def reduce(q):
                a_mul.done(e, q)
                a_add.free(e, q, 2)
                e.tensor_reduce(parts[:, q % 2, :], prods[:, q % 2, :].rearrange("p (h d) -> p h d", d=HD),
                                AX.X, ALU.add).then_inc(a_red.sem, 1)

            def add(q):
                a_red.done(e, q)
                part = parts[:, q % 2, :].rearrange("p (k h) -> p k h", h=HEADS)
                for first, n, to in score_parts(q):
                    ins = e.scalar_tensor_tensor(to, part[:, first:first + n, :], SCALE, to, ALU.mult, ALU.add)
                ins.then_inc(a_add.sem, 1)

            for q in range(QUADS + 2):
                if q < QUADS:
                    hot_of(q)
                if q >= 2:
                    reduce(q - 2)
                if 1 <= q <= QUADS:
                    multiply(q - 1)
                if q >= 2:
                    add(q - 2)
                if piece_at(q, 2) is not None:
                    penalties(e, c, piece_at(q, 2))

        phase(scalar=a_scalar, gpsimd=a_gather, tensor=a_tensor, vector=a_vector)

        s_mt, s_ms, s_edge, s_car = sem("s_mt"), sem("s_ms"), sem("s_edge"), sem("s_car")
        s_mc = [sem("s_mc0"), sem("s_mc1")]
        s_mb, s_sub, s_exp = sem("s_mb"), sem("s_sub"), sem("s_exp")

        def copy_piece(e, n):
            j0, nj = pieces[n]
            e.wait_ge(s_mt, n + 1)
            to, ps = scan_s[:, j0 * P:(j0 + nj) * P], pb[:, n % 4, 0:nj * P]
            if n % 2:
                e.tensor_copy(to, ps).then_inc(s_mc[1], 1)
            else:
                e.activation(to, ps, ACT.Copy).then_inc(s_mc[0], 1)

        def max_tensor(e):
            for n, (j0, nj) in enumerate(pieces):
                if n >= 4:
                    e.wait_ge(s_mc[n % 2], n // 2 - 1)
                for q in range(nj):
                    ins = e.transpose(pb[:, n % 4, q * P:(q + 1) * P], score_v[:, j0 + q, :], ident[:])
                ins.then_inc(s_mt, 1)
            for r in range(3):
                e.wait_ge(s_ends, r + 1)
                e.transpose(pb[0:1, 4, r * P:(r + 1) * P], small[:, r:r + 1], ident[:]).then_inc(s_edge, 1)
            e.wait_ge(s_ends, 4)
            e.matmul(pb[:, 5, 0:1], row[8], ones[0:1, 0:1], start=True, stop=True).then_inc(s_edge, 1)
            e.wait_ge(s_ends, 5)
            e.transpose(pb[0:1, 6, 0:P], small[:, 3:4], ident[:]).then_inc(s_edge, 1)
            e.wait_ge(s_ends, 6)
            e.matmul(pb[:, 7, 0:1], row[8], ones[0:1, 0:1], start=True, stop=True).then_inc(s_edge, 1)
            e.wait_ge(s_car, 1)
            for n in range(PIECES):
                if n >= 2:
                    e.wait_ge(s_sub, n - 1)
                j0, nj = pieces[n]
                for q in range(nj):
                    ins = e.transpose(pb[:, n % 2, q * P:(q + 1) * P], scan_s[:, (j0 + q) * P:(j0 + q + 1) * P],
                                      ident[:])
                ins.then_inc(s_mb, 1)

        def max_scalar(e):
            for n in range(0, PIECES, 2):
                copy_piece(e, n)
            for c in range(CH):
                e.wait_ge(s_sub, PIECES)
                part_ = edge_s[:, c * CJ * HEADS:(c + 1) * CJ * HEADS]
                e.activation(part_, part_, ACT.Exp).then_inc(s_exp, 1)

        def max_vector(e):
            c = Chain(e, s_ms)
            for n in range(1, PIECES, 2):
                copy_piece(e, n)
            e.wait_ge(s_mc[0], PIECES - PIECES // 2)
            e.wait_ge(s_mc[1], PIECES // 2)
            c(e.tensor_tensor_scan(scan_s, pen[:, 0:CL], scan_s, LOW, ALU.add, ALU.max))
            c(e.tensor_copy(small[:, 2:3], scan_s[:, CL - 1:CL]))
            e.sem_inc(s_ends, 1)
            e.wait_ge(s_edge, 3)
            first, last, value, cont, whole, step, base, t0 = row[0:8]
            hc = "a (c h) -> a h c"

            def by_head(to, ps):
                c(e.tensor_copy(to.rearrange("a (h c) -> a h c", h=HEADS), ps.rearrange(hc, h=HEADS)))

            by_head(first, pb[0:1, 4, 0:P])
            by_head(last, pb[0:1, 4, P:2 * P])
            by_head(value, pb[0:1, 4, 2 * P:3 * P])
            c(e.memset(cont, 0.0))
            c(e.tensor_tensor(cont[:, 1:P], first[:, 1:P], last[:, 0:P - 1], ALU.is_equal))
            c(e.memset(cont.rearrange("a (h c) -> a h c", h=HEADS)[:, :, 0:1], 0.0))
            c(e.tensor_tensor(whole, first, last, ALU.is_equal))

            def carry_in(shift):
                c(e.memset(step, LOW))
                c(e.memset(base, LOW))
                if shift == 1:
                    here, there, flag = slice(1, P), slice(0, P - 1), cont[:, 1:P]
                else:
                    here, there, flag = slice(0, P - 1), slice(1, P), cont[:, 1:P]
                c(e.tensor_tensor(t0[:, 0:P - 1], flag, whole[:, there], ALU.mult))
                c(e.tensor_scalar(step[:, here], t0[:, 0:P - 1], 1.0, -LOW, ALU.subtract, ALU.mult))
                c(e.tensor_scalar(t0[:, 0:P - 1], flag, 1.0, -LOW, ALU.subtract, ALU.mult))
                c(e.tensor_tensor(base[:, here], value[:, there], t0[:, 0:P - 1], ALU.add))
                if shift == 1:
                    c(e.tensor_tensor_scan(row[9], step, base, LOW, ALU.add, ALU.max))
                else:
                    c(e.tensor_tensor_scan(row[9][:, ::-1], step[:, ::-1], base[:, ::-1], LOW, ALU.add, ALU.max))
                c(e.tensor_copy(row[8].rearrange("a (c h) -> a c h", h=HEADS),
                                row[9].rearrange("a (h c) -> a c h", h=HEADS)))
                e.sem_inc(s_ends, 1)

            carry_in(1)
            e.wait_ge(s_edge, 4)
            c(e.tensor_copy(carry[:, 0:1], pb[:, 5, 0:1]))
            c(e.tensor_tensor_scan(scan_s, pen[:, 0:CL], scan_s, carry[:, 0:1], ALU.add, ALU.max))
            back_s, back_p = scan_s[:, ::-1], pen[:, 1:CL + 1][:, ::-1]
            c(e.tensor_tensor_scan(back_s, back_p, back_s, LOW, ALU.add, ALU.max))
            c(e.tensor_copy(small[:, 3:4], scan_s[:, 0:1]))
            e.sem_inc(s_ends, 1)
            e.wait_ge(s_edge, 5)
            by_head(value, pb[0:1, 6, 0:P])
            carry_in(-1)
            e.wait_ge(s_edge, 6)
            c(e.tensor_copy(carry[:, 1:2], pb[:, 7, 0:1]))
            c(e.tensor_tensor_scan(back_s, back_p, back_s, carry[:, 1:2], ALU.add, ALU.max))
            e.sem_inc(s_car, 1)
            for n, (j0, nj) in enumerate(pieces):
                e.wait_ge(s_mb, n + 1)
                to = edge_s[:, j0 * P:(j0 + nj) * P]
                e.tensor_tensor(to, to, pb[:, n % 2, 0:nj * P], ALU.subtract).then_inc(s_sub, 1)

        phase(scalar=max_scalar, tensor=max_tensor, vector=max_vector)

        s_vg = [sem(f"s_vg{k}") for k in range(ROW_RING)]
        b_exp, b_hot, b_msg, b_sum, b_add = (Count(sem(n)) for n in (
            "s_b_exp", "s_b_hot", "s_b_msg", "s_b_sum", "s_b_add"))
        s_bz = sem("s_bz")

        def b_gather(e):
            gather_rows(e, v_table, s_vg, b_msg)

        def b_scalar(e):
            for q in range(QUADS):
                b_sum.free(e, (q + 1) * QUAD - 1, 2 * QUAD)
                for first, n, ex in score_parts(q):
                    ins = e.activation(msgs[:, q % 2, first:first + n, D:AW], ex, ACT.Copy)
                ins.then_inc(b_exp.sem, 1)

        def b_tensor(e):
            for q in range(QUADS):
                b_hot.done(e, q)
                b_msg.done(e, q)
                for k in range(QUAD):
                    i = q * QUAD + k
                    b_add.free(e, i, 8)
                    e.matmul(pb[:, i % 8, 0:AW], w_hot[:, q % 2, k * P:(k + 1) * P], msgs[:, q % 2, k, :],
                             start=True, stop=True).then_inc(b_sum.sem, 1)

        def b_vector(e):
            win = Windows(e, "b_win")

            def hot_of(q, k):
                i = q * QUAD + k
                return e.tensor_scalar(w_hot[:, q % 2, k * P:(k + 1) * P], iota_q[:, 0:P], dl_i[:, i:i + 1], None,
                                       ALU.is_equal)

            def add(q, k, at):
                i = q * QUAD + k
                b_sum.done(e, i)
                b_add.free(e, i, 1)
                to = acc[:, bass.ds(at[k], AW)]
                e.tensor_tensor(to, to, pb[:, i % 8, 0:AW], ALU.add).then_inc(b_add.sem, 1)

            for q in range(QUADS + 1):
                for w in range(q * QUAD, min((q + 1) * QUAD, W)):
                    e.memset(acc_w[:, w, :], 0.0).then_inc(s_bz, 1)
                if q:
                    e.wait_ge(s_bz, min(q * QUAD, W))
                    at = win.load(q - 1)
                if q < QUADS:
                    b_sum.free(e, (q + 1) * QUAD - 1, 2 * QUAD)
                for k in range(QUAD):
                    if q < QUADS:
                        ins = hot_of(q, k)
                    if q < QUADS and k == QUAD - 1:
                        ins.then_inc(b_hot.sem, 1)
                        rows_in(e, q, s_vg)
                        b_exp.done(e, q)
                        e.tensor_tensor(msgs[:, q % 2, :, 0:D].rearrange("p k (h d) -> p k h d", h=HEADS),
                                        rows[:, q % ROW_RING, :, :].rearrange("p k (h d) -> p k h d", h=HEADS),
                                        msgs[:, q % 2, :, D:AW].unsqueeze(3).to_broadcast([P, QUAD, HEADS, HD]),
                                        ALU.mult).then_inc(b_msg.sem, 1)
                    if q:
                        add(q - 1, k, at)

        phase(scalar=b_scalar, gpsimd=b_gather, tensor=b_tensor, vector=b_vector)

        s_fw0, s_fw = sem("s_fw0"), sem("s_fw")
        s_x1l = [sem(f"s_x1l{k}") for k in range(len(chunks))]
        s_fc, s_rooted, s_vars = sem("s_fc"), sem("s_rooted"), sem("s_vars")
        f_att, f_turn, f_turned, f_proj, f_z, f_h1, f_w1, f_gelu, f_w2, f_y, f_out = (
            Count(sem("s_f_" + n)) for n in ("att", "turn", "turned", "proj", "z", "h1", "w1", "gelu", "w2", "y",
                                             "out"))
        s_store = sem("s_store")
        groups = [list(range(w, min(w + 4, W))) for w in range(0, W, 4)]
        STEPS = len(chunks) + 4

        def chunk(n):
            return chunks[n] if 0 <= n < len(chunks) else []

        def groups_of(n):
            return [g for g, ws in enumerate(groups) if ws[0] in chunk(n)]

        turns = {}
        for n in range(STEPS):
            for key in [("h1", w) for w in chunk(n - 2)] + [("att", w) for w in chunk(n)]:
                turns[key] = len(turns)

        def f_io(e):
            def load_x1(k):
                lo, hi = chunks[k][0], chunks[k][-1] + 1
                e.dma_start(x1[:, lo:hi, :], x1_store[lo * P:hi * P, :].rearrange("(w p) d -> p w d", p=P))\
                    .then_inc(s_x1l[k], 16)

            e.dma_start(wp, a["L1_gnn_Wp"].rearrange("(k p) n -> p k n", p=P)).then_inc(s_fw0, 16)
            for n in vec:
                e.dma_start(vec[n], a["L1_gnn_" + n].rearrange("(a d) -> a d", a=1).to_broadcast([P, D]))\
                    .then_inc(s_fw0, 16)
            load_x1(0)
            e.dma_start(w1, a["L1_gnn_W1"].rearrange("(k p) n -> p k n", p=P)).then_inc(s_fw, 16)
            e.dma_start(b1c, a["L1_gnn_b1"].rearrange("(k p) -> p k", p=P), allow_slow_non_contiguous=True)\
                .then_inc(s_fw, 16)
            e.dma_start(w2, a["L1_gnn_W2"].rearrange("(k p) n -> p k n", p=P)).then_inc(s_fw, 16)
            for k in range(1, len(chunks)):
                load_x1(k)
            for w in range(W):
                f_out.done(e, w)
                e.dma_start(out[w * P:w * P + node_rows(w), :], x1[0:node_rows(w), w, :]).then_inc(s_store, 16)
            e.wait_ge(s_store, 16 * W)

        def f_vector(e):
            c = Chain(e, s_fc)
            e.wait_ge(s_fw0, 16 * (1 + len(vec)))
            moments = [m.rearrange("p (w t) -> p w t", t=2) for m in
                       (mv[:], mv2[:, 0:2 * W], mv2[:, 2 * W:4 * W])]
            rs = roots_s[:].rearrange("p (v k i) -> p v k i", v=2, k=3)
            c(e.memset(roots_s[:], 1.0))

            def z(w):
                return acc_w[:, w, 0:D]

            def stat(k, data=z):
                def slot(w):
                    return stats[:, w % STATS * 6:(w % STATS + 1) * 6]
                return (lambda w: e.bn_stats(slot(w), data(w)),
                        lambda w: e.bn_aggr(moments[k][:, w, :], slot(w)))

            def scale_of(k, w):
                return rs[:, 0, k, w % CHUNK:w % CHUNK + 1], rs[:, 1, k, w % CHUNK:w % CHUNK + 1]

            def norm(k, g, b):
                return (lambda w: e.tensor_scalar(z(w), z(w), *scale_of(k, w), ALU.mult, ALU.add),
                        lambda w: e.tensor_tensor(z(w), z(w), vec[g], ALU.mult),
                        lambda w: e.tensor_tensor(z(w), z(w), vec[b], ALU.add))

            def roots(n):
                now = [(k, ws) for k, ws in enumerate((chunk(n), chunk(n - 2), chunk(n - 3))) if ws]
                if not now:
                    return
                for w in chunk(n - 4)[-1:]:
                    f_out.done(e, w)
                for k, ws in now:
                    c(e.tensor_scalar(rs[:, 0, k, 0:len(ws)], moments[k][:, ws[0]:ws[-1] + 1, 1], EPS, None, ALU.add))
                e.sem_inc(s_vars, 1)
                e.wait_ge(s_rooted, n + 1)
                c(e.reciprocal(roots_s[:, 0:3 * CHUNK], roots_s[:, 0:3 * CHUNK]))
                for k, ws in now:
                    c(e.scalar_tensor_tensor(rs[:, 1, k, 0:len(ws)], moments[k][:, ws[0]:ws[-1] + 1, 0], -1.0,
                                             rs[:, 0, k, 0:len(ws)], ALU.mult, ALU.mult))

            def first_done(w):
                e.sem_inc(f_h1.sem, 1)

            def read_y(ws):
                def add_y(w):
                    f_w2.done(e, w)
                    return e.tensor_tensor(z(w), z(w), pb[:, 6 + w % 2, 0:D], ALU.add)

                def y_read(w):
                    e.sem_inc(f_y.sem, 1)
                    return e.tensor_tensor(z(w), z(w), vec["b2"], ALU.add)
                staggered(c, ws, add_y, y_read, *stat(1))

            def attention(ws):
                n = len(ws)
                den = recip[:, 0:n * HEADS]
                c(e.tensor_scalar(den.rearrange("p (w h) -> p w h", h=HEADS), acc_w[:, ws[0]:ws[-1] + 1, D:AW],
                                  1e-30, None, ALU.max))
                c(e.reciprocal(den, den))
                for i, w in enumerate(ws):
                    v = z(w).rearrange("p (h d) -> p h d", h=HEADS)
                    e.tensor_tensor(v, v, den[:, i * HEADS:(i + 1) * HEADS].unsqueeze(2)
                                    .to_broadcast([P, HEADS, HD]), ALU.mult).then_inc(f_att.sem, 1)

            def project(ws):
                def add_x(w):
                    e.wait_ge(s_x1l[w // CHUNK], 16)
                    f_proj.done(e, w)
                    f_att.done(e, w)
                    return e.tensor_tensor(z(w), pb[:, 2 + w % 2, 0:D], x1[:, w, :], ALU.add)

                def z_read(w):
                    e.sem_inc(f_z.sem, 1)
                    return e.tensor_tensor(z(w), z(w), vec["bp"], ALU.add)
                staggered(c, ws, add_x, z_read, *stat(0))

            for n in range(STEPS):
                if chunk(n - 1):
                    staggered(c, chunk(n - 1), *norm(0, "ln1_g", "ln1_b"), first_done)
                if chunk(n - 3):
                    staggered(c, chunk(n - 3), *norm(1, "ln2_g", "ln2_b"),
                              lambda w: e.tensor_tensor(z(w), z(w), x1[:, w, :], ALU.add), *stat(2))
                for w in chunk(n - 4):
                    e.tensor_scalar(x1[:, w, :], z(w), *scale_of(2, w), ALU.mult, ALU.add).then_inc(f_out.sem, 1)
                if chunk(n):
                    attention(chunk(n))
                net = groups_of(n - 2)
                if net:
                    read_y(groups[net[0]])
                if chunk(n):
                    project(chunk(n))
                for g in net[1:]:
                    read_y(groups[g])
                roots(n)

        def f_tensor(e):
            e.wait_ge(s_fw0, 16 * (1 + len(vec)))

            def turn(what, w):
                t = turns[what, w]
                f_turned.free(e, t, 2)
                for k in range(KC):
                    ins = e.transpose(pb[:, t % 2, k * P:(k + 1) * P], acc_w[:, w, k * P:(k + 1) * P], ident[:])
                ins.then_inc(f_turn.sem, 1)

            def net_in(g):
                ws = groups[g]
                cols = len(ws) * P
                for w in ws:
                    f_h1.done(e, w)
                    turn("h1", w)
                f_turned.done(e, turns["h1", ws[-1]])
                for f in range(FC):
                    m = g * FC + f
                    f_gelu.free(e, m, 2)
                    for k in range(KC):
                        ins = e.matmul(pb[:, 4 + m % 2, 0:cols], w1[:, k, f * P:(f + 1) * P],
                                       h1_t[:, g % 2, k, 0:cols], start=(k == 0), stop=(k == KC - 1))
                    ins.then_inc(f_w1.sem, 1)

            def net_out(g):
                f_gelu.done(e, g * FC + FC - 1)
                for i, w in enumerate(groups[g]):
                    f_y.free(e, w, 2)
                    for f in range(FC):
                        ins = e.matmul(pb[:, 6 + w % 2, 0:D], hid[g % 2][:, f, i * P:(i + 1) * P], w2[:, f, :],
                                       start=(f == 0), stop=(f == FC - 1))
                    ins.then_inc(f_w2.sem, 1)

            def project(ws):
                for i, w in enumerate(ws):
                    for v in ws[i:i + 2] if i == 0 else ws[i + 1:i + 2]:
                        f_att.done(e, v)
                        turn("att", v)
                    f_turned.done(e, turns["att", w])
                    f_z.free(e, w, 2)
                    for k in range(KC):
                        ins = e.matmul(pb[:, 2 + w % 2, 0:D], att_t[:, w % 2, k, :], wp[:, k, :],
                                       start=(k == 0), stop=(k == KC - 1))
                    ins.then_inc(f_proj.sem, 1)

            for n in range(STEPS):
                net = groups_of(n - 2)
                if n == 2:
                    e.wait_ge(s_fw, 48)
                for g in net:
                    net_in(g)
                if net:
                    net_out(net[0])
                project(chunk(n))
                for g in net[1:]:
                    net_out(g)

        def f_scalar(e):
            e.wait_ge(s_fw, 48)

            def net(g):
                ws = groups[g]
                cols = len(ws) * P
                for i, w in enumerate(ws):
                    t = turns["h1", w]
                    f_turn.done(e, t)
                    f_w1.free(e, g * FC + FC - 1, 2 * FC)
                    e.activation(h1_t[:, g % 2, :, i * P:(i + 1) * P],
                                 pb[:, t % 2, 0:D].rearrange("p (k n) -> p k n", k=KC), ACT.Copy)\
                        .then_inc(f_turned.sem, 1)
                for f in range(FC):
                    f_w1.done(e, g * FC + f)
                    if g >= 2:
                        f_w2.done(e, groups[g - 2][-1])
                    e.activation(hid[g % 2][:, f, 0:cols], pb[:, 4 + (g * FC + f) % 2, 0:cols], ACT.Gelu,
                                 bias=b1c[:, f:f + 1]).then_inc(f_gelu.sem, 1)

            for n in range(STEPS):
                for g in groups_of(n - 2):
                    net(g)
                for w in chunk(n):
                    t = turns["att", w]
                    f_turn.done(e, t)
                    f_proj.free(e, w, 2)
                    e.activation(att_t[:, w % 2, :, :],
                                 pb[:, t % 2, 0:D].rearrange("p (k n) -> p k n", k=KC), ACT.Copy)\
                        .then_inc(f_turned.sem, 1)
                if chunk(n) or chunk(n - 2) or chunk(n - 3):
                    e.wait_ge(s_vars, n + 1)
                    e.activation(roots_s[:, 0:3 * CHUNK], roots_s[:, 0:3 * CHUNK], ACT.Sqrt).then_inc(s_rooted, 1)

        phase(sync=f_io, vector=f_vector, tensor=f_tensor, scalar=f_scalar)

        block = ctx.enter_context(nc.Block())

        def run(e, name):
            for todo in engines[name]:
                if todo is not None:
                    todo(e)
                meet(e)

        @block.sync
        def _(e):
            run(e, "sync")

        @block.gpsimd
        def _(e):
            run(e, "gpsimd")

        @block.scalar
        def _(e):
            run(e, "scalar")

        @block.tensor
        def _(e):
            run(e, "tensor")

        @block.vector
        def _(e):
            run(e, "vector")


INPUTS = ["x", "src", "dst", "edge_type_8", "edge_weight1", "L0_gnn_weight", "L0_gnn_bias", "L1_gnn_Wq",
          "L1_gnn_Wk", "L1_gnn_Wv", "L1_gnn_Wp", "L1_gnn_bp", "L1_gnn_ln1_g", "L1_gnn_ln1_b", "L1_gnn_ln2_g",
          "L1_gnn_ln2_b", "L1_gnn_W1", "L1_gnn_b1", "L1_gnn_W2", "L1_gnn_b2"]


def kernel(**inputs):
    import concourse.bacc as bacc
    from concourse.bass_utils import run_bass_kernel_spmd

    nc = bacc.Bacc("TRN2", target_bir_lowering=False, num_devices=1)
    arrays, args = {}, {}
    for name in INPUTS:
        v = np.ascontiguousarray(inputs[name])
        if name == "edge_weight1":
            v = v.reshape(-1)
        arrays["in_" + name] = v
        args[name] = nc.dram_tensor("in_" + name, v.shape, mybir.dt.from_np(v.dtype), kind="ExternalInput").ap()
    out = nc.dram_tensor("out", (N, D), F32, kind="ExternalOutput").ap()
    build(nc, args, out)
    return run_bass_kernel_spmd(nc, [arrays], core_ids=[0]).results[0]["out"]
```
